# Optimizing a Trainium2 kernel written in Bass

```python
import numpy as np
import jax
import jax.numpy as jnp

def _softmax(x, axis=-1):
    return jax.nn.softmax(x, axis=axis)

def _gelu(x):
    return jax.nn.gelu(x, approximate=True)

def _silu(x):
    return jax.nn.silu(x)

def _sigmoid(x):
    return jax.nn.sigmoid(x)

def _layernorm(x, axis=-1, eps=1e-05):
    m = jnp.mean(x, axis=axis, keepdims=True)
    v = jnp.var(x, axis=axis, keepdims=True)
    return (x - m) / jnp.sqrt(v + eps)

def _scatter_add(tgt, idx, src, axis=0):
    return tgt.at[idx].add(src)

def _segment_sum(src, seg, n):
    return jax.ops.segment_sum(src, seg, n)
kernel_name = 'mk_seq_postln_d1_jaxref_r4_775450'

def setup_inputs(seed: int=0):
    np.random.seed(seed)
    _w = jnp.asarray

    def _L0_attn_setup():
        import math
        import jax, jax.numpy as jnp
        import numpy as np
        H = 16
        LAYER_POS = 12
        LAM_INIT = 0.8 - 0.6 * math.exp(-0.3 * (LAYER_POS - 1))
        LN_EPS = 1e-05

        def _heads(t, B, S, h, d):
            return t.reshape(B, S, h, d).transpose(0, 2, 1, 3)
        key = jax.random.key(seed)
        ks = jax.random.split(key, 12)
        B, S, E = (2, 512, 256)
        d = E // H
        w = 0.02
        return {'x': jax.random.normal(ks[0], (B, S, E), jnp.float32), 'Wq1': jax.random.normal(ks[1], (E, E), jnp.float32) * w, 'Wq2': jax.random.normal(ks[2], (E, E), jnp.float32) * w, 'Wk1': jax.random.normal(ks[3], (E, E), jnp.float32) * w, 'Wk2': jax.random.normal(ks[4], (E, E), jnp.float32) * w, 'Wv': jax.random.normal(ks[5], (E, 2 * E), jnp.float32) * w, 'Wo': jax.random.normal(ks[6], (2 * E, E), jnp.float32) * w, 'lq1': jax.random.normal(ks[7], (H, d), jnp.float32) * 0.1, 'lk1': jax.random.normal(ks[8], (H, d), jnp.float32) * 0.1, 'lq2': jax.random.normal(ks[9], (H, d), jnp.float32) * 0.1, 'lk2': jax.random.normal(ks[10], (H, d), jnp.float32) * 0.1}
    _L0_attn_in = _L0_attn_setup()

    def _L0_ffn_setup():
        import jax, jax.numpy as jnp
        import numpy as np
        D_IN, D_HID = (256, 1024)

        def _ternary(key, shape):
            return jax.random.randint(key, shape, -1, 2).astype(jnp.float32)

        def _tlin(x, w, s):
            return jnp.einsum('bsi,oi->bso', x, w) * s
        key = jax.random.key(seed)
        ks = jax.random.split(key, 12)
        inv = lambda fan: 1.0 / np.sqrt(fan).astype(np.float32)
        return {'x': jax.random.normal(ks[0], (4, 512, D_IN), dtype=jnp.float32), 'w1_w': _ternary(ks[1], (D_HID, D_IN)), 'w1_s': jax.random.uniform(ks[2], (D_HID,), dtype=jnp.float32) * inv(D_IN), 'w2_w': _ternary(ks[3], (D_HID, D_IN)), 'w2_s': jax.random.uniform(ks[4], (D_HID,), dtype=jnp.float32) * inv(D_IN), 'h1_w': _ternary(ks[5], (D_HID, D_HID)), 'h1_s': jax.random.uniform(ks[6], (D_HID,), dtype=jnp.float32) * inv(D_HID), 'h2_w': _ternary(ks[7], (D_HID, D_HID)), 'h2_s': jax.random.uniform(ks[8], (D_HID,), dtype=jnp.float32) * inv(D_HID), 'w3_w': _ternary(ks[9], (D_IN, D_HID)), 'w3_s': jax.random.uniform(ks[10], (D_IN,), dtype=jnp.float32) * inv(D_HID)}
    _L0_ffn_in = _L0_ffn_setup()
    _d = {'L0_attn_x': _L0_attn_in['x'], 'L0_attn_Wq1': _L0_attn_in['Wq1'], 'L0_attn_Wq2': _L0_attn_in['Wq2'], 'L0_attn_Wk1': _L0_attn_in['Wk1'], 'L0_attn_Wk2': _L0_attn_in['Wk2'], 'L0_attn_Wv': _L0_attn_in['Wv'], 'L0_attn_Wo': _L0_attn_in['Wo'], 'L0_attn_lq1': _L0_attn_in['lq1'], 'L0_attn_lk1': _L0_attn_in['lk1'], 'L0_attn_lq2': _L0_attn_in['lq2'], 'L0_attn_lk2': _L0_attn_in['lk2'], 'L0_ffn_w1_w': _L0_ffn_in['w1_w'], 'L0_ffn_w1_s': _L0_ffn_in['w1_s'], 'L0_ffn_w2_w': _L0_ffn_in['w2_w'], 'L0_ffn_w2_s': _L0_ffn_in['w2_s'], 'L0_ffn_h1_w': _L0_ffn_in['h1_w'], 'L0_ffn_h1_s': _L0_ffn_in['h1_s'], 'L0_ffn_h2_w': _L0_ffn_in['h2_w'], 'L0_ffn_h2_s': _L0_ffn_in['h2_s'], 'L0_ffn_w3_w': _L0_ffn_in['w3_w'], 'L0_ffn_w3_s': _L0_ffn_in['w3_s']}
    _x0 = _d['L0_attn_x']
    _d['L0_attn_x'] = jax.random.normal(jax.random.fold_in(jax.random.key(seed), 1), (2, 2048, 256), dtype=_x0.dtype)
    del _x0
    return _d

def reference(L0_attn_x, L0_attn_Wq1, L0_attn_Wq2, L0_attn_Wk1, L0_attn_Wk2, L0_attn_Wv, L0_attn_Wo, L0_attn_lq1, L0_attn_lk1, L0_attn_lq2, L0_attn_lk2, L0_ffn_w1_w, L0_ffn_w1_s, L0_ffn_w2_w, L0_ffn_w2_s, L0_ffn_h1_w, L0_ffn_h1_s, L0_ffn_h2_w, L0_ffn_h2_s, L0_ffn_w3_w, L0_ffn_w3_s):

    def _L0_attn_ref(x, Wq1, Wq2, Wk1, Wk2, Wv, Wo, lq1, lk1, lq2, lk2):
        import math
        import jax, jax.numpy as jnp
        import numpy as np
        H = 16
        LAYER_POS = 12
        LAM_INIT = 0.8 - 0.6 * math.exp(-0.3 * (LAYER_POS - 1))
        LN_EPS = 1e-05

        def _heads(t, B, S, h, d):
            return t.reshape(B, S, h, d).transpose(0, 2, 1, 3)
        B, S, E = x.shape
        d = E // H
        scale = 1.0 / math.sqrt(d)
        q1 = _heads(x @ Wq1, B, S, H, d)
        q2 = _heads(x @ Wq2, B, S, H, d)
        k1 = _heads(x @ Wk1, B, S, H, d)
        k2 = _heads(x @ Wk2, B, S, H, d)
        v = _heads(x @ Wv, B, S, H, 2 * d)
        causal = jnp.tril(jnp.ones((S, S), dtype=bool))
        neg_inf = jnp.float32(-jnp.inf)
        s1 = jnp.einsum('bhqd,bhkd->bhqk', q1, k1) * scale
        s2 = jnp.einsum('bhqd,bhkd->bhqk', q2, k2) * scale
        a1 = jax.nn.softmax(jnp.where(causal, s1, neg_inf), axis=-1)
        a2 = jax.nn.softmax(jnp.where(causal, s2, neg_inf), axis=-1)
        lam = jnp.exp(jnp.sum(lq1 * lk1, axis=-1)) - jnp.exp(jnp.sum(lq2 * lk2, axis=-1)) + LAM_INIT
        comb = a1 - lam[None, :, None, None] * a2
        out = jnp.einsum('bhqk,bhkv->bhqv', comb, v)
        mu = jnp.mean(out, axis=-1, keepdims=True)
        var = jnp.mean(jnp.square(out - mu), axis=-1, keepdims=True)
        normed = (out - mu) * jax.lax.rsqrt(var + LN_EPS)
        scaled = normed * (1.0 - LAM_INIT)
        merged = scaled.transpose(0, 2, 1, 3).reshape(B, S, 2 * E)
        return merged @ Wo

    def _L0_ffn_ref(x, w1_w, w1_s, w2_w, w2_s, h1_w, h1_s, h2_w, h2_s, w3_w, w3_s):
        import jax, jax.numpy as jnp
        import numpy as np
        D_IN, D_HID = (256, 1024)

        def _ternary(key, shape):
            return jax.random.randint(key, shape, -1, 2).astype(jnp.float32)

        def _tlin(x, w, s):
            return jnp.einsum('bsi,oi->bso', x, w) * s
        h = jax.nn.silu(_tlin(x, w1_w, w1_s)) * _tlin(x, w2_w, w2_s)
        h = jax.nn.gelu(_tlin(h, h1_w, h1_s), approximate=False)
        h = jax.nn.gelu(_tlin(h, h2_w, h2_s), approximate=False)
        return _tlin(h, w3_w, w3_s)
    x = L0_attn_x
    x = _layernorm(x + _L0_attn_ref(x, L0_attn_Wq1, L0_attn_Wq2, L0_attn_Wk1, L0_attn_Wk2, L0_attn_Wv, L0_attn_Wo, L0_attn_lq1, L0_attn_lk1, L0_attn_lq2, L0_attn_lk2), axis=-1)
    x = _layernorm(x + _L0_ffn_ref(x, L0_ffn_w1_w, L0_ffn_w1_s, L0_ffn_w2_w, L0_ffn_w2_s, L0_ffn_h1_w, L0_ffn_h1_s, L0_ffn_h2_w, L0_ffn_h2_s, L0_ffn_w3_w, L0_ffn_w3_s), axis=-1)
    return x

_drawn_inputs = setup_inputs


def setup_inputs(seed=0):
    import zlib

    import numpy as np

    out = dict(_drawn_inputs(seed))
    spreads = {}
    factors = {'L0_attn_lq1': 7.062,
     'L0_attn_lk1': 6.921,
     'L0_attn_lq2': 7.347,
     'L0_attn_lk2': 7.514,
     'L0_ffn_w1_w': 8.0,
     'L0_ffn_w1_s': 8.0,
     'L0_ffn_w2_w': 8.0,
     'L0_ffn_w2_s': 8.0,
     'L0_ffn_h1_w': 8.0,
     'L0_ffn_h1_s': 8.0,
     'L0_ffn_h2_w': 8.0,
     'L0_ffn_h2_s': 8.0,
     'L0_ffn_w3_w': 8.0,
     'L0_ffn_w3_s': 8.0}
    for name, (base, spread) in spreads.items():
        noise = np.random.default_rng([zlib.crc32(name.encode()), seed]).standard_normal(out[name].shape)
        drawn = base * np.exp(spread * noise) if base else spread * noise
        out[name] = jnp.asarray(drawn.astype(out[name].dtype))
    for name, factor in factors.items():
        out[name] = (out[name] * factor).astype(out[name].dtype)
    return out
```

```python
import math
from contextlib import ExitStack

import concourse.bass as bass
from concourse import mybir

F32 = mybir.dt.float32
BF16 = mybir.dt.bfloat16
I32 = mybir.dt.int32
ACT = mybir.ActivationFunctionType
ALU = mybir.AluOpType
AXIS = mybir.AxisListType

BATCH, SEQ, EMBED = 2, 2048, 256
HEADS, HEAD_DIM = 16, 16
VALUE_DIM = 2 * HEAD_DIM
HIDDEN = 1024
TOKENS = BATCH * SEQ
PARTS = 128
TILE = 512
SUBS = TILE // PARTS
TILES = TOKENS // TILE
BLOCKS = TOKENS // PARTS
EC = EMBED // PARTS
HC = HIDDEN // PARTS
VC = HEADS * VALUE_DIM // PARTS
KEY_BLOCKS = SEQ // PARTS
QUERY_TILES = SEQ // TILE

SCALE = 1.0 / math.sqrt(HEAD_DIM)
LAM_INIT = 0.8 - 0.6 * math.exp(-0.3 * (12 - 1))
LN_EPS = 1e-5
LOWEST = -3.0e38

PART_PAIRS = [(0, 0), (1, 0), (2, 0), (0, 1), (1, 1), (0, 2)]
SCORE_ROWS = len(PART_PAIRS) * HEAD_DIM
SHIFT_ROWS = 3
STACK_ROWS = SCORE_ROWS + SHIFT_ROWS
KINDS = ("q1", "q2", "k1", "k2")
SET_COLS = VALUE_DIM + 1
RAW_COLS = 2 * SET_COLS
SAFE_BOUND = 30.0
BOUND_MARGIN = 1.02


def layer_kernel(nc, x, wq1, wq2, wk1, wk2, wv, wo, lq1, lk1, lq2, lk2,
                 w1, s1, w2, s2, h1, hs1, h2, hs2, w3, s3, out):
    qk_parts = nc.dram_tensor("qk_parts", (len(KINDS), 3, EMBED, TOKENS), BF16, kind="Internal").ap()
    values = nc.dram_tensor("values", (HEADS, PARTS, BLOCKS, VALUE_DIM), F32, kind="Internal").ap()
    shift = nc.dram_tensor("shift", (SHIFT_ROWS, HEADS, BATCH, 2, SEQ), BF16, kind="Internal").ap()
    raw = nc.dram_tensor("raw", (BLOCKS, PARTS, HEADS, RAW_COLS), F32, kind="Internal").ap()
    mid = nc.dram_tensor("mid", (BLOCKS, PARTS, EMBED), F32, kind="Internal").ap()
    mid_t = nc.dram_tensor("mid_t", (EC, PARTS, TOKENS), F32, kind="Internal").ap()

    with ExitStack() as ctx:
        def sb(name, shape, dt=F32):
            return ctx.enter_context(nc.sbuf_tensor(name, shape, dt))

        keep = dict(
            w1t=sb("w1t", [PARTS, EC, HIDDEN]), w2t=sb("w2t", [PARTS, EC, HIDDEN]),
            h1t=sb("h1t", [PARTS, HC, HIDDEN]), h2t=sb("h2t", [PARTS, HC, HIDDEN]),
            w3t=sb("w3t", [PARTS, HC, EMBED]),
            s1=sb("s1", [PARTS, HC]), s2=sb("s2", [PARTS, HC]), hs1=sb("hs1", [PARTS, HC]), hs2=sb("hs2", [PARTS, HC]),
            s3=sb("s3", [PARTS, EMBED]),
            ident=sb("ident", [PARTS, PARTS]), neg_lam=sb("neg_lam", [PARTS, HEADS]),
            bound=sb("bound", [PARTS, 4]), exact=sb("exact", [PARTS, 1], I32),
        )
        project_phase(nc, keep, x, (wq1, wq2, wk1, wk2), wv, (lq1, lk1, lq2, lk2),
                      (w1, w2, h1, h2, w3), (s1, s2, hs1, hs2, s3), qk_parts, values)
        maximum_phase(nc, keep, qk_parts, shift)
        attention_phase(nc, keep, qk_parts, shift, values, raw)
        merge_phase(nc, keep, x, wo, raw, mid, mid_t)
        ffn_phase(nc, keep, mid, mid_t, out)


class Room:

    def __init__(self, nc, phase):
        self.nc, self.phase, self.ctx = nc, phase, ExitStack()

    def __enter__(self):
        return self

    def __exit__(self, *a):
        return self.ctx.__exit__(*a)

    def sb(self, name, shape, dt=F32):
        return self.ctx.enter_context(self.nc.sbuf_tensor(f"{self.phase}_{name}", shape, dt))

    def ps(self, name, shape):
        return self.ctx.enter_context(self.nc.psum_tensor(f"{self.phase}_{name}", shape, F32))

    def sem(self, name):
        return self.ctx.enter_context(self.nc.semaphore(f"{self.phase}_{name}"))

    def block(self):
        return self.ctx.enter_context(self.nc.Block())


def give_credits(nc, credits):
    with nc.Block() as block:
        @block.sync
        def _(sp):
            for sem, n in credits:
                sp.sem_inc(sem, n)


def project_phase(nc, keep, x, w_qk, wv, lam_in, ffn_w, ffn_s, qk_parts, values):
    w1, w2, h1, h2, w3 = ffn_w
    s1, s2, hs1, hs2, s3 = ffn_s
    M_TILES = len(KINDS) * EC
    x_v = x.rearrange("b (t s p) e -> (b t) p s e", s=SUBS, p=PARTS)
    with Room(nc, "proj") as room:
        wqk_sb = room.sb("wqk", [PARTS, len(KINDS), EC, EMBED])
        wv_sb = room.sb("wv", [PARTS, EC * HEADS, VALUE_DIM])
        wv_mean = room.sb("wv_mean", [PARTS, EC * HEADS])
        lam_sb = room.sb("lam", [PARTS, 4, HEADS * HEAD_DIM])
        lam_sum = room.sb("lam_sum", [PARTS, 2, HEADS])
        lam_exp = room.sb("lam_exp", [PARTS, 2, HEADS])
        x_sb = [room.sb(f"x{u}", [PARTS, SUBS, EMBED]) for u in range(2)]
        xt = [room.sb(f"xt{u}", [PARTS, EC, TILE]) for u in range(2)]
        parts = [room.sb(f"parts{n}", [PARTS, 3, TILE], BF16) for n in range(4)]
        resid = room.sb("resid", [PARTS, TILE])
        biggest = room.sb("biggest", [PARTS, len(KINDS), TILE], BF16)
        smallest = room.sb("smallest", [PARTS, len(KINDS), TILE], BF16)
        small_col = room.sb("small_col", [PARTS, len(KINDS)])
        big_col = room.sb("big_col", [PARTS, len(KINDS)])
        big_all = room.sb("big_all", [PARTS, len(KINDS)])
        v_sb = [room.sb(f"v{u}", [PARTS, HEADS, SUBS, VALUE_DIM]) for u in range(2)]
        w_rows = [room.sb(f"w_rows{u}", [PARTS, 2 * EMBED + 2 * HIDDEN]) for u in range(2)]
        w3_rows = room.sb("w3_rows", [PARTS, EC, HIDDEN])
        ident = keep["ident"]
        xt_ps = room.ps("xt_ps", [PARTS, EC, TILE])
        qk_ps = [room.ps(f"qk_ps{n}", [PARTS, TILE]) for n in range(2)]
        v_ps = [room.ps(f"v_ps{n}", [PARTS, HEADS, VALUE_DIM]) for n in range(2)]
        w_ps = [room.ps(f"w_ps{n}", [PARTS, 4, PARTS]) for n in range(2)]

        const_loaded = room.sem("const_loaded")
        wv_loaded = room.sem("wv_loaded")
        lam_loaded = room.sem("lam_loaded")
        w3_loaded = room.sem("w3_loaded")
        x_loaded = [room.sem(f"x_loaded{u}") for u in range(2)]
        w_loaded = [room.sem(f"w_loaded{u}") for u in range(2)]
        ident_done = room.sem("ident_done")
        prep_done = room.sem("prep_done")
        ones_done = room.sem("ones_done")
        lam_ready = room.sem("lam_ready")
        exp_done = room.sem("exp_done")
        x_transposed = room.sem("x_transposed")
        xt_ready = room.sem("xt_ready")
        xt_free = room.sem("xt_free")
        w_transposed = room.sem("w_transposed")
        w_bank_free = room.sem("w_bank_free")
        qk_projected = room.sem("qk_projected")
        qk_bank_free = room.sem("qk_bank_free")
        high_ready = room.sem("high_ready")
        mid_ready = room.sem("mid_ready")
        parts_ready = room.sem("parts_ready")
        parts_stored = [room.sem(f"parts_stored{n}") for n in range(4)]
        biggest_done = room.sem("biggest_done")
        v_projected = room.sem("v_projected")
        v_bank_free = room.sem("v_bank_free")
        v_stored = [room.sem(f"v_stored{u}") for u in range(2)]
        big_ready = room.sem("big_ready")
        big_reduced = room.sem("big_reduced")
        flag_steps = room.sem("flag_steps")

        groups = [(0, "w1t", 0, EC), (EMBED, "w2t", 0, EC)]
        for n, name in enumerate(("h1t", "h2t")):
            for c in range(0, HC, 4):
                groups.append((2 * EMBED + n * HIDDEN + c * PARTS, name, c, 4))
        G = len(groups)
        w3_groups = [(o, c) for o in range(EC) for c in range(0, HC, 4)]

        give_credits(nc, [(xt_free, 2), (w_bank_free, 2), (qk_bank_free, 2), (v_bank_free, 2)])
        block = room.block()

        @block.sync
        def _(sp):
            def load_x(t, u):
                sp.dma_start(x_sb[u][:, :, :], x_v[t]).then_inc(x_loaded[u], 16)

            def load_w(t, u):
                rows = bass.ts(t, PARTS)
                col = 0
                for w in (w1, w2, h1, h2):
                    n = w.shape[1]
                    sp.dma_start(w_rows[u][:, col:col + n], w[rows, :]).then_inc(w_loaded[u], 16)
                    col += n

            def tile(i, u, last):
                t = 2 * i + u
                for m in range(M_TILES):
                    kind, c = divmod(m, EC)
                    sp.wait_ge(parts_ready, M_TILES * t + m + 1)
                    sp.dma_start(qk_parts[kind, :, c * PARTS:(c + 1) * PARTS, bass.ts(t, TILE)].rearrange("a p n -> p a n"),
                                 parts[m % 4][:, :, :]).then_inc(parts_stored[m % 4], 16)
                sp.wait_ge(v_bank_free, 2 + SUBS * t + SUBS)
                sp.dma_start(values[:, :, bass.ts(t, SUBS), :].rearrange("h p s d -> p h (s d)"),
                             v_sb[u][:, :, :, :].rearrange("p h s d -> p h (s d)")).then_inc(v_stored[u], 16)
                if not last:
                    sp.wait_ge(x_transposed, t + 1)
                    load_x(t + 2, u)
                    sp.wait_ge(w_transposed, G * t + G)
                    load_w(t + 2, u)

            load_x(0, 0)
            load_x(1, 1)
            load_w(0, 0)
            load_w(1, 1)
            with sp.Fori(0, TILES // 2 - 1) as i:
                for u in range(2):
                    tile(i, u, False)
            for u in range(2):
                tile(TILES // 2 - 1, u, True)
            for u in range(2):
                sp.wait_ge(v_stored[u], 16 * (TILES // 2))
            for n in range(4):
                sp.wait_ge(parts_stored[n], 16 * (TILES * M_TILES // 4))

        @block.gpsimd
        def _(pool):
            pool.memset(ident[:, :], 0.0).then_inc(ident_done, 1)
            pool.wait_ge(ident_done, 1)
            pool.affine_select(out=ident[:, :], in_=ident[:, :], compare_op=ALU.not_equal, fill=1.0, base=0,
                               pattern=[[-1, PARTS]], channel_multiplier=1).then_inc(ident_done, 1)
            for u in range(2):
                pool.memset(v_sb[u][:, :, :, VALUE_DIM - 1:VALUE_DIM], 1.0).then_inc(ones_done, 1)
            pool.dma_start(keep["s3"][:, :], s3.partition_broadcast(PARTS)).then_inc(lam_loaded, 16)
            for n, v in enumerate(lam_in):
                pool.dma_start(lam_sb[:, n, :], v.rearrange("h d -> (h d)").partition_broadcast(PARTS)).then_inc(lam_loaded, 16)
            pool.wait_ge(big_ready, 1)
            pool.partition_all_reduce(big_all[:, :], big_col[:, :], PARTS, bass.bass_isa.ReduceOp.max).then_inc(big_reduced, 1)

        @block.scalar
        def _(act):
            act.dma_start(wv_sb[:, :, :].rearrange("p (c h) d -> p c (h d)", c=EC),
                          wv.rearrange("(c p) n -> p c n", p=PARTS)).then_inc(wv_loaded, 16)
            for n, w in enumerate(w_qk):
                act.dma_start(wqk_sb[:, n, :, :], w.rearrange("(c p) n -> p c n", p=PARTS)).then_inc(const_loaded, 16)
            with nc.allow_non_contiguous_dma(reason="small vectors of scales"):
                for name, s in (("s1", s1), ("s2", s2), ("hs1", hs1), ("hs2", hs2)):
                    act.dma_start(keep[name][:, :], s.rearrange("(c p) -> p c", p=PARTS)).then_inc(const_loaded, 16)
            act.dma_start(w3_rows[:, :, :], w3.rearrange("(o p) i -> p o i", p=PARTS)).then_inc(w3_loaded, 16)
            act.wait_ge(lam_ready, 4)
            nc.scalar.activation(lam_exp[:, :, :], lam_sum[:, :, :], ACT.Exp).then_inc(exp_done, 1)
            for n, (o, c) in enumerate(w3_groups):
                act.wait_ge(w_transposed, n + 1)
                nc.scalar.copy(keep["w3t"][:, c:c + 4, o * PARTS:(o + 1) * PARTS], w_ps[n % 2][:, :, :]).then_inc(w_bank_free, 1)
            w0 = len(w3_groups)
            act.wait_ge(ones_done, 2)
            with act.Fori(0, TILES // 2) as i:
                for u in range(2):
                    t = 2 * i + u
                    act.wait_ge(x_transposed, t + 1)
                    act.wait_ge(xt_free, t + 1)
                    nc.scalar.copy(xt[u][:, 0, :], xt_ps[:, 0, :]).then_inc(xt_ready, 1)
                    for g, (_, name, c, n) in enumerate(groups):
                        act.wait_ge(w_transposed, w0 + G * t + g + 1)
                        nc.scalar.copy(keep[name][:, c:c + n, bass.ts(t, PARTS)], w_ps[(w0 + G * u + g) % 2][:, 0:n, :]).then_inc(w_bank_free, 1)
                    for m in range(M_TILES):
                        act.wait_ge(qk_projected, M_TILES * t + m + 1)
                        act.wait_ge(parts_stored[m % 4], 16 * (t * (M_TILES // 4) + m // 4))
                        nc.scalar.copy(parts[m % 4][:, 0, :], qk_ps[m % 2][:, :]).then_inc(high_ready, 1)
                    act.wait_ge(v_stored[u], 16 * i)
                    for s in range(SUBS):
                        act.wait_ge(v_projected, SUBS * t + s + 1)
                        nc.scalar.copy(v_sb[u][:, :, s, 0:VALUE_DIM - 1], v_ps[s % 2][:, :, 0:VALUE_DIM - 1]).then_inc(v_bank_free, 1)

        @block.vector
        def _(dve):
            dve.wait_ge(wv_loaded, 16)
            nc.vector.tensor_reduce(wv_mean[:, :], wv_sb[:, :, :], AXIS.X, ALU.add).then_inc(prep_done, 1)
            nc.vector.memset(biggest[:, :, :], 0.0).then_inc(biggest_done, 1)
            nc.vector.memset(smallest[:, :, :], 0.0).then_inc(biggest_done, 1)
            dve.wait_ge(prep_done, 1)
            nc.vector.scalar_tensor_tensor(wv_sb[:, :, :], wv_mean[:, :].unsqueeze(2).to_broadcast([PARTS, EC * HEADS, VALUE_DIM]),
                                           -1.0 / VALUE_DIM, wv_sb[:, :, :], ALU.mult, ALU.add).then_inc(prep_done, 1)
            dve.wait_ge(lam_loaded, 16 * 5)
            for n in range(2):
                nc.vector.tensor_tensor(lam_sb[:, 2 * n, :], lam_sb[:, 2 * n, :], lam_sb[:, 2 * n + 1, :], ALU.mult).then_inc(lam_ready, 1)
            dve.wait_ge(lam_ready, 2)
            for n in range(2):
                nc.vector.tensor_reduce(lam_sum[:, n, :], lam_sb[:, 2 * n, :].rearrange("p (h d) -> p h d", h=HEADS), AXIS.X, ALU.add).then_inc(lam_ready, 1)
            dve.wait_ge(exp_done, 1)
            nc.vector.scalar_tensor_tensor(keep["neg_lam"][:, :], lam_exp[:, 1, :], -LAM_INIT, lam_exp[:, 0, :], ALU.add, ALU.subtract)
            with dve.Fori(0, TILES // 2) as i:
                for u in range(2):
                    t = 2 * i + u
                    dve.wait_ge(x_transposed, t + 1)
                    dve.wait_ge(xt_free, t + 1)
                    nc.vector.tensor_copy(xt[u][:, 1, :], xt_ps[:, 1, :]).then_inc(xt_ready, 1)
                    for m in range(M_TILES):
                        kind = m // EC
                        n = M_TILES * t + m
                        p = parts[m % 4]
                        dve.wait_ge(high_ready, n + 1)
                        dve.wait_ge(parts_ready, n)
                        nc.vector.tensor_tensor(resid[:, :], qk_ps[m % 2][:, :], p[:, 0, :], ALU.subtract).then_inc(qk_bank_free, 1)
                        dve.wait_ge(biggest_done, 2 * n + 2)
                        nc.vector.tensor_tensor(biggest[:, kind, :], biggest[:, kind, :], p[:, 0, :], ALU.max).then_inc(biggest_done, 1)
                        nc.vector.tensor_tensor(smallest[:, kind, :], smallest[:, kind, :], p[:, 0, :], ALU.min).then_inc(biggest_done, 1)
                        dve.wait_ge(qk_bank_free, 2 + n + 1)
                        nc.vector.tensor_copy(p[:, 1, :], resid[:, :]).then_inc(mid_ready, 1)
                        dve.wait_ge(mid_ready, n + 1)
                        nc.vector.tensor_tensor(p[:, 2, :], resid[:, :], p[:, 1, :], ALU.subtract).then_inc(parts_ready, 1)
            dve.wait_ge(biggest_done, 2 + 2 * TILES * M_TILES)
            nc.vector.tensor_reduce(big_col[:, :], biggest[:, :, :], AXIS.X, ALU.max).then_inc(flag_steps, 1)
            nc.vector.tensor_reduce(small_col[:, :], smallest[:, :, :], AXIS.X, ALU.min).then_inc(flag_steps, 1)
            dve.wait_ge(flag_steps, 2)
            nc.vector.scalar_tensor_tensor(big_col[:, :], small_col[:, :], -1.0, big_col[:, :], ALU.mult, ALU.max).then_inc(big_ready, 1)
            dve.wait_ge(big_reduced, 1)
            bound = keep["bound"]
            nc.vector.tensor_tensor(bound[:, 0:2], big_all[:, 0:2], big_all[:, 2:4], ALU.mult).then_inc(flag_steps, 1)
            dve.wait_ge(flag_steps, 3)
            nc.vector.tensor_tensor(bound[:, 2:3], bound[:, 0:1], bound[:, 1:2], ALU.max).then_inc(flag_steps, 1)
            dve.wait_ge(flag_steps, 4)
            nc.vector.tensor_scalar(bound[:, 3:4], bound[:, 2:3], HEAD_DIM * BOUND_MARGIN, None, ALU.mult).then_inc(flag_steps, 1)
            dve.wait_ge(flag_steps, 5)
            nc.vector.tensor_scalar(keep["exact"][:, :], bound[:, 3:4], SAFE_BOUND / SCALE, None, ALU.is_gt).then_inc(flag_steps, 1)
            dve.wait_ge(flag_steps, 6)

        @block.tensor
        def _(pe):
            pe.wait_ge(ident_done, 2)
            pe.wait_ge(w3_loaded, 16)
            for n, (o, c) in enumerate(w3_groups):
                pe.wait_ge(w_bank_free, n + 1)
                for k in range(4):
                    last = nc.tensor.transpose(w_ps[n % 2][:, k, :], w3_rows[:, o, (c + k) * PARTS:(c + k + 1) * PARTS], ident[:, :])
                last.then_inc(w_transposed, 1)
            w0 = len(w3_groups)
            pe.wait_ge(const_loaded, 16 * 8)
            pe.wait_ge(prep_done, 2)
            with pe.Fori(0, TILES // 2) as i:
                for u in range(2):
                    t = 2 * i + u
                    pe.wait_ge(x_loaded[u], 16 * i + 16)
                    pe.wait_ge(xt_ready, EC * t)
                    for c in range(EC):
                        for s in range(SUBS):
                            last = nc.tensor.transpose(xt_ps[:, c, s * PARTS:(s + 1) * PARTS], x_sb[u][:, s, c * PARTS:(c + 1) * PARTS], ident[:, :])
                    last.then_inc(x_transposed, 1)
                    pe.wait_ge(w_loaded[u], 64 * i + 64)
                    for g, (col, _, _, n) in enumerate(groups):
                        bank = w_ps[(w0 + G * u + g) % 2]
                        pe.wait_ge(w_bank_free, w0 + G * t + g + 1)
                        for k in range(n):
                            last = nc.tensor.transpose(bank[:, k, :], w_rows[u][:, col + k * PARTS:col + (k + 1) * PARTS], ident[:, :])
                        last.then_inc(w_transposed, 1)
                    pe.wait_ge(xt_ready, EC * t + EC)
                    for m in range(M_TILES):
                        kind, o = divmod(m, EC)
                        pe.wait_ge(qk_bank_free, M_TILES * t + m + 1)
                        for c in range(EC):
                            last = nc.tensor.matmul(qk_ps[m % 2][:, :], wqk_sb[:, kind, c, o * PARTS:(o + 1) * PARTS], xt[u][:, c, :],
                                                    start=(c == 0), stop=(c == EC - 1))
                        last.then_inc(qk_projected, 1)
                    for s in range(SUBS):
                        pe.wait_ge(v_bank_free, SUBS * t + s + 1)
                        for c in range(EC):
                            last = nc.tensor.matmul(v_ps[s % 2][:, :, :], xt[u][:, c, s * PARTS:(s + 1) * PARTS],
                                                    wv_sb[:, c * HEADS:(c + 1) * HEADS, :], start=(c == 0), stop=(c == EC - 1))
                        last.then_inc(v_projected, 1)
                    pe.wait_ge(v_projected, SUBS * t + SUBS)
                    pe.sem_inc(xt_free, 1)


def load_stack(dma, stack, qk_parts, sem, kind, which, head, b):
    for n, pair in enumerate(PART_PAIRS):
        dma(stack[n * HEAD_DIM:(n + 1) * HEAD_DIM, :],
            qk_parts[kind, pair[which], bass.ts(head, HEAD_DIM), b * SEQ:(b + 1) * SEQ]).then_inc(sem, 16)


STACK_DMAS = 4 * len(PART_PAIRS)


def maximum_phase(nc, keep, qk_parts, shift):
    CHUNKS = [(qb, s, c) for qb in range(KEY_BLOCKS) for s in range(2) for c in range(qb // SUBS + 1)]
    NCH = len(CHUNKS)
    BANKS = 4
    with Room(nc, "max") as room:
        q_sb = [room.sb(f"q{u}", [SCORE_ROWS, 2, SEQ], BF16) for u in range(2)]
        k_sb = [room.sb(f"k{u}", [SCORE_ROWS, 2, SEQ], BF16) for u in range(2)]
        future = room.sb("future", [PARTS, PARTS], BF16)
        ident_b = room.sb("ident_b", [PARTS, PARTS], BF16)
        chunk_max = room.sb("chunk_max", [PARTS, 2, KEY_BLOCKS, QUERY_TILES])
        row_max = room.sb("row_max", [PARTS, 2 * KEY_BLOCKS])
        neg = room.sb("neg", [2 * KEY_BLOCKS, PARTS])
        rest = room.sb("rest", [2 * KEY_BLOCKS, PARTS])
        neg_parts = room.sb("neg_parts", [2 * KEY_BLOCKS, 3, PARTS], BF16)
        fill = room.sb("fill", [PARTS, 2, HEADS * BATCH * 2 * SEQ // PARTS], BF16)
        s_ps = [room.ps(f"s_ps{n}", [PARTS, TILE]) for n in range(BANKS)]
        t_ps = room.ps("t_ps", [2 * KEY_BLOCKS, PARTS])

        const_done = room.sem("const_done")
        loaded = [room.sem(f"loaded{u}") for u in range(2)]
        scored = room.sem("scored")
        bank_free = room.sem("bank_free")
        reduced = room.sem("reduced")
        row_ready = room.sem("row_ready")
        transposed = room.sem("transposed")
        cut = room.sem("cut")
        stored = room.sem("stored")
        filled = room.sem("filled")
        fill_ready = room.sem("fill_ready")
        CUTS = 4

        give_credits(nc, [(bank_free, BANKS)])
        block = room.block()

        @block.gpsimd
        def _(pool):
            exact = pool.value_load(keep["exact"][0:1, 0:1])
            with pool.If(exact != 0):
                pool.memset(future[:, :], 0.0).then_inc(const_done, 1)
                pool.memset(ident_b[:, :], 0.0).then_inc(const_done, 1)
                pool.wait_ge(const_done, 2)
                pool.affine_select(out=future[:, :], in_=future[:, :], compare_op=ALU.is_ge, fill=LOWEST, base=0,
                                   pattern=[[-1, PARTS]], channel_multiplier=1).then_inc(const_done, 1)
                pool.affine_select(out=ident_b[:, :], in_=ident_b[:, :], compare_op=ALU.not_equal, fill=1.0, base=0,
                                   pattern=[[-1, PARTS]], channel_multiplier=1).then_inc(const_done, 1)

        @block.sync
        def _(sp):
            exact = sp.value_load(keep["exact"][0:1, 0:1])
            flat = shift.rearrange("a h b s (r n) -> a (h b s r) n", n=PARTS)
            with sp.If(exact != 0):
                with sp.Fori(0, HEADS) as h:
                    for b in range(BATCH):
                        sp.wait_ge(scored, (h * BATCH) * NCH)
                        for kind, (buf, s) in enumerate([(q_sb, 0), (q_sb, 1), (k_sb, 0), (k_sb, 1)]):
                            load_stack(sp.dma_start, buf[b][:, s, :], qk_parts, loaded[b], kind, kind // 2, h, b)
                    for b in range(BATCH):
                        n = h * BATCH + b
                        sp.wait_ge(cut, CUTS * n + CUTS)
                        sp.dma_start(flat[:, bass.ts(n, 2 * KEY_BLOCKS), :].rearrange("a r n -> r a n"), neg_parts[:, :, :]).then_inc(stored, 16)
                sp.wait_ge(stored, 16 * HEADS * BATCH)
            with sp.If(exact == 0):
                sp.wait_ge(fill_ready, 2)
                for a in range(SHIFT_ROWS):
                    sp.dma_start(shift[a].rearrange("h b s n -> (h b s n)").rearrange("(p n) -> p n", p=PARTS),
                                 fill[:, min(a, 1), :]).then_inc(filled, 16)
                sp.wait_ge(filled, 16 * SHIFT_ROWS)

        @block.tensor
        def _(pe):
            exact = pe.value_load(keep["exact"][0:1, 0:1])
            with pe.If(exact != 0):
                pe.wait_ge(const_done, 4)
                with pe.Fori(0, HEADS) as h:
                    for b in range(BATCH):
                        n = h * BATCH + b
                        pe.wait_ge(loaded[b], 16 * STACK_DMAS * h + 16 * STACK_DMAS)
                        for m, (qb, s, c) in enumerate(CHUNKS):
                            cols = min(TILE, (qb + 1) * PARTS - c * TILE)
                            bank = s_ps[m % BANKS]
                            on_diagonal = c == qb // SUBS
                            pe.wait_ge(bank_free, n * NCH + m + 1)
                            last = nc.tensor.matmul(bank[:, 0:cols], q_sb[b][:, s, qb * PARTS:(qb + 1) * PARTS],
                                                    k_sb[b][:, s, c * TILE:c * TILE + cols], start=True, stop=not on_diagonal)
                            if on_diagonal:
                                last = nc.tensor.matmul(bank[:, cols - PARTS:cols], ident_b[:, :], future[:, :], start=False, stop=True)
                            last.then_inc(scored, 1)
                        pe.wait_ge(row_ready, n + 1)
                        pe.wait_ge(cut, CUTS * n)
                        nc.tensor.transpose(t_ps[:, :], row_max[:, :], keep["ident"][:, :]).then_inc(transposed, 1)

        @block.vector
        def _(dve):
            exact = dve.value_load(keep["exact"][0:1, 0:1])
            with dve.If(exact != 0):
                nc.vector.memset(chunk_max[:, :, :, :], LOWEST).then_inc(reduced, 1)
                dve.wait_ge(reduced, 1)
                with dve.Fori(0, HEADS) as h:
                    for b in range(BATCH):
                        n = h * BATCH + b
                        for m, (qb, s, c) in enumerate(CHUNKS):
                            cols = min(TILE, (qb + 1) * PARTS - c * TILE)
                            dve.wait_ge(scored, n * NCH + m + 1)
                            nc.vector.tensor_reduce(chunk_max[:, s, qb, c:c + 1], s_ps[m % BANKS][:, 0:cols], AXIS.X, ALU.max).then_inc(bank_free, 1)
                        dve.wait_ge(bank_free, BANKS + n * NCH + NCH)
                        dve.wait_ge(transposed, n)
                        nc.vector.tensor_reduce(row_max[:, :].rearrange("p (s q) -> p s q", s=2), chunk_max[:, :, :, :], AXIS.X, ALU.max).then_inc(row_ready, 1)
                        dve.wait_ge(transposed, n + 1)
                        dve.wait_ge(stored, 16 * n)
                        nc.vector.tensor_scalar(neg[:, :], t_ps[:, :], -1.0, None, ALU.mult).then_inc(cut, 1)
                        dve.wait_ge(cut, CUTS * n + 1)
                        nc.vector.tensor_copy(neg_parts[:, 0, :], neg[:, :]).then_inc(cut, 1)
                        dve.wait_ge(cut, CUTS * n + 2)
                        nc.vector.tensor_tensor(rest[:, :], neg[:, :], neg_parts[:, 0, :], ALU.subtract).then_inc(reduced, 1)
                        dve.wait_ge(reduced, 1 + n + 1)
                        nc.vector.tensor_copy(neg_parts[:, 1, :], rest[:, :]).then_inc(cut, 1)
                        dve.wait_ge(cut, CUTS * n + 3)
                        nc.vector.tensor_tensor(neg_parts[:, 2, :], rest[:, :], neg_parts[:, 1, :], ALU.subtract).then_inc(cut, 1)
            with dve.If(exact == 0):
                nc.vector.memset(fill[:, :, :], 0.0).then_inc(fill_ready, 1)
                dve.wait_ge(fill_ready, 1)
                nc.vector.tensor_scalar(fill[:, 0, :], fill[:, 1, :], keep["bound"][:, 3:4], -1.0, ALU.add, ALU.mult).then_inc(fill_ready, 1)


def attention_phase(nc, keep, qk_parts, shift, values, raw):
    PAIRS = [(t, p) for t in range(QUERY_TILES) for p in range(SUBS * (t + 1) // 2)]
    NP = len(PAIRS)
    STEPS = [(b, t, p) for b in range(BATCH) for t, p in PAIRS]
    NS = len(STEPS)
    NT = BATCH * QUERY_TILES
    DIAG = SUBS // 2
    LOADS = STACK_DMAS + 2 + 1

    def window(t, j):
        return max(0, j - SUBS * t) * PARTS

    def is_last(t, p):
        return p == SUBS * (t + 1) // 2 - 1

    with Room(nc, "attn") as room:
        q_sb = [room.sb(f"q{b}", [STACK_ROWS, 2, SEQ], BF16) for b in range(BATCH)]
        k_sb = [room.sb(f"k{b}", [STACK_ROWS, 2, SEQ], BF16) for b in range(BATCH)]
        v_sb = [room.sb(f"v{b}", [PARTS, KEY_BLOCKS, VALUE_DIM]) for b in range(BATCH)]
        probs = [room.sb(f"probs{n}", [PARTS, 2, 2, TILE]) for n in range(2)]
        zeros = room.sb("zeros", [PARTS, VALUE_DIM])
        sums_sb = room.sb("sums_sb", [PARTS, TILE])
        combine = room.sb("combine", [PARTS, 2, SET_COLS])
        raw_sb = [room.sb(f"raw{b}", [PARTS, KEY_BLOCKS, RAW_COLS]) for b in range(BATCH)]
        s_ps = [room.ps(f"s_ps{n}", [PARTS, 2, TILE]) for n in range(2)]
        sums_ps = [room.ps(f"sums_ps{n}", [PARTS, TILE]) for n in range(2)]
        raw_ps = room.ps("raw_ps", [PARTS, SUBS, RAW_COLS])

        const_done = room.sem("const_done")
        loaded = [room.sem(f"loaded{b}") for b in range(BATCH)]
        scored = room.sem("scored")
        exp_done = room.sem("exp_done")
        mask_begun = room.sem("mask_begun")
        masked = room.sem("masked")
        probs_free = room.sem("probs_free")
        sums_copied = room.sem("sums_copied")
        combined = room.sem("combined")
        raw_done = room.sem("raw_done")
        raw_stored = [room.sem(f"raw_stored{b}") for b in range(BATCH)]

        CONSTS = BATCH + 2 + 4 * 4
        give_credits(nc, [(probs_free, 2)])
        block = room.block()

        @block.sync
        def _(sp):
            def load(h, b):
                for kind, (buf, s) in enumerate([(q_sb, 0), (q_sb, 1), (k_sb, 0), (k_sb, 1)]):
                    load_stack(sp.dma_start, buf[b][0:SCORE_ROWS, s, :], qk_parts, loaded[b], kind, kind // 2, h, b)
                for s in range(2):
                    sp.dma_start(q_sb[b][SCORE_ROWS:STACK_ROWS, s, :], shift[:, h, b, s, :]).then_inc(loaded[b], 16)
                sp.dma_start(v_sb[b][:, :, :], values[h, :, b * KEY_BLOCKS:(b + 1) * KEY_BLOCKS, :]).then_inc(loaded[b], 16)

            def store(h, b):
                sp.wait_ge(raw_done, NT * h + QUERY_TILES * (b + 1))
                sp.dma_start(raw[b * KEY_BLOCKS:(b + 1) * KEY_BLOCKS, :, h, :].rearrange("k p n -> p k n"), raw_sb[b][:, :, :]).then_inc(raw_stored[b], 16)

            for b in range(BATCH):
                load(0, b)
            with sp.Fori(0, HEADS - 1) as h:
                for b in range(BATCH):
                    sp.wait_ge(probs_free, 2 + NS * h + NP * (b + 1))
                    load(h + 1, b)
                    store(h, b)
            for b in range(BATCH):
                store(HEADS - 1, b)
            for b in range(BATCH):
                sp.wait_ge(raw_stored[b], 16 * HEADS)

        @block.gpsimd
        def _(pool):
            for b in range(BATCH):
                pool.memset(k_sb[b][SCORE_ROWS:STACK_ROWS, :, :], 1.0).then_inc(const_done, 1)
                pool.wait_ge(const_done, b + 1)
            pool.memset(zeros[:, :], 0.0).then_inc(const_done, 1)
            pool.memset(combine[:, :, :], 0.0).then_inc(const_done, 1)
            pool.wait_ge(const_done, BATCH + 2)
            steps = BATCH + 2
            for parity in range(2):
                for s in range(2):
                    rows = combine[(2 * parity + s) * VALUE_DIM:(2 * parity + s + 1) * VALUE_DIM, s, :]
                    pool.memset(rows[:, VALUE_DIM - 1:VALUE_DIM], -1.0).then_inc(const_done, 1)
                    steps += 1
                    pool.wait_ge(const_done, steps)
                    pool.affine_select(out=rows[:, 0:VALUE_DIM - 1], in_=rows[:, 0:VALUE_DIM - 1], compare_op=ALU.not_equal, fill=1.0,
                                       base=0, pattern=[[-1, VALUE_DIM - 1]], channel_multiplier=1).then_inc(const_done, 1)
                    steps += 1
                    pool.wait_ge(const_done, steps)
                    pool.affine_select(out=rows[:, VALUE_DIM - 1:VALUE_DIM], in_=rows[:, VALUE_DIM - 1:VALUE_DIM], compare_op=ALU.not_equal, fill=0.0,
                                       base=1 - VALUE_DIM, pattern=[[0, 1]], channel_multiplier=1).then_inc(const_done, 1)
                    steps += 1
                    pool.wait_ge(const_done, steps)
                    pool.affine_select(out=rows[:, VALUE_DIM:SET_COLS], in_=rows[:, VALUE_DIM:SET_COLS], compare_op=ALU.not_equal, fill=1.0,
                                       base=1 - VALUE_DIM, pattern=[[0, 1]], channel_multiplier=1).then_inc(const_done, 1)
                    steps += 1
                    pool.wait_ge(const_done, steps)
            with pool.Fori(0, HEADS) as h:
                n = 0
                for k, (b, t, p) in enumerate(STEPS):
                    for par in range(2):
                        j = 2 * p + par
                        if j < SUBS * t:
                            continue
                        off = window(t, j)
                        pool.wait_ge(exp_done, 2 * NS * h + 2 * k + par + 1)
                        pool.sem_inc(mask_begun, 1)
                        block_probs = probs[k % 2][:, par, :, off:off + PARTS]
                        pool.affine_select(out=block_probs, in_=block_probs, compare_op=ALU.is_ge, fill=0.0, base=0,
                                           pattern=[[0, 2], [1, PARTS]], channel_multiplier=-1).then_inc(masked, 1)

        @block.scalar
        def _(act):
            with act.Fori(0, HEADS) as h:
                for k, (b, t, p) in enumerate(STEPS):
                    act.wait_ge(probs_free, NS * h + k + 1)
                    for par in range(2):
                        off = window(t, 2 * p + par)
                        act.wait_ge(scored, 2 * NS * h + 2 * k + par + 1)
                        nc.scalar.activation(probs[k % 2][:, par, :, off:TILE], s_ps[par][:, :, off:TILE], ACT.Exp, scale=SCALE).then_inc(exp_done, 1)

        @block.tensor
        def _(pe):
            pe.wait_ge(const_done, CONSTS)

            def scores(h, k):
                b, t, p = STEPS[k]
                if t == 0 and p == 0:
                    pe.wait_ge(loaded[b], 16 * LOADS * h + 16 * LOADS)
                for par in range(2):
                    j = 2 * p + par
                    off = window(t, j)
                    if k > 0:
                        pe.wait_ge(exp_done, 2 * NS * h + 2 * (k - 1) + par + 1)
                    for s in range(2):
                        last = nc.tensor.matmul(s_ps[par][:, s, off:TILE], k_sb[b][:, s, j * PARTS:(j + 1) * PARTS],
                                                q_sb[b][:, s, t * TILE + off:(t + 1) * TILE], start=True, stop=True)
                    last.then_inc(scored, 1)

            def weigh(h, k):
                b, t, p = STEPS[k]
                T = b * QUERY_TILES + t
                sums = sums_ps[T % 2]
                pe.wait_ge(exp_done, 2 * NS * h + 2 * k + 2)
                diagonals = SUBS * T + max(0, 2 * p + 2 - SUBS * t)
                if 2 * p + 2 > SUBS * t:
                    pe.wait_ge(masked, SUBS * NT * h + diagonals)
                if p == 0 and T >= 2:
                    pe.wait_ge(sums_copied, NT * h + T - 1)
                if p == 0 and t == 0:
                    for s in range(2):
                        nc.tensor.matmul(sums[(2 + s) * VALUE_DIM:(3 + s) * VALUE_DIM, :], zeros[:, :], probs[k % 2][:, 0, s, :],
                                         start=True, stop=False)
                for par in range(2):
                    j = 2 * p + par
                    off = window(t, j)
                    for s in range(2):
                        c = 2 * par + s
                        last = nc.tensor.matmul(sums[c * VALUE_DIM:(c + 1) * VALUE_DIM, off:TILE], v_sb[b][:, j, :],
                                                probs[k % 2][:, par, s, off:TILE],
                                                start=(p == 0 and not (t == 0 and par == 1)), stop=is_last(t, p))
                last.then_inc(probs_free, 1)

            def turn(h, T):
                pe.wait_ge(sums_copied, NT * h + T + 1)
                pe.wait_ge(raw_done, NT * h + T)
                for i in range(SUBS):
                    last = nc.tensor.matmul(raw_ps[:, i, :], sums_sb[:, i * PARTS:(i + 1) * PARTS], combine[:, :, :], start=True, stop=True)
                last.then_inc(combined, 1)

            with pe.Fori(0, HEADS) as h:
                scores(h, 0)
                ended = None
                for k in range(1, NS + 1):
                    if k < NS:
                        scores(h, k)
                    weigh(h, k - 1)
                    if ended is not None:
                        turn(h, ended)
                    b, t, p = STEPS[k - 1]
                    ended = b * QUERY_TILES + t if is_last(t, p) else None
                turn(h, ended)

        @block.vector
        def _(dve):
            with dve.Fori(0, HEADS) as h:
                for k, (b, t, p) in enumerate(STEPS):
                    if not is_last(t, p):
                        continue
                    T = b * QUERY_TILES + t
                    dve.wait_ge(probs_free, 2 + NS * h + k + 1)
                    dve.wait_ge(combined, NT * h + T)
                    nc.vector.tensor_copy(sums_sb[:, :], sums_ps[T % 2][:, :]).then_inc(sums_copied, 1)
                    if t == 0:
                        dve.wait_ge(raw_stored[b], 16 * h)
                    dve.wait_ge(combined, NT * h + T + 1)
                    nc.vector.tensor_copy(raw_sb[b][:, SUBS * t:SUBS * (t + 1), :], raw_ps[:, :, :]).then_inc(raw_done, 1)


def merge_phase(nc, keep, x, wo, raw, mid, mid_t):
    x_v = x.rearrange("b (t p) e -> (b t) p e", p=PARTS)
    D = VALUE_DIM
    with Room(nc, "merge") as room:
        wo_sb = room.sb("wo", [PARTS, VC, EMBED])
        raw_sb = [room.sb(f"raw{u}", [PARTS, HEADS, 2, SET_COLS]) for u in range(2)]
        x_sb = [room.sb(f"x{u}", [PARTS, EMBED]) for u in range(2)]
        recip = room.sb("recip", [PARTS, HEADS, 2])
        first = room.sb("first", [PARTS, HEADS, D])
        second = room.sb("second", [PARTS, HEADS, D])
        diff = room.sb("diff", [PARTS, HEADS, D])
        square = room.sb("square", [PARTS, HEADS, D])
        var = room.sb("var", [PARTS, HEADS])
        rstd = room.sb("rstd", [PARTS, HEADS])
        normed = [room.sb(f"normed{u}", [PARTS, HEADS, D]) for u in range(2)]
        normed_t = room.sb("normed_t", [PARTS, VC, PARTS])
        y = room.sb("y", [PARTS, EMBED])
        stats = room.sb("stats", [PARTS, 6])
        mean_var = room.sb("mean_var", [PARTS, 2])
        y_rstd = room.sb("y_rstd", [PARTS, 1])
        root = room.sb("root", [PARTS, HEADS])
        quotient = room.sb("quotient", [PARTS, HEADS])
        y_var = room.sb("y_var", [PARTS, 1])
        y_root = room.sb("y_root", [PARTS, 1])
        y_quotient = room.sb("y_quotient", [PARTS, 1])
        out_sb = [room.sb(f"out{u}", [PARTS, EMBED]) for u in range(2)]
        out_t = [room.sb(f"out_t{u}", [PARTS, EC, PARTS]) for u in range(2)]
        nt_ps = room.ps("nt_ps", [PARTS, VC, PARTS])
        y_ps = room.ps("y_ps", [PARTS, EMBED])
        ot_ps = room.ps("ot_ps", [PARTS, EC, PARTS])

        wo_loaded = room.sem("wo_loaded")
        loaded = [room.sem(f"loaded{u}") for u in range(2)]
        scaled2 = room.sem("scaled2")
        diff_done = room.sem("diff_done")
        squared = room.sem("squared")
        vec = room.sem("vec")
        aggr_begun = room.sem("aggr_begun")
        var_ready = room.sem("var_ready")
        root_ready = room.sem("root_ready")
        y_var_ready = room.sem("y_var_ready")
        y_root_ready = room.sem("y_root_ready")
        normed_ready = room.sem("normed_ready")
        normed_turned = room.sem("normed_turned")
        nt_ready = room.sem("nt_ready")
        projected = room.sem("projected")
        out_ready = room.sem("out_ready")
        out_turned = room.sem("out_turned")
        ot_ready = room.sem("ot_ready")
        stored = [room.sem(f"stored{u}") for u in range(2)]
        stored_t = [room.sem(f"stored_t{u}") for u in range(2)]
        VEC = 15
        block = room.block()

        @block.sync
        def _(sp):
            def load(n, u):
                sp.dma_start(raw_sb[u][:, :, :, :].rearrange("p h s c -> p h (s c)"), raw[n]).then_inc(loaded[u], 16)
                sp.dma_start(x_sb[u][:, :], x_v[n]).then_inc(loaded[u], 16)

            def block_of(i, u, last):
                n = 2 * i + u
                sp.wait_ge(out_ready, n + 1)
                sp.dma_start(mid[n], out_sb[u][:, :]).then_inc(stored[u], 16)
                if not last:
                    load(n + 2, u)
                sp.wait_ge(ot_ready, n + 1)
                sp.dma_start(mid_t[:, :, bass.ts(n, PARTS)].rearrange("c p n -> p c n"), out_t[u][:, :, :]).then_inc(stored_t[u], 16)

            sp.dma_start(wo_sb[:, :, :], wo.rearrange("(c p) n -> p c n", p=PARTS)).then_inc(wo_loaded, 16)
            for u in range(2):
                load(u, u)
            with sp.Fori(0, BLOCKS // 2 - 1) as i:
                for u in range(2):
                    block_of(i, u, False)
            for u in range(2):
                block_of(BLOCKS // 2 - 1, u, True)
            for u in range(2):
                sp.wait_ge(stored[u], 16 * (BLOCKS // 2))
                sp.wait_ge(stored_t[u], 16 * (BLOCKS // 2))

        @block.gpsimd
        def _(pool):
            with pool.Fori(0, BLOCKS // 2) as i:
                for u in range(2):
                    n = 2 * i + u
                    pool.wait_ge(vec, VEC * n + 2)
                    pool.wait_ge(diff_done, n)
                    pool.tensor_tensor(second[:, :, :], raw_sb[u][:, :, 1, 0:D], recip[:, :, 1:2].to_broadcast([PARTS, HEADS, D]), ALU.mult).then_inc(scaled2, 1)

        @block.scalar
        def _(act):
            with act.Fori(0, BLOCKS // 2) as i:
                for u in range(2):
                    n = 2 * i + u
                    act.wait_ge(diff_done, n + 1)
                    nc.scalar.activation(square[:, :, :], diff[:, :, :], ACT.Square).then_inc(squared, 1)
                    act.wait_ge(var_ready, n + 1)
                    nc.scalar.activation(root[:, :], var[:, :], ACT.Sqrt).then_inc(root_ready, 1)
                    act.wait_ge(normed_turned, n + 1)
                    nc.scalar.copy(normed_t[:, :, :], nt_ps[:, :, :]).then_inc(nt_ready, 1)
                    act.wait_ge(y_var_ready, n + 1)
                    nc.scalar.activation(y_root[:, :], y_var[:, :], ACT.Sqrt).then_inc(y_root_ready, 1)
                    act.wait_ge(out_turned, n + 1)
                    act.wait_ge(stored_t[u], 16 * i)
                    nc.scalar.copy(out_t[u][:, :, :], ot_ps[:, :, :]).then_inc(ot_ready, 1)

        @block.vector
        def _(dve):
            with dve.Fori(0, BLOCKS // 2) as i:
                for u in range(2):
                    n = 2 * i + u
                    v0 = VEC * n
                    dve.wait_ge(loaded[u], 32 * i + 32)
                    r = raw_sb[u]
                    nc.vector.reciprocal(recip[:, :, :], r[:, :, :, D]).then_inc(vec, 1)
                    dve.wait_ge(vec, v0 + 1)
                    nc.vector.tensor_tensor(recip[:, :, 1], recip[:, :, 1], keep["neg_lam"][:, :], ALU.mult).then_inc(vec, 1)
                    nc.vector.tensor_tensor(first[:, :, :], r[:, :, 0, 0:D], recip[:, :, 0:1].to_broadcast([PARTS, HEADS, D]), ALU.mult).then_inc(vec, 1)
                    dve.wait_ge(vec, v0 + 3)
                    dve.wait_ge(scaled2, n + 1)
                    nc.vector.tensor_tensor(diff[:, :, :], first[:, :, :], second[:, :, :], ALU.add).then_inc(diff_done, 1)
                    dve.wait_ge(squared, n + 1)
                    nc.vector.tensor_reduce(var[:, :], square[:, :, :], AXIS.X, ALU.add).then_inc(vec, 1)
                    dve.wait_ge(vec, v0 + 4)
                    nc.vector.tensor_scalar(var[:, :], var[:, :], 1.0 / D, LN_EPS, ALU.mult, ALU.add).then_inc(var_ready, 1)
                    dve.wait_ge(root_ready, n + 1)
                    nc.vector.reciprocal(quotient[:, :], root[:, :]).then_inc(vec, 1)
                    dve.wait_ge(vec, v0 + 5)
                    nc.vector.tensor_tensor(quotient[:, :], quotient[:, :], var[:, :], ALU.mult).then_inc(vec, 1)
                    dve.wait_ge(vec, v0 + 6)
                    nc.vector.tensor_tensor(quotient[:, :], quotient[:, :], root[:, :], ALU.add).then_inc(vec, 1)
                    dve.wait_ge(vec, v0 + 7)
                    nc.vector.reciprocal(rstd[:, :], quotient[:, :]).then_inc(vec, 1)
                    dve.wait_ge(vec, v0 + 8)
                    nc.vector.scalar_tensor_tensor(normed[u][:, :, :], diff[:, :, :], 2.0 * (1.0 - LAM_INIT),
                                                   rstd[:, :].unsqueeze(2).to_broadcast([PARTS, HEADS, D]), ALU.mult, ALU.mult).then_inc(normed_ready, 1)
                    dve.wait_ge(projected, n + 1)
                    nc.vector.tensor_tensor(y[:, :], y_ps[:, :], x_sb[u][:, :], ALU.add).then_inc(vec, 1)
                    dve.wait_ge(vec, v0 + 9)
                    nc.vector.bn_stats(stats[:, :], y[:, :]).then_inc(vec, 1)
                    dve.wait_ge(vec, v0 + 10)
                    dve.sem_inc(aggr_begun, 1)
                    nc.vector.bn_aggr(mean_var[:, :], stats[:, :]).then_inc(vec, 1)
                    dve.wait_ge(vec, v0 + 11)
                    nc.vector.tensor_scalar(y_var[:, :], mean_var[:, 1:2], LN_EPS, None, ALU.add).then_inc(y_var_ready, 1)
                    dve.wait_ge(y_root_ready, n + 1)
                    nc.vector.reciprocal(y_quotient[:, :], y_root[:, :]).then_inc(vec, 1)
                    dve.wait_ge(vec, v0 + 12)
                    nc.vector.tensor_scalar(y_quotient[:, :], y_quotient[:, :], y_var[:, 0:1], y_root[:, 0:1], ALU.mult, ALU.add).then_inc(vec, 1)
                    dve.wait_ge(vec, v0 + 13)
                    nc.vector.tensor_scalar(y_quotient[:, :], y_quotient[:, :], 0.5, None, ALU.mult).then_inc(vec, 1)
                    dve.wait_ge(vec, v0 + 14)
                    nc.vector.reciprocal(y_rstd[:, :], y_quotient[:, :]).then_inc(vec, 1)
                    dve.wait_ge(vec, v0 + 15)
                    dve.wait_ge(stored[u], 16 * i)
                    dve.wait_ge(out_turned, n)
                    nc.vector.tensor_scalar(out_sb[u][:, :], y[:, :], mean_var[:, 0:1], y_rstd[:, 0:1], ALU.subtract, ALU.mult).then_inc(out_ready, 1)

        @block.tensor
        def _(pe):
            ident = keep["ident"]
            pe.wait_ge(wo_loaded, 16)
            with pe.Fori(0, BLOCKS // 2) as i:
                for u in range(2):
                    n = 2 * i + u
                    pe.wait_ge(normed_ready, n + 1)
                    flat = normed[u][:, :, :].rearrange("p h d -> p (h d)")
                    for c in range(VC):
                        last = nc.tensor.transpose(nt_ps[:, c, :], flat[:, c * PARTS:(c + 1) * PARTS], ident[:, :])
                    last.then_inc(normed_turned, 1)
                    pe.wait_ge(nt_ready, n + 1)
                    for c in range(VC):
                        last = nc.tensor.matmul(y_ps[:, :], normed_t[:, c, :], wo_sb[:, c, :], start=(c == 0), stop=(c == VC - 1))
                    last.then_inc(projected, 1)
                    pe.wait_ge(out_ready, n + 1)
                    pe.wait_ge(ot_ready, n)
                    for c in range(EC):
                        last = nc.tensor.transpose(ot_ps[:, c, :], out_sb[u][:, c * PARTS:(c + 1) * PARTS], ident[:, :])
                    last.then_inc(out_turned, 1)


def ffn_phase(nc, keep, mid, mid_t, out):
    out_v = out.rearrange("b (t s p) e -> (b t) p s e", s=SUBS, p=PARTS)
    mid_v = mid.rearrange("(t s) p e -> t p s e", s=SUBS)
    with Room(nc, "ffn") as room:
        xt = [room.sb(f"xt{u}", [PARTS, EC, TILE]) for u in range(2)]
        x_sb = [room.sb(f"x{u}", [PARTS, SUBS, EMBED]) for u in range(2)]
        gate = [room.sb(f"gate{n}", [PARTS, TILE]) for n in range(2)]
        hid_a = room.sb("hid_a", [PARTS, HC, TILE])
        hid_b = room.sb("hid_b", [PARTS, HC, TILE])
        y = room.sb("y", [PARTS, SUBS, EMBED])
        stats = room.sb("stats", [PARTS, SUBS, 6])
        mean_var = room.sb("mean_var", [PARTS, SUBS, 2])
        var = room.sb("var", [PARTS, SUBS])
        root = room.sb("root", [PARTS, SUBS])
        quotient = room.sb("quotient", [PARTS, SUBS])
        rstd = room.sb("rstd", [PARTS, SUBS])
        out_sb = [room.sb(f"out{u}", [PARTS, SUBS, EMBED]) for u in range(2)]
        up_ps = [[room.ps(f"up_ps{n}{k}", [PARTS, TILE]) for k in range(2)] for n in range(2)]
        hid_ps = [room.ps(f"hid_ps{n}", [PARTS, TILE]) for n in range(2)]
        y_ps = [room.ps(f"y_ps{n}", [PARTS, EMBED]) for n in range(2)]

        loaded = [room.sem(f"loaded{u}") for u in range(2)]
        up_projected = room.sem("up_projected")
        up_free = room.sem("up_free")
        gate_ready = room.sem("gate_ready")
        hid_projected = room.sem("hid_projected")
        hid_free = room.sem("hid_free")
        y_projected = room.sem("y_projected")
        y_free = room.sem("y_free")
        vec = room.sem("vec")
        aggr_begun = room.sem("aggr_begun")
        var_ready = room.sem("var_ready")
        root_ready = room.sem("root_ready")
        out_ready = room.sem("out_ready")
        stored = [room.sem(f"stored{u}") for u in range(2)]
        VEC = 1 + SUBS + SUBS + 5
        give_credits(nc, [(up_free, 2), (hid_free, 2), (y_free, 2)])
        block = room.block()

        @block.sync
        def _(sp):
            def load(t, u):
                sp.dma_start(xt[u][:, :, :], mid_t[:, :, bass.ts(t, TILE)].rearrange("c p n -> p c n")).then_inc(loaded[u], 16)
                sp.dma_start(x_sb[u][:, :, :], mid_v[t]).then_inc(loaded[u], 16)

            def tile(i, u, last):
                t = 2 * i + u
                sp.wait_ge(out_ready, SUBS * t + SUBS)
                if not last:
                    load(t + 2, u)
                sp.dma_start(out_v[t], out_sb[u][:, :, :]).then_inc(stored[u], 16)

            for u in range(2):
                load(u, u)
            with sp.Fori(0, TILES // 2 - 1) as i:
                for u in range(2):
                    tile(i, u, False)
            for u in range(2):
                tile(TILES // 2 - 1, u, True)
            for u in range(2):
                sp.wait_ge(stored[u], 16 * (TILES // 2))

        @block.tensor
        def _(pe):
            with pe.Fori(0, TILES // 2) as i:
                for u in range(2):
                    t = 2 * i + u
                    pe.wait_ge(loaded[u], 32 * i + 32)
                    for m in range(HC):
                        cols = slice(m * PARTS, (m + 1) * PARTS)
                        pe.wait_ge(up_free, HC * t + m + 1)
                        for w, bank in zip(("w1t", "w2t"), up_ps[m % 2]):
                            for c in range(EC):
                                last = nc.tensor.matmul(bank[:, :], keep[w][:, c, cols], xt[u][:, c, :], start=(c == 0), stop=(c == EC - 1))
                        last.then_inc(up_projected, 1)
                    for layer, (w, hid, ready, first) in enumerate([("h1t", hid_a, up_free, 2 + HC * t), ("h2t", hid_b, hid_free, 2 + 2 * HC * t)]):
                        for m in range(HC):
                            pe.wait_ge(hid_free, 2 * HC * t + HC * layer + m + 1)
                            for c in range(HC):
                                if m == 0:
                                    pe.wait_ge(ready, first + c + 1)
                                last = nc.tensor.matmul(hid_ps[m % 2][:, :], keep[w][:, c, m * PARTS:(m + 1) * PARTS], hid[:, c, :],
                                                        start=(c == 0), stop=(c == HC - 1))
                            last.then_inc(hid_projected, 1)
                    for s in range(SUBS):
                        pe.wait_ge(y_free, SUBS * t + s + 1)
                        for c in range(HC):
                            if s == 0:
                                pe.wait_ge(hid_free, 2 + 2 * HC * t + HC + c + 1)
                            last = nc.tensor.matmul(y_ps[s % 2][:, :], hid_a[:, c, s * PARTS:(s + 1) * PARTS], keep["w3t"][:, c, :],
                                                    start=(c == 0), stop=(c == HC - 1))
                        last.then_inc(y_projected, 1)

        @block.scalar
        def _(act):
            with act.Fori(0, TILES // 2) as i:
                for u in range(2):
                    t = 2 * i + u
                    for m in range(HC):
                        act.wait_ge(up_projected, HC * t + m + 1)
                        nc.scalar.activation(gate[m % 2][:, :], up_ps[m % 2][0][:, :], ACT.Silu, scale=keep["s1"][:, m:m + 1]).then_inc(gate_ready, 1)
                    for layer, (hid, s) in enumerate([(hid_b, "hs1"), (hid_a, "hs2")]):
                        for m in range(HC):
                            act.wait_ge(hid_projected, 2 * HC * t + HC * layer + m + 1)
                            nc.scalar.activation(hid[:, m, :], hid_ps[m % 2][:, :], ACT.Gelu, scale=keep[s][:, m:m + 1]).then_inc(hid_free, 1)
                    act.wait_ge(var_ready, t + 1)
                    nc.scalar.activation(root[:, :], var[:, :], ACT.Sqrt).then_inc(root_ready, 1)

        @block.vector
        def _(dve):
            with dve.Fori(0, TILES // 2) as i:
                for u in range(2):
                    t = 2 * i + u
                    for m in range(HC):
                        dve.wait_ge(gate_ready, HC * t + m + 1)
                        nc.vector.scalar_tensor_tensor(hid_a[:, m, :], up_ps[m % 2][1][:, :], keep["s2"][:, m:m + 1], gate[m % 2][:, :],
                                                       ALU.mult, ALU.mult).then_inc(up_free, 1)
                    dve.wait_ge(out_ready, SUBS * t)
                    for s in range(SUBS):
                        dve.wait_ge(y_projected, SUBS * t + s + 1)
                        nc.vector.tensor_tensor(y[:, s, :], y_ps[s % 2][:, :], keep["s3"][:, :], ALU.mult).then_inc(y_free, 1)
                    v0 = VEC * t
                    dve.wait_ge(y_free, 2 + SUBS * t + SUBS)
                    nc.vector.tensor_tensor(y[:, :, :], y[:, :, :], x_sb[u][:, :, :], ALU.add).then_inc(vec, 1)
                    dve.wait_ge(vec, v0 + 1)
                    for s in range(SUBS):
                        nc.vector.bn_stats(stats[:, s, :], y[:, s, :]).then_inc(vec, 1)
                    dve.wait_ge(vec, v0 + 1 + SUBS)
                    dve.sem_inc(aggr_begun, 1)
                    for s in range(SUBS):
                        nc.vector.bn_aggr(mean_var[:, s, :], stats[:, s, :]).then_inc(vec, 1)
                    dve.wait_ge(vec, v0 + 1 + 2 * SUBS)
                    nc.vector.tensor_scalar(var[:, :], mean_var[:, :, 1], LN_EPS, None, ALU.add).then_inc(var_ready, 1)
                    dve.wait_ge(root_ready, t + 1)
                    v1 = v0 + 1 + 2 * SUBS
                    nc.vector.reciprocal(quotient[:, :], root[:, :]).then_inc(vec, 1)
                    dve.wait_ge(vec, v1 + 1)
                    nc.vector.tensor_tensor(quotient[:, :], quotient[:, :], var[:, :], ALU.mult).then_inc(vec, 1)
                    dve.wait_ge(vec, v1 + 2)
                    nc.vector.tensor_tensor(quotient[:, :], quotient[:, :], root[:, :], ALU.add).then_inc(vec, 1)
                    dve.wait_ge(vec, v1 + 3)
                    nc.vector.tensor_scalar(quotient[:, :], quotient[:, :], 0.5, None, ALU.mult).then_inc(vec, 1)
                    dve.wait_ge(vec, v1 + 4)
                    nc.vector.reciprocal(rstd[:, :], quotient[:, :]).then_inc(vec, 1)
                    dve.wait_ge(vec, v1 + 5)
                    dve.wait_ge(stored[u], 16 * i)
                    for s in range(SUBS):
                        nc.vector.tensor_scalar(out_sb[u][:, s, :], y[:, s, :], mean_var[:, s, 0:1], rstd[:, s:s + 1], ALU.subtract, ALU.mult).then_inc(out_ready, 1)


INPUTS = ["L0_attn_x", "L0_attn_Wq1", "L0_attn_Wq2", "L0_attn_Wk1", "L0_attn_Wk2", "L0_attn_Wv", "L0_attn_Wo",
          "L0_attn_lq1", "L0_attn_lk1", "L0_attn_lq2", "L0_attn_lk2",
          "L0_ffn_w1_w", "L0_ffn_w1_s", "L0_ffn_w2_w", "L0_ffn_w2_s", "L0_ffn_h1_w", "L0_ffn_h1_s",
          "L0_ffn_h2_w", "L0_ffn_h2_s", "L0_ffn_w3_w", "L0_ffn_w3_s"]


def kernel(**inputs):
    import numpy as np
    import concourse.bacc as bacc
    from concourse.bass_utils import run_bass_kernel_spmd

    nc = bacc.Bacc("TRN2", target_bir_lowering=False, num_devices=1)
    arrays, args = {}, []
    for name in INPUTS:
        a = np.ascontiguousarray(inputs[name])
        arrays[f"in_{name}"] = a
        args.append(nc.dram_tensor(f"in_{name}", a.shape, mybir.dt.from_np(a.dtype), kind="ExternalInput").ap())
    out = nc.dram_tensor("out", (BATCH, SEQ, EMBED), F32, kind="ExternalOutput").ap()
    layer_kernel(nc, *args, out)
    result = run_bass_kernel_spmd(nc, [arrays], core_ids=[0])
    return result.results[0]["out"]
```

```python
import math
from contextlib import ExitStack

import concourse.bass as bass
from concourse import mybir

F32 = mybir.dt.float32
F32R = mybir.dt.float32r
BF16 = mybir.dt.bfloat16
I32 = mybir.dt.int32
ACT = mybir.ActivationFunctionType
ALU = mybir.AluOpType
AXIS = mybir.AxisListType

BATCH, SEQ, EMBED = 2, 2048, 256
HEADS, HEAD_DIM = 16, 16
VALUE_DIM = 2 * HEAD_DIM
HIDDEN = 1024
TOKENS = BATCH * SEQ
PARTS = 128
TILE = 512
SUBS = TILE // PARTS
TILES = TOKENS // TILE
BLOCKS = TOKENS // PARTS
EC = EMBED // PARTS
HC = HIDDEN // PARTS
VC = HEADS * VALUE_DIM // PARTS
KEY_BLOCKS = SEQ // PARTS
QUERY_TILES = SEQ // TILE

SCALE = 1.0 / math.sqrt(HEAD_DIM)
LAM_INIT = 0.8 - 0.6 * math.exp(-0.3 * (12 - 1))
LN_EPS = 1e-5
LOWEST = -3.0e38

PART_PAIRS = [(0, 0), (1, 0), (2, 0), (0, 1), (1, 1), (0, 2)]
SCORE_ROWS = len(PART_PAIRS) * HEAD_DIM
SHIFT_ROWS = 3
STACK_ROWS = SCORE_ROWS + SHIFT_ROWS
KINDS = ("q1", "q2", "k1", "k2")
FFN_SHAPES = [("w1t", [PARTS, EC, HIDDEN]), ("w2t", [PARTS, EC, HIDDEN]), ("h1t", [PARTS, HC, HIDDEN]),
              ("h2t", [PARTS, HC, HIDDEN]), ("w3t", [PARTS, HC, EMBED])]
ROW_COLS = 2 * EMBED + 2 * HIDDEN
TURN_GROUPS = [(0, "w1t", 0, EC), (EMBED, "w2t", 0, EC)] + [
    (2 * EMBED + n * HIDDEN + c * PARTS, name, c, 4) for n, name in enumerate(("h1t", "h2t")) for c in range(0, HC, 4)]
W3_GROUPS = [(o, c) for o in range(EC) for c in range(0, HC, 4)]
SAFE_BOUND = 30.0
BOUND_MARGIN = 1.02


def layer_kernel(nc, x, wq1, wq2, wk1, wk2, wv, wo, lq1, lk1, lq2, lk2,
                 w1, s1, w2, s2, h1, hs1, h2, hs2, w3, s3, out):
    qk_parts = nc.dram_tensor("qk_parts", (len(KINDS), 3, EMBED, TOKENS), BF16, kind="Internal").ap()
    values = nc.dram_tensor("values", (HEADS, PARTS, BLOCKS, VALUE_DIM), F32, kind="Internal").ap()
    shift = nc.dram_tensor("shift", (SHIFT_ROWS, HEADS, BATCH, 2, SEQ), BF16, kind="Internal").ap()
    diffs = nc.dram_tensor("diffs", (BLOCKS, PARTS, HEADS, VALUE_DIM), F32, kind="Internal").ap()
    mid = nc.dram_tensor("mid", (BLOCKS, PARTS, EMBED), F32, kind="Internal").ap()
    mid_t = nc.dram_tensor("mid_t", (EC, PARTS, TOKENS), F32, kind="Internal").ap()

    with ExitStack() as ctx:
        def sb(name, shape, dt=F32):
            return ctx.enter_context(nc.sbuf_tensor(name, shape, dt))

        keep = dict(
            s1=sb("s1", [PARTS, HC]), s2=sb("s2", [PARTS, HC]), hs1=sb("hs1", [PARTS, HC]), hs2=sb("hs2", [PARTS, HC]),
            s3=sb("s3", [PARTS, EMBED]),
            ident=sb("ident", [PARTS, PARTS]), neg_lam=sb("neg_lam", [PARTS, HEADS]),
            bound=sb("bound", [PARTS, 4]), exact=sb("exact", [PARTS, 1], I32), wide=sb("wide", [PARTS, 1], I32),
        )
        ffn_w = (w1, w2, h1, h2, w3)
        with ExitStack() as weights:
            rounded = {name: weights.enter_context(nc.sbuf_tensor(f"{name}_r", shape, F32R)) for name, shape in FFN_SHAPES}
            project_phase(nc, keep, rounded, x, (wq1, wq2, wk1, wk2), wv, (lq1, lk1, lq2, lk2),
                          ffn_w, (s1, s2, hs1, hs2, s3), qk_parts, values)
            maximum_phase(nc, keep, qk_parts, shift)
            attention_phase(nc, keep, qk_parts, shift, values, diffs)
            merge_phase(nc, keep, x, wo, diffs, mid, mid_t)
            ffn_split_phase(nc, keep, rounded, mid, mid_t, out)
        ffn_full_phase(nc, keep, ffn_w, mid, mid_t, out)


class Room:

    def __init__(self, nc, phase):
        self.nc, self.phase, self.ctx = nc, phase, ExitStack()

    def __enter__(self):
        return self

    def __exit__(self, *a):
        return self.ctx.__exit__(*a)

    def sb(self, name, shape, dt=F32):
        return self.ctx.enter_context(self.nc.sbuf_tensor(f"{self.phase}_{name}", shape, dt))

    def ps(self, name, shape):
        return self.ctx.enter_context(self.nc.psum_tensor(f"{self.phase}_{name}", shape, F32))

    def sem(self, name):
        return self.ctx.enter_context(self.nc.semaphore(f"{self.phase}_{name}"))

    def block(self):
        return self.ctx.enter_context(self.nc.Block())


def give_credits(nc, credits):
    with nc.Block() as block:
        @block.sync
        def _(sp):
            for sem, n in credits:
                sp.sem_inc(sem, n)


def project_phase(nc, keep, rounded, x, w_qk, wv, lam_in, ffn_w, ffn_s, qk_parts, values):
    w1, w2, h1, h2, w3 = ffn_w
    s1, s2, hs1, hs2, s3 = ffn_s
    M_TILES = len(KINDS) * EC
    x_v = x.rearrange("b (t s p) e -> (b t) p s e", s=SUBS, p=PARTS)
    with Room(nc, "proj") as room:
        wqk_sb = room.sb("wqk", [PARTS, len(KINDS), EC, EMBED])
        wv_sb = room.sb("wv", [PARTS, EC * HEADS, VALUE_DIM])
        wv_mean = room.sb("wv_mean", [PARTS, EC * HEADS])
        lam_sb = room.sb("lam", [PARTS, 4, HEADS * HEAD_DIM])
        lam_sum = room.sb("lam_sum", [PARTS, 2, HEADS])
        lam_exp = room.sb("lam_exp", [PARTS, 2, HEADS])
        x_sb = [room.sb(f"x{u}", [PARTS, SUBS, EMBED]) for u in range(2)]
        xt = [room.sb(f"xt{u}", [PARTS, EC, TILE]) for u in range(2)]
        parts = [room.sb(f"parts{n}", [PARTS, 3, TILE], BF16) for n in range(4)]
        resid = room.sb("resid", [PARTS, TILE])
        biggest = room.sb("biggest", [PARTS, len(KINDS), TILE], BF16)
        smallest = room.sb("smallest", [PARTS, len(KINDS), TILE], BF16)
        small_col = room.sb("small_col", [PARTS, len(KINDS)])
        big_col = room.sb("big_col", [PARTS, len(KINDS)])
        big_all = room.sb("big_all", [PARTS, len(KINDS)])
        v_sb = [room.sb(f"v{u}", [PARTS, HEADS, SUBS, VALUE_DIM]) for u in range(2)]
        w_rows = [room.sb(f"w_rows{u}", [PARTS, ROW_COLS]) for u in range(2)]
        w3_rows = room.sb("w3_rows", [PARTS, EC * HIDDEN])
        short = room.sb("short", [PARTS, ROW_COLS], F32R)
        differs = room.sb("differs", [PARTS, ROW_COLS], BF16)
        counts = room.sb("counts", [PARTS, TILES + 1])
        count_col = room.sb("count_col", [PARTS, 1])
        count_all = room.sb("count_all", [PARTS, 1])
        ident = keep["ident"]
        turn_ps = [room.ps(f"turn_ps{n}", [PARTS, 4, PARTS]) for n in range(2)]
        qk_ps = [room.ps(f"qk_ps{n}", [PARTS, TILE]) for n in range(4)]
        v_ps = [room.ps(f"v_ps{n}", [PARTS, HEADS, VALUE_DIM]) for n in range(2)]

        const_loaded = room.sem("const_loaded")
        wv_loaded = room.sem("wv_loaded")
        lam_loaded = room.sem("lam_loaded")
        w3_loaded = room.sem("w3_loaded")
        x_loaded = [room.sem(f"x_loaded{u}") for u in range(2)]
        w_loaded = [room.sem(f"w_loaded{u}") for u in range(2)]
        ident_done = room.sem("ident_done")
        prep_done = room.sem("prep_done")
        ones_done = room.sem("ones_done")
        lam_ready = room.sem("lam_ready")
        exp_done = room.sem("exp_done")
        turned = room.sem("turned")
        turn_bank_free = room.sem("turn_bank_free")
        xt_free = room.sem("xt_free")
        short_done = room.sem("short_done")
        compared = room.sem("compared")
        count_ready = room.sem("count_ready")
        count_reduced = room.sem("count_reduced")
        qk_projected = room.sem("qk_projected")
        qk_bank_free = room.sem("qk_bank_free")
        high_ready = room.sem("high_ready")
        mid_ready = room.sem("mid_ready")
        parts_ready = room.sem("parts_ready")
        parts_stored = [room.sem(f"parts_stored{n}") for n in range(4)]
        biggest_done = room.sem("biggest_done")
        v_projected = room.sem("v_projected")
        v_bank_free = room.sem("v_bank_free")
        v_stored = [room.sem(f"v_stored{u}") for u in range(2)]
        big_ready = room.sem("big_ready")
        big_reduced = room.sem("big_reduced")
        flag_steps = room.sem("flag_steps")

        G = EC + len(TURN_GROUPS)
        W0 = len(W3_GROUPS)
        give_credits(nc, [(turn_bank_free, 2), (xt_free, 2), (qk_bank_free, 4), (v_bank_free, 2)])
        block = room.block()

        @block.sync
        def _(sp):
            def load_x(t, u):
                sp.dma_start(x_sb[u][:, :, :], x_v[t]).then_inc(x_loaded[u], 16)

            def load_w(t, u):
                rows = bass.ts(t, PARTS)
                col = 0
                for w in (w1, w2, h1, h2):
                    n = w.shape[1]
                    sp.dma_start(w_rows[u][:, col:col + n], w[rows, :]).then_inc(w_loaded[u], 16)
                    col += n

            def tile(i, u, last):
                t = 2 * i + u
                for m in range(M_TILES):
                    kind, c = divmod(m, EC)
                    sp.wait_ge(parts_ready, M_TILES * t + m + 1)
                    sp.dma_start(qk_parts[kind, :, c * PARTS:(c + 1) * PARTS, bass.ts(t, TILE)].rearrange("a p n -> p a n"),
                                 parts[m % 4][:, :, :]).then_inc(parts_stored[m % 4], 16)
                sp.wait_ge(v_bank_free, 2 + SUBS * t + SUBS)
                sp.dma_start(values[:, :, bass.ts(t, SUBS), :].rearrange("h p s d -> p h (s d)"),
                             v_sb[u][:, :, :, :].rearrange("p h s d -> p h (s d)")).then_inc(v_stored[u], 16)
                if not last:
                    sp.wait_ge(turned, W0 + G * t + G)
                    load_x(t + 2, u)
                    sp.wait_ge(compared, t + 2)
                    load_w(t + 2, u)

            load_x(0, 0)
            load_x(1, 1)
            load_w(0, 0)
            load_w(1, 1)
            with sp.Fori(0, TILES // 2 - 1) as i:
                for u in range(2):
                    tile(i, u, False)
            for u in range(2):
                tile(TILES // 2 - 1, u, True)
            for u in range(2):
                sp.wait_ge(v_stored[u], 16 * (TILES // 2))
            for n in range(4):
                sp.wait_ge(parts_stored[n], 16 * (TILES * M_TILES // 4))

        @block.gpsimd
        def _(pool):
            pool.memset(ident[:, :], 0.0).then_inc(ident_done, 1)
            pool.wait_ge(ident_done, 1)
            pool.affine_select(out=ident[:, :], in_=ident[:, :], compare_op=ALU.not_equal, fill=1.0, base=0,
                               pattern=[[-1, PARTS]], channel_multiplier=1).then_inc(ident_done, 1)
            for u in range(2):
                pool.memset(v_sb[u][:, :, :, VALUE_DIM - 1:VALUE_DIM], 1.0).then_inc(ones_done, 1)
            pool.dma_start(keep["s3"][:, :], s3.partition_broadcast(PARTS)).then_inc(lam_loaded, 16)
            for n, v in enumerate(lam_in):
                pool.dma_start(lam_sb[:, n, :], v.rearrange("h d -> (h d)").partition_broadcast(PARTS)).then_inc(lam_loaded, 16)
            pool.wait_ge(big_ready, 1)
            pool.partition_all_reduce(big_all[:, :], big_col[:, :], PARTS, bass.bass_isa.ReduceOp.max).then_inc(big_reduced, 1)
            pool.wait_ge(count_ready, 1)
            pool.wait_ge(big_reduced, 1)
            pool.partition_all_reduce(count_all[:, :], count_col[:, :], PARTS, bass.bass_isa.ReduceOp.add).then_inc(count_reduced, 1)

        @block.scalar
        def _(act):
            act.dma_start(wv_sb[:, :, :].rearrange("p (c h) d -> p c (h d)", c=EC),
                          wv.rearrange("(c p) n -> p c n", p=PARTS)).then_inc(wv_loaded, 16)
            for n, w in enumerate(w_qk):
                act.dma_start(wqk_sb[:, n, :, :], w.rearrange("(c p) n -> p c n", p=PARTS)).then_inc(const_loaded, 16)
            with nc.allow_non_contiguous_dma(reason="small vectors of scales"):
                for name, s in (("s1", s1), ("s2", s2), ("hs1", hs1), ("hs2", hs2)):
                    act.dma_start(keep[name][:, :], s.rearrange("(c p) -> p c", p=PARTS)).then_inc(const_loaded, 16)
            act.dma_start(w3_rows[:, :].rearrange("p (o i) -> p o i", o=EC), w3.rearrange("(o p) i -> p o i", p=PARTS)).then_inc(w3_loaded, 16)
            act.wait_ge(lam_ready, 4)
            nc.scalar.activation(lam_exp[:, :, :], lam_sum[:, :, :], ACT.Exp).then_inc(exp_done, 1)
            for n, (o, c) in enumerate(W3_GROUPS):
                act.wait_ge(turned, n + 1)
                nc.scalar.copy(rounded["w3t"][:, c:c + 4, o * PARTS:(o + 1) * PARTS], turn_ps[n % 2][:, :, :]).then_inc(turn_bank_free, 1)
            act.wait_ge(ones_done, 2)
            with act.Fori(0, TILES // 2) as i:
                for u in range(2):
                    t = 2 * i + u
                    act.wait_ge(xt_free, t + 1)
                    for c in range(EC):
                        act.wait_ge(turned, W0 + G * t + c + 1)
                        nc.scalar.copy(xt[u][:, c, :], turn_ps[c % 2][:, :, :].rearrange("p s n -> p (s n)")).then_inc(turn_bank_free, 1)
                    for g, (_, name, c, n) in enumerate(TURN_GROUPS):
                        act.wait_ge(turned, W0 + G * t + EC + g + 1)
                        nc.scalar.copy(rounded[name][:, c:c + n, bass.ts(t, PARTS)], turn_ps[g % 2][:, 0:n, :]).then_inc(turn_bank_free, 1)
                    for m in range(M_TILES):
                        act.wait_ge(qk_projected, M_TILES * t + m + 1)
                        act.wait_ge(parts_stored[m % 4], 16 * (t * (M_TILES // 4) + m // 4))
                        nc.scalar.copy(parts[m % 4][:, 0, :], qk_ps[m % 4][:, :]).then_inc(high_ready, 1)
                    act.wait_ge(v_stored[u], 16 * i)
                    for s in range(SUBS):
                        act.wait_ge(v_projected, SUBS * t + s + 1)
                        nc.scalar.copy(v_sb[u][:, :, s, 0:VALUE_DIM - 1], v_ps[s % 2][:, :, 0:VALUE_DIM - 1]).then_inc(v_bank_free, 1)

        @block.vector
        def _(dve):
            dve.wait_ge(wv_loaded, 16)
            nc.vector.tensor_reduce(wv_mean[:, :], wv_sb[:, :, :], AXIS.X, ALU.add).then_inc(prep_done, 1)
            nc.vector.memset(biggest[:, :, :], 0.0).then_inc(biggest_done, 1)
            nc.vector.memset(smallest[:, :, :], 0.0).then_inc(biggest_done, 1)
            dve.wait_ge(prep_done, 1)
            nc.vector.scalar_tensor_tensor(wv_sb[:, :, :], wv_mean[:, :].unsqueeze(2).to_broadcast([PARTS, EC * HEADS, VALUE_DIM]),
                                           -1.0 / VALUE_DIM, wv_sb[:, :, :], ALU.mult, ALU.add).then_inc(prep_done, 1)
            dve.wait_ge(lam_loaded, 16 * 5)
            for n in range(2):
                nc.vector.tensor_tensor(lam_sb[:, 2 * n, :], lam_sb[:, 2 * n, :], lam_sb[:, 2 * n + 1, :], ALU.mult).then_inc(lam_ready, 1)
            dve.wait_ge(lam_ready, 2)
            for n in range(2):
                nc.vector.tensor_reduce(lam_sum[:, n, :], lam_sb[:, 2 * n, :].rearrange("p (h d) -> p h d", h=HEADS), AXIS.X, ALU.add).then_inc(lam_ready, 1)
            dve.wait_ge(exp_done, 1)
            nc.vector.scalar_tensor_tensor(keep["neg_lam"][:, :], lam_exp[:, 1, :], -LAM_INIT, lam_exp[:, 0, :], ALU.add, ALU.subtract)
            dve.wait_ge(w3_loaded, 16)
            nc.vector.tensor_copy(short[:, 0:EC * HIDDEN], w3_rows[:, :]).then_inc(short_done, 1)
            dve.wait_ge(short_done, 1)
            nc.vector.scalar_tensor_tensor(differs[:, 0:EC * HIDDEN], short[:, 0:EC * HIDDEN].bitcast(F32), 1.0, w3_rows[:, :], ALU.mult, ALU.not_equal,
                                           accum_out=counts[:, TILES:TILES + 1]).then_inc(compared, 1)
            with dve.Fori(0, TILES // 2) as i:
                for u in range(2):
                    t = 2 * i + u
                    for m in range(M_TILES):
                        if m == 2:
                            dve.wait_ge(w_loaded[u], 64 * i + 64)
                            dve.wait_ge(compared, t + 1)
                            nc.vector.tensor_copy(short[:, :], w_rows[u][:, :]).then_inc(short_done, 1)
                        if m == 4:
                            dve.wait_ge(short_done, t + 2)
                            nc.vector.scalar_tensor_tensor(differs[:, :], short[:, :].bitcast(F32), 1.0, w_rows[u][:, :], ALU.mult, ALU.not_equal,
                                                           accum_out=counts[:, bass.ts(t, 1)]).then_inc(compared, 1)
                        kind = m // EC
                        n = M_TILES * t + m
                        p = parts[m % 4]
                        dve.wait_ge(high_ready, n + 1)
                        dve.wait_ge(parts_ready, n)
                        nc.vector.tensor_tensor(resid[:, :], qk_ps[m % 4][:, :], p[:, 0, :], ALU.subtract).then_inc(qk_bank_free, 1)
                        dve.wait_ge(biggest_done, 2 * n + 2)
                        nc.vector.tensor_tensor(biggest[:, kind, :], biggest[:, kind, :], p[:, 0, :], ALU.max).then_inc(biggest_done, 1)
                        nc.vector.tensor_tensor(smallest[:, kind, :], smallest[:, kind, :], p[:, 0, :], ALU.min).then_inc(biggest_done, 1)
                        dve.wait_ge(qk_bank_free, 4 + n + 1)
                        nc.vector.tensor_copy(p[:, 1, :], resid[:, :]).then_inc(mid_ready, 1)
                        dve.wait_ge(mid_ready, n + 1)
                        nc.vector.tensor_tensor(p[:, 2, :], resid[:, :], p[:, 1, :], ALU.subtract).then_inc(parts_ready, 1)
            dve.wait_ge(compared, 1 + TILES)
            nc.vector.tensor_reduce(count_col[:, :], counts[:, :], AXIS.X, ALU.add).then_inc(count_ready, 1)
            dve.wait_ge(biggest_done, 2 + 2 * TILES * M_TILES)
            nc.vector.tensor_reduce(big_col[:, :], biggest[:, :, :], AXIS.X, ALU.max).then_inc(flag_steps, 1)
            nc.vector.tensor_reduce(small_col[:, :], smallest[:, :, :], AXIS.X, ALU.min).then_inc(flag_steps, 1)
            dve.wait_ge(flag_steps, 2)
            nc.vector.scalar_tensor_tensor(big_col[:, :], small_col[:, :], -1.0, big_col[:, :], ALU.mult, ALU.max).then_inc(big_ready, 1)
            dve.wait_ge(big_reduced, 1)
            bound = keep["bound"]
            nc.vector.tensor_tensor(bound[:, 0:2], big_all[:, 0:2], big_all[:, 2:4], ALU.mult).then_inc(flag_steps, 1)
            dve.wait_ge(flag_steps, 3)
            nc.vector.tensor_tensor(bound[:, 2:3], bound[:, 0:1], bound[:, 1:2], ALU.max).then_inc(flag_steps, 1)
            dve.wait_ge(flag_steps, 4)
            nc.vector.tensor_scalar(bound[:, 3:4], bound[:, 2:3], HEAD_DIM * BOUND_MARGIN, None, ALU.mult).then_inc(flag_steps, 1)
            dve.wait_ge(flag_steps, 5)
            nc.vector.tensor_scalar(keep["exact"][:, :], bound[:, 3:4], SAFE_BOUND / SCALE, None, ALU.is_gt).then_inc(flag_steps, 1)
            dve.wait_ge(count_reduced, 1)
            nc.vector.tensor_scalar(keep["wide"][:, :], count_all[:, :], 0.0, None, ALU.is_gt).then_inc(flag_steps, 1)
            dve.wait_ge(flag_steps, 7)

        @block.tensor
        def _(pe):
            pe.wait_ge(ident_done, 2)
            pe.wait_ge(w3_loaded, 16)
            for n, (o, c) in enumerate(W3_GROUPS):
                pe.wait_ge(turn_bank_free, n + 1)
                for k in range(4):
                    col = o * HIDDEN + (c + k) * PARTS
                    last = nc.tensor.transpose(turn_ps[n % 2][:, k, :], w3_rows[:, col:col + PARTS], ident[:, :])
                last.then_inc(turned, 1)
            pe.wait_ge(const_loaded, 16 * 8)
            pe.wait_ge(prep_done, 2)
            with pe.Fori(0, TILES // 2) as i:
                for u in range(2):
                    t = 2 * i + u
                    pe.wait_ge(x_loaded[u], 16 * i + 16)
                    for c in range(EC):
                        pe.wait_ge(turn_bank_free, W0 + G * t + c + 1)
                        for s in range(SUBS):
                            last = nc.tensor.transpose(turn_ps[c % 2][:, s, :], x_sb[u][:, s, c * PARTS:(c + 1) * PARTS], ident[:, :])
                        last.then_inc(turned, 1)
                    pe.wait_ge(w_loaded[u], 64 * i + 64)
                    for g, (col, _, _, n) in enumerate(TURN_GROUPS):
                        pe.wait_ge(turn_bank_free, W0 + G * t + EC + g + 1)
                        for k in range(n):
                            last = nc.tensor.transpose(turn_ps[g % 2][:, k, :], w_rows[u][:, col + k * PARTS:col + (k + 1) * PARTS], ident[:, :])
                        last.then_inc(turned, 1)
                    pe.wait_ge(turn_bank_free, 2 + W0 + G * t + EC)
                    for m in range(M_TILES):
                        kind, o = divmod(m, EC)
                        pe.wait_ge(qk_bank_free, M_TILES * t + m + 1)
                        for c in range(EC):
                            last = nc.tensor.matmul(qk_ps[m % 4][:, :], wqk_sb[:, kind, c, o * PARTS:(o + 1) * PARTS], xt[u][:, c, :],
                                                    start=(c == 0), stop=(c == EC - 1))
                        last.then_inc(qk_projected, 1)
                    for s in range(SUBS):
                        pe.wait_ge(v_bank_free, SUBS * t + s + 1)
                        for c in range(EC):
                            last = nc.tensor.matmul(v_ps[s % 2][:, :, :], xt[u][:, c, s * PARTS:(s + 1) * PARTS],
                                                    wv_sb[:, c * HEADS:(c + 1) * HEADS, :], start=(c == 0), stop=(c == EC - 1))
                        last.then_inc(v_projected, 1)
                    pe.wait_ge(v_projected, SUBS * t + SUBS)
                    pe.sem_inc(xt_free, 1)


def load_stack(dma, stack, qk_parts, sem, kind, which, head, b):
    for n, pair in enumerate(PART_PAIRS):
        dma(stack[n * HEAD_DIM:(n + 1) * HEAD_DIM, :],
            qk_parts[kind, pair[which], bass.ts(head, HEAD_DIM), b * SEQ:(b + 1) * SEQ]).then_inc(sem, 16)


STACK_DMAS = 4 * len(PART_PAIRS)


def maximum_phase(nc, keep, qk_parts, shift):
    CHUNKS = [(qb, s, c) for qb in range(KEY_BLOCKS) for s in range(2) for c in range(qb // SUBS + 1)]
    NCH = len(CHUNKS)
    BANKS = 4
    with Room(nc, "max") as room:
        q_sb = [room.sb(f"q{u}", [SCORE_ROWS, 2, SEQ], BF16) for u in range(2)]
        k_sb = [room.sb(f"k{u}", [SCORE_ROWS, 2, SEQ], BF16) for u in range(2)]
        future = room.sb("future", [PARTS, PARTS], BF16)
        ident_b = room.sb("ident_b", [PARTS, PARTS], BF16)
        chunk_max = room.sb("chunk_max", [PARTS, 2, KEY_BLOCKS, QUERY_TILES])
        row_max = room.sb("row_max", [PARTS, 2 * KEY_BLOCKS])
        neg = room.sb("neg", [2 * KEY_BLOCKS, PARTS])
        rest = room.sb("rest", [2 * KEY_BLOCKS, PARTS])
        neg_parts = room.sb("neg_parts", [2 * KEY_BLOCKS, 3, PARTS], BF16)
        fill = room.sb("fill", [PARTS, 2, HEADS * BATCH * 2 * SEQ // PARTS], BF16)
        s_ps = [room.ps(f"s_ps{n}", [PARTS, TILE]) for n in range(BANKS)]
        t_ps = room.ps("t_ps", [2 * KEY_BLOCKS, PARTS])

        const_done = room.sem("const_done")
        loaded = [room.sem(f"loaded{u}") for u in range(2)]
        scored = room.sem("scored")
        bank_free = room.sem("bank_free")
        reduced = room.sem("reduced")
        row_ready = room.sem("row_ready")
        transposed = room.sem("transposed")
        cut = room.sem("cut")
        stored = room.sem("stored")
        filled = room.sem("filled")
        fill_ready = room.sem("fill_ready")
        CUTS = 4

        give_credits(nc, [(bank_free, BANKS)])
        block = room.block()

        @block.gpsimd
        def _(pool):
            exact = pool.value_load(keep["exact"][0:1, 0:1])
            with pool.If(exact != 0):
                pool.memset(future[:, :], 0.0).then_inc(const_done, 1)
                pool.memset(ident_b[:, :], 0.0).then_inc(const_done, 1)
                pool.wait_ge(const_done, 2)
                pool.affine_select(out=future[:, :], in_=future[:, :], compare_op=ALU.is_ge, fill=LOWEST, base=0,
                                   pattern=[[-1, PARTS]], channel_multiplier=1).then_inc(const_done, 1)
                pool.affine_select(out=ident_b[:, :], in_=ident_b[:, :], compare_op=ALU.not_equal, fill=1.0, base=0,
                                   pattern=[[-1, PARTS]], channel_multiplier=1).then_inc(const_done, 1)

        @block.sync
        def _(sp):
            exact = sp.value_load(keep["exact"][0:1, 0:1])
            flat = shift.rearrange("a h b s (r n) -> a (h b s r) n", n=PARTS)
            with sp.If(exact != 0):
                with sp.Fori(0, HEADS) as h:
                    for b in range(BATCH):
                        sp.wait_ge(scored, (h * BATCH) * NCH)
                        for kind, (buf, s) in enumerate([(q_sb, 0), (q_sb, 1), (k_sb, 0), (k_sb, 1)]):
                            load_stack(sp.dma_start, buf[b][:, s, :], qk_parts, loaded[b], kind, kind // 2, h, b)
                    for b in range(BATCH):
                        n = h * BATCH + b
                        sp.wait_ge(cut, CUTS * n + CUTS)
                        sp.dma_start(flat[:, bass.ts(n, 2 * KEY_BLOCKS), :].rearrange("a r n -> r a n"), neg_parts[:, :, :]).then_inc(stored, 16)
                sp.wait_ge(stored, 16 * HEADS * BATCH)
            with sp.If(exact == 0):
                sp.wait_ge(fill_ready, 2)
                for a in range(SHIFT_ROWS):
                    sp.dma_start(shift[a].rearrange("h b s n -> (h b s n)").rearrange("(p n) -> p n", p=PARTS),
                                 fill[:, min(a, 1), :]).then_inc(filled, 16)
                sp.wait_ge(filled, 16 * SHIFT_ROWS)

        @block.tensor
        def _(pe):
            exact = pe.value_load(keep["exact"][0:1, 0:1])
            with pe.If(exact != 0):
                pe.wait_ge(const_done, 4)
                with pe.Fori(0, HEADS) as h:
                    for b in range(BATCH):
                        n = h * BATCH + b
                        pe.wait_ge(loaded[b], 16 * STACK_DMAS * h + 16 * STACK_DMAS)
                        for m, (qb, s, c) in enumerate(CHUNKS):
                            cols = min(TILE, (qb + 1) * PARTS - c * TILE)
                            bank = s_ps[m % BANKS]
                            on_diagonal = c == qb // SUBS
                            pe.wait_ge(bank_free, n * NCH + m + 1)
                            last = nc.tensor.matmul(bank[:, 0:cols], q_sb[b][:, s, qb * PARTS:(qb + 1) * PARTS],
                                                    k_sb[b][:, s, c * TILE:c * TILE + cols], start=True, stop=not on_diagonal)
                            if on_diagonal:
                                last = nc.tensor.matmul(bank[:, cols - PARTS:cols], ident_b[:, :], future[:, :], start=False, stop=True)
                            last.then_inc(scored, 1)
                        pe.wait_ge(row_ready, n + 1)
                        pe.wait_ge(cut, CUTS * n)
                        nc.tensor.transpose(t_ps[:, :], row_max[:, :], keep["ident"][:, :]).then_inc(transposed, 1)

        @block.vector
        def _(dve):
            exact = dve.value_load(keep["exact"][0:1, 0:1])
            with dve.If(exact != 0):
                nc.vector.memset(chunk_max[:, :, :, :], LOWEST).then_inc(reduced, 1)
                dve.wait_ge(reduced, 1)
                with dve.Fori(0, HEADS) as h:
                    for b in range(BATCH):
                        n = h * BATCH + b
                        for m, (qb, s, c) in enumerate(CHUNKS):
                            cols = min(TILE, (qb + 1) * PARTS - c * TILE)
                            dve.wait_ge(scored, n * NCH + m + 1)
                            nc.vector.tensor_reduce(chunk_max[:, s, qb, c:c + 1], s_ps[m % BANKS][:, 0:cols], AXIS.X, ALU.max).then_inc(bank_free, 1)
                        dve.wait_ge(bank_free, BANKS + n * NCH + NCH)
                        dve.wait_ge(transposed, n)
                        nc.vector.tensor_reduce(row_max[:, :].rearrange("p (s q) -> p s q", s=2), chunk_max[:, :, :, :], AXIS.X, ALU.max).then_inc(row_ready, 1)
                        dve.wait_ge(transposed, n + 1)
                        dve.wait_ge(stored, 16 * n)
                        nc.vector.tensor_scalar(neg[:, :], t_ps[:, :], -1.0, None, ALU.mult).then_inc(cut, 1)
                        dve.wait_ge(cut, CUTS * n + 1)
                        nc.vector.tensor_copy(neg_parts[:, 0, :], neg[:, :]).then_inc(cut, 1)
                        dve.wait_ge(cut, CUTS * n + 2)
                        nc.vector.tensor_tensor(rest[:, :], neg[:, :], neg_parts[:, 0, :], ALU.subtract).then_inc(reduced, 1)
                        dve.wait_ge(reduced, 1 + n + 1)
                        nc.vector.tensor_copy(neg_parts[:, 1, :], rest[:, :]).then_inc(cut, 1)
                        dve.wait_ge(cut, CUTS * n + 3)
                        nc.vector.tensor_tensor(neg_parts[:, 2, :], rest[:, :], neg_parts[:, 1, :], ALU.subtract).then_inc(cut, 1)
            with dve.If(exact == 0):
                nc.vector.memset(fill[:, :, :], 0.0).then_inc(fill_ready, 1)
                dve.wait_ge(fill_ready, 1)
                nc.vector.tensor_scalar(fill[:, 0, :], fill[:, 1, :], keep["bound"][:, 3:4], -1.0, ALU.add, ALU.mult).then_inc(fill_ready, 1)


def attention_phase(nc, keep, qk_parts, shift, values, diffs):
    PAIRS = [(t, p) for t in range(QUERY_TILES) for p in range(SUBS * (t + 1) // 2)]
    NP = len(PAIRS)
    STEPS = [(b, t, p) for b in range(BATCH) for t, p in PAIRS]
    NS = len(STEPS)
    NT = BATCH * QUERY_TILES
    LOADS = STACK_DMAS + 2 + 1
    SLOTS = 3
    PROBS = 4
    D = VALUE_DIM
    VEC = 6

    def window(t, j):
        return max(0, j - SUBS * t) * PARTS

    def is_last(t, p):
        return p == SUBS * (t + 1) // 2 - 1

    with Room(nc, "attn") as room:
        q_sb = [room.sb(f"q{b}", [STACK_ROWS, 2, SEQ], BF16) for b in range(BATCH)]
        k_sb = [room.sb(f"k{b}", [STACK_ROWS, 2, SEQ], BF16) for b in range(BATCH)]
        v_sb = [room.sb(f"v{b}", [PARTS, KEY_BLOCKS, D]) for b in range(BATCH)]
        probs = [room.sb(f"probs{n}", [PARTS, 2, 2, TILE]) for n in range(PROBS)]
        zeros = room.sb("zeros", [PARTS, D])
        sums_sb = room.sb("sums_sb", [PARTS, TILE])
        raw_sb = [room.sb(f"raw{b}", [PARTS, KEY_BLOCKS, 2, D]) for b in range(BATCH)]
        recip = room.sb("recip", [PARTS, KEY_BLOCKS, 2])
        first = room.sb("first", [PARTS, KEY_BLOCKS, D - 1])
        second = room.sb("second", [PARTS, KEY_BLOCKS, D - 1])
        total = room.sb("total", [PARTS, KEY_BLOCKS])
        diff = [room.sb(f"diff{b}", [PARTS, KEY_BLOCKS, D]) for b in range(BATCH)]
        s_ps = [room.ps(f"s_ps{n}", [PARTS, 2, TILE]) for n in range(SLOTS)]
        sums_ps = [room.ps(f"sums_ps{n}", [PARTS, TILE]) for n in range(2)]

        const_done = room.sem("const_done")
        loaded = [room.sem(f"loaded{b}") for b in range(BATCH)]
        scored = room.sem("scored")
        exp_done = room.sem("exp_done")
        mask_begun = room.sem("mask_begun")
        masked = room.sem("masked")
        probs_free = room.sem("probs_free")
        sums_copied = room.sem("sums_copied")
        turned = room.sem("turned")
        evens_done = room.sem("evens_done")
        sums_bank_free = room.sem("sums_bank_free")
        vec = room.sem("vec")
        diff_ready = room.sem("diff_ready")
        stored = [room.sem(f"stored{b}") for b in range(BATCH)]

        CONSTS = BATCH + 1
        give_credits(nc, [(probs_free, PROBS), (sums_bank_free, 2)])
        block = room.block()

        @block.sync
        def _(sp):
            def load(h, b):
                for kind, (buf, s) in enumerate([(q_sb, 0), (q_sb, 1), (k_sb, 0), (k_sb, 1)]):
                    load_stack(sp.dma_start, buf[b][0:SCORE_ROWS, s, :], qk_parts, loaded[b], kind, kind // 2, h, b)
                for s in range(2):
                    sp.dma_start(q_sb[b][SCORE_ROWS:STACK_ROWS, s, :], shift[:, h, b, s, :]).then_inc(loaded[b], 16)
                sp.dma_start(v_sb[b][:, :, :], values[h, :, b * KEY_BLOCKS:(b + 1) * KEY_BLOCKS, :]).then_inc(loaded[b], 16)

            def store(h, b):
                sp.wait_ge(diff_ready, BATCH * h + b + 1)
                sp.dma_start(diffs[b * KEY_BLOCKS:(b + 1) * KEY_BLOCKS, :, h, :].rearrange("k p n -> p k n"), diff[b][:, :, :]).then_inc(stored[b], 16)

            for b in range(BATCH):
                load(0, b)
            with sp.Fori(0, HEADS - 1) as h:
                for b in range(BATCH):
                    sp.wait_ge(probs_free, PROBS + NS * h + NP * (b + 1))
                    load(h + 1, b)
                    store(h, b)
            for b in range(BATCH):
                store(HEADS - 1, b)
            for b in range(BATCH):
                sp.wait_ge(stored[b], 16 * HEADS)

        @block.gpsimd
        def _(pool):
            for b in range(BATCH):
                pool.memset(k_sb[b][SCORE_ROWS:STACK_ROWS, :, :], 1.0).then_inc(const_done, 1)
                pool.wait_ge(const_done, b + 1)
            pool.memset(zeros[:, :], 0.0).then_inc(const_done, 1)
            with pool.Fori(0, HEADS) as h:
                for k, (b, t, p) in enumerate(STEPS):
                    for par in range(2):
                        j = 2 * p + par
                        if j < SUBS * t:
                            continue
                        off = window(t, j)
                        pool.wait_ge(exp_done, 2 * NS * h + 2 * k + par + 1)
                        pool.sem_inc(mask_begun, 1)
                        corner = probs[k % PROBS][:, par, :, off:off + PARTS]
                        pool.affine_select(out=corner, in_=corner, compare_op=ALU.is_ge, fill=0.0, base=0,
                                           pattern=[[0, 2], [1, PARTS]], channel_multiplier=-1).then_inc(masked, 1)

        @block.scalar
        def _(act):
            with act.Fori(0, HEADS) as h:
                for k, (b, t, p) in enumerate(STEPS):
                    act.wait_ge(probs_free, NS * h + k + 1)
                    for par in range(2):
                        off = window(t, 2 * p + par)
                        act.wait_ge(scored, 2 * NS * h + 2 * k + par + 1)
                        nc.scalar.activation(probs[k % PROBS][:, par, :, off:TILE], s_ps[(2 * k + par) % SLOTS][:, :, off:TILE],
                                             ACT.Exp, scale=SCALE).then_inc(exp_done, 1)

        @block.tensor
        def _(pe):
            pe.wait_ge(const_done, CONSTS)

            def scores(h, g, exps):
                b, t, p = STEPS[g // 2]
                j = 2 * p + g % 2
                off = window(t, j)
                if g % (2 * NP) == 0:
                    pe.wait_ge(loaded[b], 16 * LOADS * h + 16 * LOADS)
                if exps is not None:
                    pe.wait_ge(exp_done, exps)
                for s in range(2):
                    last = nc.tensor.matmul(s_ps[g % SLOTS][:, s, off:TILE], k_sb[b][:, s, j * PARTS:(j + 1) * PARTS],
                                            q_sb[b][:, s, t * TILE + off:(t + 1) * TILE], start=True, stop=True)
                last.then_inc(scored, 1)

            def weigh(h, k):
                b, t, p = STEPS[k]
                T = b * QUERY_TILES + t
                sums = sums_ps[T % 2]
                pe.wait_ge(exp_done, 2 * NS * h + 2 * k + 2)
                if 2 * p + 2 > SUBS * t:
                    pe.wait_ge(masked, SUBS * NT * h + SUBS * T + 2 * p + 2 - SUBS * t)
                if p == 0:
                    pe.wait_ge(sums_bank_free, NT * h + T + 1)
                if p == 0 and t == 0:
                    for s in range(2):
                        nc.tensor.matmul(sums[(2 + s) * D:(3 + s) * D, :], zeros[:, :], probs[k % PROBS][:, 0, s, :], start=True, stop=False)
                for par in range(2):
                    j = 2 * p + par
                    off = window(t, j)
                    for s in range(2):
                        c = 2 * par + s
                        last = nc.tensor.matmul(sums[c * D:(c + 1) * D, off:TILE], v_sb[b][:, j, :], probs[k % PROBS][:, par, s, off:TILE],
                                                start=(p == 0 and not (t == 0 and par == 1)), stop=is_last(t, p))
                last.then_inc(probs_free, 1)

            def turn(h, T):
                pe.wait_ge(sums_copied, NT * h + T + 1)
                for i in range(SUBS):
                    last = nc.tensor.transpose(sums_ps[T % 2][:, i * PARTS:(i + 1) * PARTS], sums_sb[:, i * PARTS:(i + 1) * PARTS], keep["ident"][:, :])
                last.then_inc(turned, 1)

            def round_of(h, final):
                ended = None
                for k in range(1, NS + 2):
                    e0 = 2 * NS * h
                    for half in range(2):
                        g = 2 * k + half
                        if SLOTS <= g < 2 * NS:
                            scores(h, g, e0 + g - SLOTS + 1)
                        if not final and k >= NS and half == 0:
                            scores(h + 1, k - NS, e0 + 2 * NS - 1 + k - NS)
                        if half == 0 and k >= 2:
                            weigh(h, k - 2)
                            if ended is not None:
                                turn(h, ended)
                            b, t, p = STEPS[k - 2]
                            ended = b * QUERY_TILES + t if is_last(t, p) else None
                if not final:
                    scores(h + 1, 2, None)
                turn(h, ended)

            for g in range(SLOTS):
                scores(0, g, None)
            with pe.Fori(0, HEADS - 1) as h:
                round_of(h, False)
            round_of(HEADS - 1, True)

        @block.vector
        def _(dve):
            def subtract(h, b):
                v0 = VEC * (BATCH * h + b)
                r = raw_sb[b]
                dve.wait_ge(sums_bank_free, 2 + NT * h + QUERY_TILES * (b + 1))
                nc.vector.reciprocal(recip[:, :, :], r[:, :, :, D - 1]).then_inc(vec, 1)
                dve.wait_ge(stored[b], 16 * h)
                dve.wait_ge(vec, v0 + 1)
                nc.vector.tensor_tensor(first[:, :, :], r[:, :, 0, 0:D - 1], recip[:, :, 0:1].to_broadcast([PARTS, KEY_BLOCKS, D - 1]), ALU.mult).then_inc(vec, 1)
                nc.vector.tensor_tensor(second[:, :, :], r[:, :, 1, 0:D - 1], recip[:, :, 1:2].to_broadcast([PARTS, KEY_BLOCKS, D - 1]), ALU.mult).then_inc(vec, 1)
                dve.wait_ge(vec, v0 + 3)
                nc.vector.scalar_tensor_tensor(diff[b][:, :, 0:D - 1], second[:, :, :], keep["neg_lam"][:, bass.ts(h, 1)], first[:, :, :], ALU.mult, ALU.add).then_inc(vec, 1)
                dve.wait_ge(vec, v0 + 4)
                nc.vector.tensor_reduce(total[:, :], diff[b][:, :, 0:D - 1], AXIS.X, ALU.add).then_inc(vec, 1)
                dve.wait_ge(vec, v0 + 5)
                nc.vector.tensor_scalar(diff[b][:, :, D - 1], total[:, :], -1.0, None, ALU.mult).then_inc(vec, 1)
                dve.wait_ge(vec, v0 + 6)
                dve.sem_inc(diff_ready, 1)

            with dve.Fori(0, HEADS) as h:
                for k, (b, t, p) in enumerate(STEPS):
                    if not is_last(t, p):
                        continue
                    T = b * QUERY_TILES + t
                    dve.wait_ge(probs_free, PROBS + NS * h + k + 1)
                    dve.wait_ge(turned, NT * h + T)
                    nc.vector.tensor_copy(sums_sb[:, :], sums_ps[T % 2][:, :]).then_inc(sums_copied, 1)
                    dve.wait_ge(turned, NT * h + T + 1)
                    tile = raw_sb[b][:, SUBS * t:SUBS * (t + 1), :, :].rearrange("p i s d -> p i (s d)")
                    both = sums_ps[T % 2][:, :].rearrange("p (i r d) -> p i r d", i=SUBS, r=2)
                    nc.vector.tensor_copy(tile, both[:, :, 0, :]).then_inc(evens_done, 1)
                    dve.wait_ge(evens_done, NT * h + T + 1)
                    nc.vector.tensor_tensor(tile, both[:, :, 1, :], tile, ALU.add).then_inc(sums_bank_free, 1)
                    if T == QUERY_TILES + 1:
                        subtract(h, 0)
                subtract(h, 1)


def merge_phase(nc, keep, x, wo, diffs, mid, mid_t):
    x_v = x.rearrange("b (t s p) e -> (b t) p s e", s=SUBS, p=PARTS)
    d_v = diffs.rearrange("(t s) p h d -> t p s (h d)", s=SUBS)
    mid_v = mid.rearrange("(t s) p e -> t p s e", s=SUBS)
    D = VALUE_DIM
    N = SUBS * HEADS
    HALF = SUBS // 2
    with Room(nc, "merge") as room:
        wo_sb = room.sb("wo", [PARTS, VC, EMBED])
        d_sb = [room.sb(f"d{u}", [PARTS, SUBS, HEADS * D]) for u in range(2)]
        x_sb = [room.sb(f"x{u}", [PARTS, SUBS, EMBED]) for u in range(2)]
        square = room.sb("square", [PARTS, N, D])
        var = room.sb("var", [PARTS, N])
        root = room.sb("root", [PARTS, N])
        quotient = room.sb("quotient", [PARTS, N])
        rstd = room.sb("rstd", [PARTS, N])
        normed = room.sb("normed", [PARTS, N, D])
        normed_t = [room.sb(f"normed_t{n}", [PARTS, VC, PARTS]) for n in range(2)]
        y = room.sb("y", [PARTS, SUBS, EMBED])
        stats = room.sb("stats", [PARTS, SUBS, 6])
        mean_var = room.sb("mean_var", [PARTS, SUBS, 2])
        y_var = room.sb("y_var", [PARTS, SUBS])
        y_root = room.sb("y_root", [PARTS, SUBS])
        y_quotient = room.sb("y_quotient", [PARTS, SUBS])
        y_rstd = room.sb("y_rstd", [PARTS, SUBS])
        out_sb = [room.sb(f"out{u}", [PARTS, SUBS, EMBED]) for u in range(2)]
        out_t = [room.sb(f"out_t{u}", [PARTS, EC, TILE]) for u in range(2)]
        nt_ps = [room.ps(f"nt_ps{n}", [PARTS, VC, PARTS]) for n in range(2)]
        y_ps = [[room.ps(f"y_ps{u}{n}", [PARTS, HALF, EMBED]) for n in range(2)] for u in range(2)]
        ot_ps = [room.ps(f"ot_ps{c}", [PARTS, TILE]) for c in range(EC)]

        wo_loaded = room.sem("wo_loaded")
        loaded = [room.sem(f"loaded{u}") for u in range(2)]
        squared = room.sem("squared")
        vec = room.sem("vec")
        var_ready = room.sem("var_ready")
        root_ready = room.sem("root_ready")
        normed_ready = room.sem("normed_ready")
        normed_turned = room.sem("normed_turned")
        nt_bank_free = room.sem("nt_bank_free")
        projected = room.sem("projected")
        y_done = room.sem("y_done")
        y_vec = room.sem("y_vec")
        aggr_begun = room.sem("aggr_begun")
        y_var_ready = room.sem("y_var_ready")
        y_root_ready = room.sem("y_root_ready")
        out_ready = room.sem("out_ready")
        out_turned = room.sem("out_turned")
        ot_copied = room.sem("ot_copied")
        stored = [room.sem(f"stored{u}") for u in range(2)]
        stored_t = [room.sem(f"stored_t{u}") for u in range(2)]
        VEC, Y_VEC = 5, 2 * SUBS + 5
        give_credits(nc, [(nt_bank_free, 2)])
        block = room.block()
        ROUNDS = TILES // 2

        def staggered(eng, first_half, second_half):
            first_half(0, 0, 0)
            with eng.Fori(0, ROUNDS - 1) as i:
                for u in range(2):
                    first_half(2 * i + u + 1, 1 - u, i + u)
                    second_half(2 * i + u, u, i)
            i = ROUNDS - 1
            first_half(2 * i + 1, 1, i)
            second_half(2 * i, 0, i)
            second_half(2 * i + 1, 1, i)

        @block.sync
        def _(sp):
            def load(t, u):
                sp.dma_start(d_sb[u][:, :, :], d_v[t]).then_inc(loaded[u], 16)
                sp.dma_start(x_sb[u][:, :, :], x_v[t]).then_inc(loaded[u], 16)

            def tile(i, u, last):
                t = 2 * i + u
                if not last:
                    sp.wait_ge(normed_ready, t + 1)
                    sp.wait_ge(y_done, 2 * t + 2)
                    load(t + 2, u)
                sp.wait_ge(out_ready, SUBS * t + SUBS)
                sp.dma_start(mid_v[t], out_sb[u][:, :, :]).then_inc(stored[u], 16)
                sp.wait_ge(ot_copied, EC * t + EC)
                sp.dma_start(mid_t[:, :, bass.ts(t, TILE)].rearrange("c p n -> p c n"), out_t[u][:, :, :]).then_inc(stored_t[u], 16)

            sp.dma_start(wo_sb[:, :, :], wo.rearrange("(c p) n -> p c n", p=PARTS)).then_inc(wo_loaded, 16)
            for u in range(2):
                load(u, u)
            with sp.Fori(0, ROUNDS - 1) as i:
                for u in range(2):
                    tile(i, u, False)
            for u in range(2):
                tile(ROUNDS - 1, u, True)
            for u in range(2):
                sp.wait_ge(stored[u], 16 * ROUNDS)
                sp.wait_ge(stored_t[u], 16 * ROUNDS)

        @block.scalar
        def _(act):
            def first_half(t, u, i):
                act.wait_ge(loaded[u], 32 * i + 32)
                act.wait_ge(var_ready, t)
                nc.scalar.activation(square[:, :, :].rearrange("p n d -> p (n d)"), d_sb[u][:, :, :].rearrange("p s n -> p (s n)"), ACT.Square).then_inc(squared, 1)
                act.wait_ge(var_ready, t + 1)
                nc.scalar.activation(root[:, :], var[:, :], ACT.Sqrt).then_inc(root_ready, 1)
                for s in range(SUBS):
                    act.wait_ge(normed_turned, SUBS * t + s + 1)
                    if s >= 2:
                        act.wait_ge(projected, SUBS * t + s - 1)
                    nc.scalar.copy(normed_t[s % 2][:, :, :], nt_ps[s % 2][:, :, :]).then_inc(nt_bank_free, 1)

            def second_half(t, u, i):
                act.wait_ge(y_var_ready, t + 1)
                nc.scalar.activation(y_root[:, :], y_var[:, :], ACT.Sqrt).then_inc(y_root_ready, 1)
                act.wait_ge(stored_t[u], 16 * i)
                for c in range(EC):
                    act.wait_ge(out_turned, EC * t + c + 1)
                    nc.scalar.copy(out_t[u][:, c, :], ot_ps[c][:, :]).then_inc(ot_copied, 1)

            staggered(act, first_half, second_half)

        @block.vector
        def _(dve):
            def first_half(t, u, i):
                v0 = VEC * t
                dve.wait_ge(squared, t + 1)
                nc.vector.tensor_reduce(var[:, :], square[:, :, :], AXIS.X, ALU.add).then_inc(vec, 1)
                dve.wait_ge(vec, v0 + 1)
                nc.vector.tensor_scalar(var[:, :], var[:, :], 1.0 / D, LN_EPS, ALU.mult, ALU.add).then_inc(var_ready, 1)
                dve.wait_ge(root_ready, t + 1)
                nc.vector.reciprocal(quotient[:, :], root[:, :]).then_inc(vec, 1)
                dve.wait_ge(vec, v0 + 2)
                nc.vector.tensor_tensor(quotient[:, :], quotient[:, :], var[:, :], ALU.mult).then_inc(vec, 1)
                dve.wait_ge(vec, v0 + 3)
                nc.vector.tensor_tensor(quotient[:, :], quotient[:, :], root[:, :], ALU.add).then_inc(vec, 1)
                dve.wait_ge(vec, v0 + 4)
                nc.vector.reciprocal(rstd[:, :], quotient[:, :]).then_inc(vec, 1)
                dve.wait_ge(vec, v0 + 5)
                dve.wait_ge(normed_turned, SUBS * t)
                nc.vector.scalar_tensor_tensor(normed[:, :, :], d_sb[u][:, :, :].rearrange("p s (h d) -> p (s h) d", d=D), 2.0 * (1.0 - LAM_INIT),
                                               rstd[:, :].unsqueeze(2).to_broadcast([PARTS, N, D]), ALU.mult, ALU.mult).then_inc(normed_ready, 1)

            def second_half(t, u, i):
                v0 = Y_VEC * t
                dve.wait_ge(out_ready, SUBS * t)
                for n in range(2):
                    dve.wait_ge(projected, SUBS * t + HALF * (n + 1))
                    nc.vector.tensor_tensor(y[:, HALF * n:HALF * (n + 1), :], y_ps[u][n][:, :, :], x_sb[u][:, HALF * n:HALF * (n + 1), :], ALU.add).then_inc(y_done, 1)
                for s in range(SUBS):
                    if s % HALF == 0:
                        dve.wait_ge(y_done, 2 * t + s // HALF + 1)
                    nc.vector.bn_stats(stats[:, s, :], y[:, s, :]).then_inc(y_vec, 1)
                dve.wait_ge(y_vec, v0 + SUBS)
                dve.sem_inc(aggr_begun, 1)
                for s in range(SUBS):
                    nc.vector.bn_aggr(mean_var[:, s, :], stats[:, s, :]).then_inc(y_vec, 1)
                dve.wait_ge(y_vec, v0 + 2 * SUBS)
                nc.vector.tensor_scalar(y_var[:, :], mean_var[:, :, 1], LN_EPS, None, ALU.add).then_inc(y_var_ready, 1)
                dve.wait_ge(y_root_ready, t + 1)
                v1 = v0 + 2 * SUBS
                nc.vector.reciprocal(y_quotient[:, :], y_root[:, :]).then_inc(y_vec, 1)
                dve.wait_ge(y_vec, v1 + 1)
                nc.vector.tensor_tensor(y_quotient[:, :], y_quotient[:, :], y_var[:, :], ALU.mult).then_inc(y_vec, 1)
                dve.wait_ge(y_vec, v1 + 2)
                nc.vector.tensor_tensor(y_quotient[:, :], y_quotient[:, :], y_root[:, :], ALU.add).then_inc(y_vec, 1)
                dve.wait_ge(y_vec, v1 + 3)
                nc.vector.tensor_scalar(y_quotient[:, :], y_quotient[:, :], 0.5, None, ALU.mult).then_inc(y_vec, 1)
                dve.wait_ge(y_vec, v1 + 4)
                nc.vector.reciprocal(y_rstd[:, :], y_quotient[:, :]).then_inc(y_vec, 1)
                dve.wait_ge(y_vec, v1 + 5)
                dve.wait_ge(stored[u], 16 * i)
                dve.wait_ge(out_turned, EC * t)
                for s in range(SUBS):
                    nc.vector.tensor_scalar(out_sb[u][:, s, :], y[:, s, :], mean_var[:, s, 0:1], y_rstd[:, s:s + 1], ALU.subtract, ALU.mult).then_inc(out_ready, 1)

            staggered(dve, first_half, second_half)

        @block.tensor
        def _(pe):
            ident = keep["ident"]
            pe.wait_ge(wo_loaded, 16)

            def first_half(t, u, i):
                pe.wait_ge(normed_ready, t + 1)
                pe.wait_ge(y_done, 2 * 2 * i)
                flat = normed[:, :, :].rearrange("p n d -> p (n d)")
                for s in range(SUBS + 1):
                    if s < SUBS:
                        pe.wait_ge(nt_bank_free, SUBS * t + s + 1)
                        for c in range(VC):
                            col = (s * VC + c) * PARTS
                            last = nc.tensor.transpose(nt_ps[s % 2][:, c, :], flat[:, col:col + PARTS], ident[:, :])
                        last.then_inc(normed_turned, 1)
                    if s > 0:
                        pe.wait_ge(nt_bank_free, 2 + SUBS * t + s)
                        for c in range(VC):
                            last = nc.tensor.matmul(y_ps[u][(s - 1) // HALF][:, (s - 1) % HALF, :], normed_t[(s - 1) % 2][:, c, :], wo_sb[:, c, :],
                                                    start=(c == 0), stop=(c == VC - 1))
                        last.then_inc(projected, 1)

            def second_half(t, u, i):
                pe.wait_ge(out_ready, SUBS * t + SUBS)
                pe.wait_ge(ot_copied, EC * t)
                for c in range(EC):
                    for s in range(SUBS):
                        last = nc.tensor.transpose(ot_ps[c][:, s * PARTS:(s + 1) * PARTS], out_sb[u][:, s, c * PARTS:(c + 1) * PARTS], ident[:, :])
                    last.then_inc(out_turned, 1)

            staggered(pe, first_half, second_half)


def ffn_split_phase(nc, keep, rounded, mid, mid_t, out):
    out_v = out.rearrange("b (t s p) e -> (b t) p s e", s=SUBS, p=PARTS)
    mid_v = mid.rearrange("(t s) p e -> t p s e", s=SUBS)
    with Room(nc, "ffn") as room:
        xt = [room.sb(f"xt{u}", [PARTS, EC, TILE]) for u in range(2)]
        xt_p = [[room.sb(f"xt_p{u}{k}", [PARTS, EC, TILE], F32R) for k in range(2)] for u in range(2)]
        x_sb = [room.sb(f"x{u}", [PARTS, SUBS, EMBED]) for u in range(2)]
        gate = [room.sb(f"gate{n}", [PARTS, TILE]) for n in range(2)]
        whole = [room.sb(f"whole{n}", [PARTS, TILE]) for n in range(2)]
        hid_a = [room.sb(f"hid_a{k}", [PARTS, HC, TILE], F32R) for k in range(2)]
        hid_b = [room.sb(f"hid_b{k}", [PARTS, HC, TILE], F32R) for k in range(2)]
        y = room.sb("y", [PARTS, SUBS, EMBED])
        stats = room.sb("stats", [PARTS, SUBS, 6])
        mean_var = room.sb("mean_var", [PARTS, SUBS, 2])
        var = room.sb("var", [PARTS, SUBS])
        root = room.sb("root", [PARTS, SUBS])
        quotient = room.sb("quotient", [PARTS, SUBS])
        rstd = room.sb("rstd", [PARTS, SUBS])
        out_sb = [room.sb(f"out{u}", [PARTS, SUBS, EMBED]) for u in range(2)]
        up_ps = [[room.ps(f"up_ps{n}{k}", [PARTS, TILE]) for k in range(2)] for n in range(2)]
        hid_ps = [room.ps(f"hid_ps{n}", [PARTS, TILE]) for n in range(2)]
        y_ps = [room.ps(f"y_ps{n}", [PARTS, EMBED]) for n in range(2)]

        loaded = [room.sem(f"loaded{u}") for u in range(2)]
        xt_high = room.sem("xt_high")
        xt_low = room.sem("xt_low")
        up_projected = room.sem("up_projected")
        up_free = room.sem("up_free")
        gate_ready = room.sem("gate_ready")
        high_a = room.sem("high_a")
        low_a = room.sem("low_a")
        hid_projected = room.sem("hid_projected")
        hid_free = room.sem("hid_free")
        hid_high = room.sem("hid_high")
        hid_low = room.sem("hid_low")
        y_projected = room.sem("y_projected")
        y_free = room.sem("y_free")
        vec = room.sem("vec")
        aggr_begun = room.sem("aggr_begun")
        var_ready = room.sem("var_ready")
        root_ready = room.sem("root_ready")
        out_ready = room.sem("out_ready")
        stored = [room.sem(f"stored{u}") for u in range(2)]
        VEC = 1 + 2 * SUBS + 5
        ROUNDS = TILES // 2
        give_credits(nc, [(up_free, 2), (hid_free, 2), (y_free, 2)])
        block = room.block()

        @block.sync
        def _(sp):
            def load(t, u):
                sp.dma_start(xt[u][:, :, :], mid_t[:, :, bass.ts(t, TILE)].rearrange("c p n -> p c n")).then_inc(loaded[u], 16)
                sp.dma_start(x_sb[u][:, :, :], mid_v[t]).then_inc(loaded[u], 16)

            def tile(i, u, last):
                t = 2 * i + u
                sp.wait_ge(out_ready, SUBS * t + SUBS)
                if not last:
                    load(t + 2, u)
                sp.dma_start(out_v[t], out_sb[u][:, :, :]).then_inc(stored[u], 16)

            wide = sp.value_load(keep["wide"][0:1, 0:1])
            with sp.If(wide == 0):
                for u in range(2):
                    load(u, u)
                with sp.Fori(0, ROUNDS - 1) as i:
                    for u in range(2):
                        tile(i, u, False)
                for u in range(2):
                    tile(ROUNDS - 1, u, True)
                for u in range(2):
                    sp.wait_ge(stored[u], 16 * ROUNDS)

        @block.tensor
        def _(pe):
            def tile(t, u):
                pe.wait_ge(xt_low, t + 1)
                for m in range(HC):
                    cols = slice(m * PARTS, (m + 1) * PARTS)
                    pe.wait_ge(up_free, HC * t + m + 1)
                    for w, bank in zip(("w1t", "w2t"), up_ps[m % 2]):
                        for c in range(EC):
                            for k in range(2):
                                last = nc.tensor.matmul(bank[:, :], rounded[w][:, c, cols], xt_p[u][k][:, c, :],
                                                        start=(c == 0 and k == 0), stop=(c == EC - 1 and k == 1))
                    last.then_inc(up_projected, 1)
                for layer, (w, hid, ready, first) in enumerate([("h1t", hid_a, low_a, HC * t), ("h2t", hid_b, hid_low, 2 * HC * t)]):
                    for m in range(HC):
                        pe.wait_ge(hid_free, 2 * HC * t + HC * layer + m + 1)
                        for c in range(HC):
                            if m == 0:
                                pe.wait_ge(ready, first + c + 1)
                            for k in range(2):
                                last = nc.tensor.matmul(hid_ps[m % 2][:, :], rounded[w][:, c, m * PARTS:(m + 1) * PARTS], hid[k][:, c, :],
                                                        start=(c == 0 and k == 0), stop=(c == HC - 1 and k == 1))
                        last.then_inc(hid_projected, 1)
                for s in range(SUBS):
                    pe.wait_ge(y_free, SUBS * t + s + 1)
                    for c in range(HC):
                        if s == 0:
                            pe.wait_ge(hid_low, 2 * HC * t + HC + c + 1)
                        for k in range(2):
                            last = nc.tensor.matmul(y_ps[s % 2][:, :], hid_a[k][:, c, s * PARTS:(s + 1) * PARTS], rounded["w3t"][:, c, :],
                                                    start=(c == 0 and k == 0), stop=(c == HC - 1 and k == 1))
                    last.then_inc(y_projected, 1)

            wide = pe.value_load(keep["wide"][0:1, 0:1])
            with pe.If(wide == 0):
                with pe.Fori(0, ROUNDS) as i:
                    for u in range(2):
                        tile(2 * i + u, u)

        @block.scalar
        def _(act):
            def tile(t):
                for m in range(HC):
                    act.wait_ge(up_projected, HC * t + m + 1)
                    nc.scalar.activation(gate[m % 2][:, :], up_ps[m % 2][0][:, :], ACT.Silu, scale=keep["s1"][:, m:m + 1]).then_inc(gate_ready, 1)
                for layer, (hid, s) in enumerate([(hid_b, "hs1"), (hid_a, "hs2")]):
                    for m in range(HC):
                        n = 2 * HC * t + HC * layer + m
                        act.wait_ge(hid_projected, n + 1)
                        if layer == 0 and m < 2:
                            act.wait_ge(low_a, HC * t + HC - 1 + m)
                        else:
                            act.wait_ge(hid_low, n - 1)
                        nc.scalar.activation(whole[m % 2][:, :], hid_ps[m % 2][:, :], ACT.Gelu, scale=keep[s][:, m:m + 1]).then_inc(hid_free, 1)
                        act.wait_ge(hid_free, 2 + n + 1)
                        nc.scalar.copy(hid[0][:, m, :], whole[m % 2][:, :]).then_inc(hid_high, 1)
                act.wait_ge(var_ready, t + 1)
                nc.scalar.activation(root[:, :], var[:, :], ACT.Sqrt).then_inc(root_ready, 1)

            wide = act.value_load(keep["wide"][0:1, 0:1])
            with act.If(wide == 0):
                with act.Fori(0, ROUNDS) as i:
                    for u in range(2):
                        tile(2 * i + u)

        @block.vector
        def _(dve):
            def cut_x(t, u, i):
                dve.wait_ge(loaded[u], 32 * i + 32)
                nc.vector.tensor_copy(xt_p[u][0][:, :, :], xt[u][:, :, :]).then_inc(xt_high, 1)
                dve.wait_ge(xt_high, t + 1)
                nc.vector.tensor_tensor(xt_p[u][1][:, :, :], xt[u][:, :, :], xt_p[u][0][:, :, :].bitcast(F32), ALU.subtract).then_inc(xt_low, 1)

            def tile(t, u, i, more):
                for m in range(HC):
                    n = HC * t + m
                    dve.wait_ge(gate_ready, n + 1)
                    if m < 2:
                        dve.wait_ge(hid_low, 2 * HC * t)
                    else:
                        dve.wait_ge(low_a, n - 1)
                    nc.vector.scalar_tensor_tensor(whole[m % 2][:, :], up_ps[m % 2][1][:, :], keep["s2"][:, m:m + 1], gate[m % 2][:, :],
                                                   ALU.mult, ALU.mult).then_inc(up_free, 1)
                    dve.wait_ge(up_free, 2 + n + 1)
                    nc.vector.tensor_copy(hid_a[0][:, m, :], whole[m % 2][:, :]).then_inc(high_a, 1)
                    dve.wait_ge(high_a, n + 1)
                    nc.vector.tensor_tensor(hid_a[1][:, m, :], whole[m % 2][:, :], hid_a[0][:, m, :].bitcast(F32), ALU.subtract).then_inc(low_a, 1)
                for layer, hid in enumerate((hid_b, hid_a)):
                    for m in range(HC):
                        dve.wait_ge(hid_high, 2 * HC * t + HC * layer + m + 1)
                        nc.vector.tensor_tensor(hid[1][:, m, :], whole[m % 2][:, :], hid[0][:, m, :].bitcast(F32), ALU.subtract).then_inc(hid_low, 1)
                if more:
                    cut_x(t + 1, 1 - u, i + u)
                dve.wait_ge(out_ready, SUBS * t)
                for s in range(SUBS):
                    dve.wait_ge(y_projected, SUBS * t + s + 1)
                    nc.vector.tensor_tensor(y[:, s, :], y_ps[s % 2][:, :], keep["s3"][:, :], ALU.mult).then_inc(y_free, 1)
                layer_norm(dve, nc, t, u, i)

            def layer_norm(dve, nc, t, u, i):
                v0 = VEC * t
                dve.wait_ge(y_free, 2 + SUBS * t + SUBS)
                nc.vector.tensor_tensor(y[:, :, :], y[:, :, :], x_sb[u][:, :, :], ALU.add).then_inc(vec, 1)
                dve.wait_ge(vec, v0 + 1)
                for s in range(SUBS):
                    nc.vector.bn_stats(stats[:, s, :], y[:, s, :]).then_inc(vec, 1)
                dve.wait_ge(vec, v0 + 1 + SUBS)
                dve.sem_inc(aggr_begun, 1)
                for s in range(SUBS):
                    nc.vector.bn_aggr(mean_var[:, s, :], stats[:, s, :]).then_inc(vec, 1)
                dve.wait_ge(vec, v0 + 1 + 2 * SUBS)
                nc.vector.tensor_scalar(var[:, :], mean_var[:, :, 1], LN_EPS, None, ALU.add).then_inc(var_ready, 1)
                dve.wait_ge(root_ready, t + 1)
                v1 = v0 + 1 + 2 * SUBS
                nc.vector.reciprocal(quotient[:, :], root[:, :]).then_inc(vec, 1)
                dve.wait_ge(vec, v1 + 1)
                nc.vector.tensor_tensor(quotient[:, :], quotient[:, :], var[:, :], ALU.mult).then_inc(vec, 1)
                dve.wait_ge(vec, v1 + 2)
                nc.vector.tensor_tensor(quotient[:, :], quotient[:, :], root[:, :], ALU.add).then_inc(vec, 1)
                dve.wait_ge(vec, v1 + 3)
                nc.vector.tensor_scalar(quotient[:, :], quotient[:, :], 0.5, None, ALU.mult).then_inc(vec, 1)
                dve.wait_ge(vec, v1 + 4)
                nc.vector.reciprocal(rstd[:, :], quotient[:, :]).then_inc(vec, 1)
                dve.wait_ge(vec, v1 + 5)
                dve.wait_ge(stored[u], 16 * i)
                for s in range(SUBS):
                    nc.vector.tensor_scalar(out_sb[u][:, s, :], y[:, s, :], mean_var[:, s, 0:1], rstd[:, s:s + 1], ALU.subtract, ALU.mult).then_inc(out_ready, 1)

            wide = dve.value_load(keep["wide"][0:1, 0:1])
            with dve.If(wide == 0):
                cut_x(0, 0, 0)
                with dve.Fori(0, ROUNDS - 1) as i:
                    for u in range(2):
                        tile(2 * i + u, u, i, True)
                for u in range(2):
                    tile(2 * ROUNDS - 2 + u, u, ROUNDS - 1, u == 0)


def ffn_full_phase(nc, keep, ffn_w, mid, mid_t, out):
    w1, w2, h1, h2, w3 = ffn_w
    out_v = out.rearrange("b (t s p) e -> (b t) p s e", s=SUBS, p=PARTS)
    mid_v = mid.rearrange("(t s) p e -> t p s e", s=SUBS)
    G, W0 = len(TURN_GROUPS), len(W3_GROUPS)
    with ExitStack() as weights:
        whole_w = {name: weights.enter_context(nc.sbuf_tensor(f"{name}_f", shape, F32)) for name, shape in FFN_SHAPES}
        with Room(nc, "wide") as room:
            w_rows = [room.sb(f"w_rows{u}", [PARTS, ROW_COLS]) for u in range(2)]
            w3_rows = room.sb("w3_rows", [PARTS, EC * HIDDEN])
            turn_ps = [room.ps(f"turn_ps{n}", [PARTS, 4, PARTS]) for n in range(2)]
            w3_loaded = room.sem("w3_loaded")
            w_loaded = [room.sem(f"w_loaded{u}") for u in range(2)]
            turned = room.sem("turned")
            turn_bank_free = room.sem("turn_bank_free")
            give_credits(nc, [(turn_bank_free, 2)])
            block = room.block()

            @block.sync
            def _(sp):
                def load(t, u):
                    col = 0
                    for w in (w1, w2, h1, h2):
                        n = w.shape[1]
                        sp.dma_start(w_rows[u][:, col:col + n], w[bass.ts(t, PARTS), :]).then_inc(w_loaded[u], 16)
                        col += n

                wide = sp.value_load(keep["wide"][0:1, 0:1])
                with sp.If(wide != 0):
                    sp.dma_start(w3_rows[:, :].rearrange("p (o i) -> p o i", o=EC), w3.rearrange("(o p) i -> p o i", p=PARTS)).then_inc(w3_loaded, 16)
                    for u in range(2):
                        load(u, u)
                    with sp.Fori(0, HC // 2 - 1) as i:
                        for u in range(2):
                            sp.wait_ge(turned, W0 + G * (2 * i + u) + G)
                            load(2 * i + u + 2, u)

            @block.tensor
            def _(pe):
                wide = pe.value_load(keep["wide"][0:1, 0:1])
                with pe.If(wide != 0):
                    pe.wait_ge(w3_loaded, 16)
                    for n, (o, c) in enumerate(W3_GROUPS):
                        pe.wait_ge(turn_bank_free, n + 1)
                        for k in range(4):
                            col = o * HIDDEN + (c + k) * PARTS
                            last = nc.tensor.transpose(turn_ps[n % 2][:, k, :], w3_rows[:, col:col + PARTS], keep["ident"][:, :])
                        last.then_inc(turned, 1)
                    with pe.Fori(0, HC // 2) as i:
                        for u in range(2):
                            pe.wait_ge(w_loaded[u], 64 * i + 64)
                            for g, (col, _, _, n) in enumerate(TURN_GROUPS):
                                pe.wait_ge(turn_bank_free, W0 + G * (2 * i + u) + g + 1)
                                for k in range(n):
                                    last = nc.tensor.transpose(turn_ps[g % 2][:, k, :], w_rows[u][:, col + k * PARTS:col + (k + 1) * PARTS], keep["ident"][:, :])
                                last.then_inc(turned, 1)

            @block.scalar
            def _(act):
                wide = act.value_load(keep["wide"][0:1, 0:1])
                with act.If(wide != 0):
                    for n, (o, c) in enumerate(W3_GROUPS):
                        act.wait_ge(turned, n + 1)
                        nc.scalar.copy(whole_w["w3t"][:, c:c + 4, o * PARTS:(o + 1) * PARTS], turn_ps[n % 2][:, :, :]).then_inc(turn_bank_free, 1)
                    with act.Fori(0, HC) as t:
                        for g, (_, name, c, n) in enumerate(TURN_GROUPS):
                            act.wait_ge(turned, W0 + G * t + g + 1)
                            nc.scalar.copy(whole_w[name][:, c:c + n, bass.ts(t, PARTS)], turn_ps[g % 2][:, 0:n, :]).then_inc(turn_bank_free, 1)

        with Room(nc, "full") as room:
            xt = [room.sb(f"xt{u}", [PARTS, EC, TILE]) for u in range(2)]
            x_sb = [room.sb(f"x{u}", [PARTS, SUBS, EMBED]) for u in range(2)]
            gate = [room.sb(f"gate{n}", [PARTS, TILE]) for n in range(2)]
            hid_a = room.sb("hid_a", [PARTS, HC, TILE])
            hid_b = room.sb("hid_b", [PARTS, HC, TILE])
            y = room.sb("y", [PARTS, SUBS, EMBED])
            stats = room.sb("stats", [PARTS, SUBS, 6])
            mean_var = room.sb("mean_var", [PARTS, SUBS, 2])
            var = room.sb("var", [PARTS, SUBS])
            root = room.sb("root", [PARTS, SUBS])
            quotient = room.sb("quotient", [PARTS, SUBS])
            rstd = room.sb("rstd", [PARTS, SUBS])
            out_sb = [room.sb(f"out{u}", [PARTS, SUBS, EMBED]) for u in range(2)]
            up_ps = [[room.ps(f"up_ps{n}{k}", [PARTS, TILE]) for k in range(2)] for n in range(2)]
            hid_ps = [room.ps(f"hid_ps{n}", [PARTS, TILE]) for n in range(2)]
            y_ps = [room.ps(f"y_ps{n}", [PARTS, EMBED]) for n in range(2)]

            loaded = [room.sem(f"loaded{u}") for u in range(2)]
            up_projected = room.sem("up_projected")
            up_free = room.sem("up_free")
            gate_ready = room.sem("gate_ready")
            hid_projected = room.sem("hid_projected")
            hid_free = room.sem("hid_free")
            y_projected = room.sem("y_projected")
            y_free = room.sem("y_free")
            vec = room.sem("vec")
            aggr_begun = room.sem("aggr_begun")
            var_ready = room.sem("var_ready")
            root_ready = room.sem("root_ready")
            out_ready = room.sem("out_ready")
            stored = [room.sem(f"stored{u}") for u in range(2)]
            VEC = 1 + 2 * SUBS + 5
            ROUNDS = TILES // 2
            give_credits(nc, [(up_free, 2), (hid_free, 2), (y_free, 2)])
            block = room.block()

            @block.sync
            def _(sp):
                def load(t, u):
                    sp.dma_start(xt[u][:, :, :], mid_t[:, :, bass.ts(t, TILE)].rearrange("c p n -> p c n")).then_inc(loaded[u], 16)
                    sp.dma_start(x_sb[u][:, :, :], mid_v[t]).then_inc(loaded[u], 16)

                def tile(i, u, last):
                    t = 2 * i + u
                    sp.wait_ge(out_ready, SUBS * t + SUBS)
                    if not last:
                        load(t + 2, u)
                    sp.dma_start(out_v[t], out_sb[u][:, :, :]).then_inc(stored[u], 16)

                wide = sp.value_load(keep["wide"][0:1, 0:1])
                with sp.If(wide != 0):
                    for u in range(2):
                        load(u, u)
                    with sp.Fori(0, ROUNDS - 1) as i:
                        for u in range(2):
                            tile(i, u, False)
                    for u in range(2):
                        tile(ROUNDS - 1, u, True)
                    for u in range(2):
                        sp.wait_ge(stored[u], 16 * ROUNDS)

            @block.tensor
            def _(pe):
                def tile(t, u, i):
                    pe.wait_ge(loaded[u], 32 * i + 32)
                    for m in range(HC):
                        cols = slice(m * PARTS, (m + 1) * PARTS)
                        pe.wait_ge(up_free, HC * t + m + 1)
                        for w, bank in zip(("w1t", "w2t"), up_ps[m % 2]):
                            for c in range(EC):
                                last = nc.tensor.matmul(bank[:, :], whole_w[w][:, c, cols], xt[u][:, c, :], start=(c == 0), stop=(c == EC - 1))
                        last.then_inc(up_projected, 1)
                    for layer, (w, hid, ready, first) in enumerate([("h1t", hid_a, up_free, 2 + HC * t), ("h2t", hid_b, hid_free, 2 + 2 * HC * t)]):
                        for m in range(HC):
                            pe.wait_ge(hid_free, 2 * HC * t + HC * layer + m + 1)
                            for c in range(HC):
                                if m == 0:
                                    pe.wait_ge(ready, first + c + 1)
                                last = nc.tensor.matmul(hid_ps[m % 2][:, :], whole_w[w][:, c, m * PARTS:(m + 1) * PARTS], hid[:, c, :],
                                                        start=(c == 0), stop=(c == HC - 1))
                            last.then_inc(hid_projected, 1)
                    for s in range(SUBS):
                        pe.wait_ge(y_free, SUBS * t + s + 1)
                        for c in range(HC):
                            if s == 0:
                                pe.wait_ge(hid_free, 2 + 2 * HC * t + HC + c + 1)
                            last = nc.tensor.matmul(y_ps[s % 2][:, :], hid_a[:, c, s * PARTS:(s + 1) * PARTS], whole_w["w3t"][:, c, :],
                                                    start=(c == 0), stop=(c == HC - 1))
                        last.then_inc(y_projected, 1)

                wide = pe.value_load(keep["wide"][0:1, 0:1])
                with pe.If(wide != 0):
                    with pe.Fori(0, ROUNDS) as i:
                        for u in range(2):
                            tile(2 * i + u, u, i)

            @block.scalar
            def _(act):
                def tile(t):
                    for m in range(HC):
                        act.wait_ge(up_projected, HC * t + m + 1)
                        nc.scalar.activation(gate[m % 2][:, :], up_ps[m % 2][0][:, :], ACT.Silu, scale=keep["s1"][:, m:m + 1]).then_inc(gate_ready, 1)
                    for layer, (hid, s) in enumerate([(hid_b, "hs1"), (hid_a, "hs2")]):
                        for m in range(HC):
                            act.wait_ge(hid_projected, 2 * HC * t + HC * layer + m + 1)
                            nc.scalar.activation(hid[:, m, :], hid_ps[m % 2][:, :], ACT.Gelu, scale=keep[s][:, m:m + 1]).then_inc(hid_free, 1)
                    act.wait_ge(var_ready, t + 1)
                    nc.scalar.activation(root[:, :], var[:, :], ACT.Sqrt).then_inc(root_ready, 1)

                wide = act.value_load(keep["wide"][0:1, 0:1])
                with act.If(wide != 0):
                    with act.Fori(0, ROUNDS) as i:
                        for u in range(2):
                            tile(2 * i + u)

            @block.vector
            def _(dve):
                def tile(t, u, i):
                    for m in range(HC):
                        dve.wait_ge(gate_ready, HC * t + m + 1)
                        nc.vector.scalar_tensor_tensor(hid_a[:, m, :], up_ps[m % 2][1][:, :], keep["s2"][:, m:m + 1], gate[m % 2][:, :],
                                                       ALU.mult, ALU.mult).then_inc(up_free, 1)
                    dve.wait_ge(out_ready, SUBS * t)
                    for s in range(SUBS):
                        dve.wait_ge(y_projected, SUBS * t + s + 1)
                        nc.vector.tensor_tensor(y[:, s, :], y_ps[s % 2][:, :], keep["s3"][:, :], ALU.mult).then_inc(y_free, 1)
                    v0 = VEC * t
                    dve.wait_ge(y_free, 2 + SUBS * t + SUBS)
                    nc.vector.tensor_tensor(y[:, :, :], y[:, :, :], x_sb[u][:, :, :], ALU.add).then_inc(vec, 1)
                    dve.wait_ge(vec, v0 + 1)
                    for s in range(SUBS):
                        nc.vector.bn_stats(stats[:, s, :], y[:, s, :]).then_inc(vec, 1)
                    dve.wait_ge(vec, v0 + 1 + SUBS)
                    dve.sem_inc(aggr_begun, 1)
                    for s in range(SUBS):
                        nc.vector.bn_aggr(mean_var[:, s, :], stats[:, s, :]).then_inc(vec, 1)
                    dve.wait_ge(vec, v0 + 1 + 2 * SUBS)
                    nc.vector.tensor_scalar(var[:, :], mean_var[:, :, 1], LN_EPS, None, ALU.add).then_inc(var_ready, 1)
                    dve.wait_ge(root_ready, t + 1)
                    v1 = v0 + 1 + 2 * SUBS
                    nc.vector.reciprocal(quotient[:, :], root[:, :]).then_inc(vec, 1)
                    dve.wait_ge(vec, v1 + 1)
                    nc.vector.tensor_tensor(quotient[:, :], quotient[:, :], var[:, :], ALU.mult).then_inc(vec, 1)
                    dve.wait_ge(vec, v1 + 2)
                    nc.vector.tensor_tensor(quotient[:, :], quotient[:, :], root[:, :], ALU.add).then_inc(vec, 1)
                    dve.wait_ge(vec, v1 + 3)
                    nc.vector.tensor_scalar(quotient[:, :], quotient[:, :], 0.5, None, ALU.mult).then_inc(vec, 1)
                    dve.wait_ge(vec, v1 + 4)
                    nc.vector.reciprocal(rstd[:, :], quotient[:, :]).then_inc(vec, 1)
                    dve.wait_ge(vec, v1 + 5)
                    dve.wait_ge(stored[u], 16 * i)
                    for s in range(SUBS):
                        nc.vector.tensor_scalar(out_sb[u][:, s, :], y[:, s, :], mean_var[:, s, 0:1], rstd[:, s:s + 1], ALU.subtract, ALU.mult).then_inc(out_ready, 1)

                wide = dve.value_load(keep["wide"][0:1, 0:1])
                with dve.If(wide != 0):
                    with dve.Fori(0, ROUNDS) as i:
                        for u in range(2):
                            tile(2 * i + u, u, i)


INPUTS = ["L0_attn_x", "L0_attn_Wq1", "L0_attn_Wq2", "L0_attn_Wk1", "L0_attn_Wk2", "L0_attn_Wv", "L0_attn_Wo",
          "L0_attn_lq1", "L0_attn_lk1", "L0_attn_lq2", "L0_attn_lk2",
          "L0_ffn_w1_w", "L0_ffn_w1_s", "L0_ffn_w2_w", "L0_ffn_w2_s", "L0_ffn_h1_w", "L0_ffn_h1_s",
          "L0_ffn_h2_w", "L0_ffn_h2_s", "L0_ffn_w3_w", "L0_ffn_w3_s"]


def kernel(**inputs):
    import numpy as np
    import concourse.bacc as bacc
    from concourse.bass_utils import run_bass_kernel_spmd

    nc = bacc.Bacc("TRN2", target_bir_lowering=False, num_devices=1)
    arrays, args = {}, []
    for name in INPUTS:
        a = np.ascontiguousarray(inputs[name])
        arrays[f"in_{name}"] = a
        args.append(nc.dram_tensor(f"in_{name}", a.shape, mybir.dt.from_np(a.dtype), kind="ExternalInput").ap())
    out = nc.dram_tensor("out", (BATCH, SEQ, EMBED), F32, kind="ExternalOutput").ap()
    layer_kernel(nc, *args, out)
    result = run_bass_kernel_spmd(nc, [arrays], core_ids=[0])
    return result.results[0]["out"]
```

```python
import math
from contextlib import ExitStack

import concourse.bass as bass
from concourse import mybir

F32 = mybir.dt.float32
F32R = mybir.dt.float32r
BF16 = mybir.dt.bfloat16
I32 = mybir.dt.int32
ACT = mybir.ActivationFunctionType
ALU = mybir.AluOpType
AXIS = mybir.AxisListType

BATCH, SEQ, EMBED = 2, 2048, 256
HEADS, HEAD_DIM = 16, 16
VALUE_DIM = 2 * HEAD_DIM
HIDDEN = 1024
TOKENS = BATCH * SEQ
PARTS = 128
TILE = 512
SUBS = TILE // PARTS
TILES = TOKENS // TILE
BLOCKS = TOKENS // PARTS
EC = EMBED // PARTS
HC = HIDDEN // PARTS
VC = HEADS * VALUE_DIM // PARTS
KEY_BLOCKS = SEQ // PARTS
QUERY_TILES = SEQ // TILE

SCALE = 1.0 / math.sqrt(HEAD_DIM)
LAM_INIT = 0.8 - 0.6 * math.exp(-0.3 * (12 - 1))
LN_EPS = 1e-5
LOWEST = -3.0e38

PART_PAIRS = [(0, 0), (1, 0), (2, 0), (0, 1), (1, 1), (0, 2)]
SCORE_ROWS = len(PART_PAIRS) * HEAD_DIM
SHIFT_ROWS = 3
STACK_ROWS = SCORE_ROWS + SHIFT_ROWS
KINDS = ("q1", "q2", "k1", "k2")
FFN_SHAPES = [("w1t", [PARTS, EC, HIDDEN]), ("w2t", [PARTS, EC, HIDDEN]), ("h1t", [PARTS, HC, HIDDEN]),
              ("h2t", [PARTS, HC, HIDDEN]), ("w3t", [PARTS, HC, EMBED])]
ROW_COLS = 2 * EMBED + 2 * HIDDEN
TURN_GROUPS = [(0, "w1t", 0, EC), (EMBED, "w2t", 0, EC)] + [
    (2 * EMBED + n * HIDDEN + c * PARTS, name, c, 4) for n, name in enumerate(("h1t", "h2t")) for c in range(0, HC, 4)]
LAYERS = 2 * HC
W3_GROUPS = [(o, c) for o in range(EC) for c in range(0, HC, 4)]
SAFE_BOUND = 30.0
BOUND_MARGIN = 1.02


def layer_kernel(nc, x, wq1, wq2, wk1, wk2, wv, wo, lq1, lk1, lq2, lk2,
                 w1, s1, w2, s2, h1, hs1, h2, hs2, w3, s3, out):
    qk_parts = nc.dram_tensor("qk_parts", (2, 3, EMBED, 2, TOKENS), BF16, kind="Internal").ap()
    values = nc.dram_tensor("values", (HEADS, PARTS, BLOCKS, VALUE_DIM), F32, kind="Internal").ap()
    shift = nc.dram_tensor("shift", (SHIFT_ROWS, HEADS, 2, TOKENS), BF16, kind="Internal").ap()
    diffs = nc.dram_tensor("diffs", (BLOCKS, PARTS, HEADS, VALUE_DIM), F32, kind="Internal").ap()

    with ExitStack() as ctx:
        def sb(name, shape, dt=F32):
            return ctx.enter_context(nc.sbuf_tensor(name, shape, dt))

        keep = dict(
            s1=sb("s1", [PARTS, HC]), s2=sb("s2", [PARTS, HC]), hs1=sb("hs1", [PARTS, HC]), hs2=sb("hs2", [PARTS, HC]),
            s3=sb("s3", [PARTS, EMBED]),
            ident=sb("ident", [PARTS, PARTS]), neg_lam=sb("neg_lam", [PARTS, HEADS]),
            bound=sb("bound", [PARTS, 4]), exact=sb("exact", [PARTS, 1], I32), wide=sb("wide", [PARTS, 1], I32),
        )
        ffn_w = (w1, w2, h1, h2, w3)
        finish = ctx.enter_context(Room(nc, "finish"))
        with ExitStack() as weights:
            rounded = {name: weights.enter_context(nc.sbuf_tensor(f"{name}_r", shape, F32R)) for name, shape in FFN_SHAPES}
            project_phase(nc, keep, rounded, x, (wq1, wq2, wk1, wk2), wv, (lq1, lk1, lq2, lk2),
                          ffn_w, (s1, s2, hs1, hs2, s3), qk_parts, values)
            with Room(nc, "heads") as room:
                heads = head_buffers(room)
                maximum_phase(nc, keep, heads, qk_parts, shift, values)
                attention_phase(nc, keep, heads, qk_parts, shift, values, diffs)
            sems = finish_sems(nc, finish)
            finish_phase(nc, keep, sems, "split", True, rounded, x, wo, diffs, out)
        whole_w = {name: sb(f"{name}_f", shape) for name, shape in FFN_SHAPES}
        turn_weights_phase(nc, keep, ffn_w, whole_w)
        finish_phase(nc, keep, sems, "full", False, whole_w, x, wo, diffs, out)


class Room:

    def __init__(self, nc, phase):
        self.nc, self.phase, self.ctx = nc, phase, ExitStack()

    def __enter__(self):
        return self

    def __exit__(self, *a):
        return self.ctx.__exit__(*a)

    def sb(self, name, shape, dt=F32):
        return self.ctx.enter_context(self.nc.sbuf_tensor(f"{self.phase}_{name}", shape, dt))

    def ps(self, name, shape):
        return self.ctx.enter_context(self.nc.psum_tensor(f"{self.phase}_{name}", shape, F32))

    def sem(self, name):
        return self.ctx.enter_context(self.nc.semaphore(f"{self.phase}_{name}"))

    def block(self):
        return self.ctx.enter_context(self.nc.Block())


def give_credits(nc, credits):
    with nc.Block() as block:
        @block.sync
        def _(sp):
            for sem, n in credits:
                sp.sem_inc(sem, n)


def project_phase(nc, keep, rounded, x, w_qk, wv, lam_in, ffn_w, ffn_s, qk_parts, values):
    w1, w2, h1, h2, w3 = ffn_w
    s1, s2, hs1, hs2, s3 = ffn_s
    M_TILES = len(KINDS) * EC
    PASSES = [(0, 0), (1, 0), (0, 1)]
    UNIT = TILE
    UNITS = ROW_COLS // UNIT
    W3_UNITS = EC * HIDDEN // UNIT
    x_v = x.rearrange("b (t s p) e -> (b t) p s e", s=SUBS, p=PARTS)
    with Room(nc, "proj") as room:
        wqk = [room.sb("wqk_high", [PARTS, len(KINDS), EC, EMBED], F32R), room.sb("wqk_low", [PARTS, len(KINDS), EC, EMBED], F32R)]
        wv_p = [room.sb("wv_high", [PARTS, EC * HEADS, VALUE_DIM], F32R), room.sb("wv_low", [PARTS, EC * HEADS, VALUE_DIM], F32R)]
        wv_mean = room.sb("wv_mean", [PARTS, EC * HEADS])
        lam_sb = room.sb("lam", [PARTS, 4, HEADS * HEAD_DIM])
        lam_sum = room.sb("lam_sum", [PARTS, 2, HEADS])
        lam_exp = room.sb("lam_exp", [PARTS, 2, HEADS])
        x_sb = [room.sb(f"x{u}", [PARTS, SUBS, EMBED]) for u in range(2)]
        xt = [[room.sb(f"xt{u}{k}", [PARTS, EC, TILE], F32R) for k in range(2)] for u in range(2)]
        parts = [room.sb(f"parts{n}", [PARTS, 3, TILE], BF16) for n in range(4)]
        resid = [room.sb(f"resid{n}", [PARTS, TILE]) for n in range(2)]
        biggest = room.sb("biggest", [PARTS, 2, TILE], BF16)
        smallest = room.sb("smallest", [PARTS, 2, TILE], BF16)
        small_col = room.sb("small_col", [PARTS, 2])
        big_col = room.sb("big_col", [PARTS, 3])
        big_all = room.sb("big_all", [PARTS, 3])
        v_sb = [room.sb(f"v{u}", [PARTS, HEADS, SUBS, VALUE_DIM]) for u in range(2)]
        wqk_whole = v_sb[1][:, :, :, :].rearrange("p h s d -> p (h s d)").rearrange("p (n c e) -> p n c e", n=len(KINDS), c=EC)
        wv_whole = v_sb[0][:, :, :, :].rearrange("p h s d -> p (h s d)")[:, 0:EC * HEADS * VALUE_DIM].rearrange("p (g d) -> p g d", d=VALUE_DIM)
        w_rows = [room.sb(f"w_rows{u}", [PARTS, ROW_COLS]) for u in range(2)]
        short = [room.sb(f"short{n}", [PARTS, UNIT], F32R) for n in range(2)]
        counts = room.sb("counts", [PARTS, UNITS * TILES + W3_UNITS])
        tile_counts = counts[:, 0:UNITS * TILES].rearrange("p (k t) -> p k t", t=TILES)
        ident = keep["ident"]
        x_ps = [room.ps(f"x_ps{c}", [PARTS, TILE]) for c in range(EC)]
        w_ps = room.ps("w_ps", [PARTS, 4, PARTS])
        qk_ps = [room.ps(f"qk_ps{n}", [PARTS, TILE]) for n in range(4)]
        v_ps = room.ps("v_ps", [PARTS, HEADS, VALUE_DIM])

        wqk_loaded = [room.sem(f"wqk_loaded{n}") for n in range(len(KINDS))]
        wv_loaded = room.sem("wv_loaded")
        lam_loaded = room.sem("lam_loaded")
        scales_loaded = room.sem("scales_loaded")
        s3_loaded = room.sem("s3_loaded")
        w3_loaded = room.sem("w3_loaded")
        x_loaded = [room.sem(f"x_loaded{u}") for u in range(2)]
        w_loaded = [room.sem(f"w_loaded{u}") for u in range(2)]
        ident_done = room.sem("ident_done")
        wqk_high_done = room.sem("wqk_high_done")
        wqk_ready = room.sem("wqk_ready")
        wv_centred = room.sem("wv_centred")
        wv_high_done = room.sem("wv_high_done")
        wv_ready = room.sem("wv_ready")
        ones_done = room.sem("ones_done")
        lam_ready = room.sem("lam_ready")
        exp_done = room.sem("exp_done")
        x_turned = room.sem("x_turned")
        w_turned = room.sem("w_turned")
        w_bank_free = room.sem("w_bank_free")
        xt_high = room.sem("xt_high")
        xt_low = room.sem("xt_low")
        short_done = room.sem("short_done")
        compared = room.sem("compared")
        qk_projected = room.sem("qk_projected")
        qk_bank_free = room.sem("qk_bank_free")
        high_ready = room.sem("high_ready")
        mid_ready = room.sem("mid_ready")
        parts_ready = room.sem("parts_ready")
        parts_stored = [room.sem(f"parts_stored{n}") for n in range(4)]
        biggest_done = room.sem("biggest_done")
        v_projected = room.sem("v_projected")
        v_bank_free = room.sem("v_bank_free")
        v_stored = [room.sem(f"v_stored{u}") for u in range(2)]
        big_ready = room.sem("big_ready")
        big_reduced = room.sem("big_reduced")
        flag_steps = room.sem("flag_steps")

        WG = len(TURN_GROUPS)
        X_AT = 1
        GROUP_AT = {1: 0, 2: 1, 3: 2, 4: 3, 5: 4, 6: 5}
        V_AT = {2: 0, 4: 1, 6: 2, 7: 3}
        UNIT_AT = {m: m - (M_TILES - UNITS) for m in range(M_TILES - UNITS, M_TILES)}

        def all_tiles(eng, tile):
            with eng.Fori(0, TILES // 2 - 1) as i:
                for u in range(2):
                    tile(2 * i + u, u, i, True)
            for u in range(2):
                tile(TILES - 2 + u, u, TILES // 2 - 1, u == 0)

        give_credits(nc, [(w_bank_free, 1), (qk_bank_free, 4), (v_bank_free, 1), (compared, 2), (parts_ready, 2), (w_turned, 1)]
                     + [(sem, 16) for sem in parts_stored + v_stored])
        block = room.block()

        @block.sync
        def _(sp):
            def load_x(t, u):
                sp.dma_start(x_sb[u][:, :, :], x_v[t]).then_inc(x_loaded[u], 16)

            def load_w(t, u, n):
                w, col = ((w1, 0), (w2, EMBED), (h1, 2 * EMBED), (h2, 2 * EMBED + HIDDEN))[n]
                sp.dma_start(w_rows[u][:, col:col + w.shape[1]], w[bass.ts(t, PARTS), :]).then_inc(w_loaded[u], 16)

            def store_v(t, u):
                sp.wait_ge(v_bank_free, 1 + SUBS * t + SUBS)
                sp.dma_start(values[:, :, bass.ts(t, SUBS), :].rearrange("h p s d -> p h (s d)"),
                             v_sb[u][:, :, :, :].rearrange("p h s d -> p h (s d)")).then_inc(v_stored[u], 16)

            def tile(t, u, r, more):
                for m in range(M_TILES):
                    kind, c = divmod(m, EC)
                    sp.wait_ge(parts_ready, 2 + M_TILES * t + m + 1)
                    sp.dma_start(qk_parts[kind // 2, :, c * PARTS:(c + 1) * PARTS, kind % 2, bass.ts(t, TILE)].rearrange("a p n -> p a n"),
                                 parts[m % 4][:, :, :]).then_inc(parts_stored[m % 4], 16)
                    if m == 0 and not isinstance(r, int):
                        sp.wait_ge(x_turned, EC * t + EC)
                        load_x(t + 2, u)
                    if 1 <= m <= 4:
                        if m == 1:
                            sp.wait_ge(w_turned, 1 + WG * t)
                            sp.wait_ge(compared, 2 + UNITS * t)
                        if more:
                            load_w(t + 1, 1 - u, m - 1)
                        elif m == 1:
                            sp.dma_start(w_rows[1 - u][:, 0:EC * HIDDEN].rearrange("p (o i) -> p o i", o=EC), w3.rearrange("(o p) i -> p o i", p=PARTS)).then_inc(w3_loaded, 16)
                store_v(t, u)

            load_x(0, 0)
            for n in range(len(ffn_w) - 1):
                load_w(0, 0, n)
            load_x(1, 1)
            with nc.allow_non_contiguous_dma(reason="small vectors of scales"):
                for name, s in (("s1", s1), ("s2", s2), ("hs1", hs1), ("hs2", hs2)):
                    sp.dma_start(keep[name][:, :], s.rearrange("(c p) -> p c", p=PARTS)).then_inc(scales_loaded, 16)
            all_tiles(sp, tile)
            for u in range(2):
                sp.wait_ge(v_stored[u], 16 + 16 * (TILES // 2))
            for n in range(4):
                sp.wait_ge(parts_stored[n], 16 + 16 * (TILES * M_TILES // 4))
            sp.wait_ge(scales_loaded, 16 * 4)
            sp.wait_ge(s3_loaded, 16)

        @block.gpsimd
        def _(pool):
            pool.memset(ident[:, :], 0.0).then_inc(ident_done, 1)
            pool.wait_ge(ident_done, 1)
            pool.affine_select(out=ident[:, :], in_=ident[:, :], compare_op=ALU.not_equal, fill=1.0, base=0,
                               pattern=[[-1, PARTS]], channel_multiplier=1).then_inc(ident_done, 1)
            for n, v in enumerate(lam_in):
                pool.dma_start(lam_sb[:, n, :], v.rearrange("h d -> (h d)").partition_broadcast(PARTS)).then_inc(lam_loaded, 16)
            pool.dma_start(keep["s3"][:, :], s3.partition_broadcast(PARTS)).then_inc(s3_loaded, 16)
            pool.wait_ge(wqk_ready, len(KINDS))
            pool.wait_ge(wv_ready, 1)
            for u in range(2):
                pool.memset(v_sb[u][:, :, :, VALUE_DIM - 1:VALUE_DIM], 1.0).then_inc(ones_done, 1)
            with pool.Fori(0, TILES) as t:
                for m in range(M_TILES):
                    n = M_TILES * t + m
                    pool.wait_ge(mid_ready, n + 1)
                    pool.tensor_tensor(parts[m % 4][:, 2, :], resid[m % 2][:, :], parts[m % 4][:, 1, :], ALU.subtract).then_inc(parts_ready, 1)
            pool.wait_ge(big_ready, 2)
            pool.partition_all_reduce(big_all[:, :], big_col[:, :], PARTS, bass.bass_isa.ReduceOp.max).then_inc(big_reduced, 1)

        @block.scalar
        def _(act):
            for n, w in enumerate(w_qk):
                act.dma_start(wqk_whole[:, n, :, :], w.rearrange("(c p) n -> p c n", p=PARTS)).then_inc(wqk_loaded[n], 16)
            act.dma_start(wv_whole[:, :, :].rearrange("p (c h) d -> p c (h d)", c=EC),
                          wv.rearrange("(c p) n -> p c n", p=PARTS)).then_inc(wv_loaded, 16)
            def high_x(t, u):
                for c in range(EC):
                    act.wait_ge(x_turned, EC * t + c + 1)
                    nc.scalar.copy(xt[u][0][:, c, :], x_ps[c][:, :]).then_inc(xt_high, 1)

            def tile(t, u, r, more):
                for m in range(M_TILES + 1):
                    n = M_TILES * t + m
                    if m < M_TILES:
                        act.wait_ge(qk_projected, n + 1)
                        act.wait_ge(parts_stored[m % 4], 16 * (t * (M_TILES // 4) + m // 4) + 16)
                        nc.scalar.copy(parts[m % 4][:, 0, :], qk_ps[m % 4][:, :]).then_inc(high_ready, 1)
                    if m in UNIT_AT:
                        k = UNIT_AT[m]
                        act.wait_ge(w_loaded[u], 64 * r + 64)
                        act.wait_ge(compared, UNITS * t + k + 1)
                        nc.scalar.copy(short[(UNITS * u + k) % 2][:, :], w_rows[u][:, k * UNIT:(k + 1) * UNIT]).then_inc(short_done, 1)
                    if m > 0:
                        act.wait_ge(qk_bank_free, 4 + n)
                        nc.scalar.copy(parts[(m - 1) % 4][:, 1, :], resid[(m - 1) % 2][:, :]).then_inc(mid_ready, 1)
                    if m in V_AT:
                        s = V_AT[m]
                        if s == 0:
                            act.wait_ge(ones_done, 2)
                            act.wait_ge(v_stored[u], 16 * r + 16)
                        act.wait_ge(v_projected, SUBS * t + s + 1)
                        nc.scalar.copy(v_sb[u][:, :, s, 0:VALUE_DIM - 1], v_ps[:, :, 0:VALUE_DIM - 1]).then_inc(v_bank_free, 1)
                    if m in GROUP_AT:
                        _, name, c, k = TURN_GROUPS[GROUP_AT[m]]
                        act.wait_ge(w_turned, 1 + WG * t + GROUP_AT[m] + 1)
                        nc.scalar.copy(rounded[name][:, c:c + k, bass.ts(t, PARTS)], w_ps[:, 0:k, :]).then_inc(w_bank_free, 1)
                    if more and m == X_AT:
                        high_x(t + 1, 1 - u)

            for n in range(len(KINDS)):
                act.wait_ge(wqk_loaded[n], 16)
                nc.scalar.copy(wqk[0][:, n, :, :], wqk_whole[:, n, :, :]).then_inc(wqk_high_done, 1)
                if n == 0:
                    high_x(0, 0)
            act.wait_ge(wv_centred, 2)
            nc.scalar.copy(wv_p[0][:, :, :], wv_whole[:, :, :]).then_inc(wv_high_done, 1)
            all_tiles(act, tile)
            for n, (o, c) in enumerate(W3_GROUPS):
                act.wait_ge(w_turned, 1 + WG * TILES + n + 1)
                nc.scalar.copy(rounded["w3t"][:, c:c + 4, o * PARTS:(o + 1) * PARTS], w_ps[:, :, :]).then_inc(w_bank_free, 1)
                act.wait_ge(compared, UNITS * TILES + n + 1)
                nc.scalar.copy(short[n % 2][:, :], w_rows[0][:, n * UNIT:(n + 1) * UNIT]).then_inc(short_done, 1)
            act.wait_ge(lam_ready, 4)
            nc.scalar.activation(lam_exp[:, :, :], lam_sum[:, :, :], ACT.Exp).then_inc(exp_done, 1)

        @block.vector
        def _(dve):
            def compare(n, buf, whole, count):
                dve.wait_ge(short_done, n + 1)
                flags = short[buf][:, :].bitcast(F32)
                nc.vector.scalar_tensor_tensor(flags, flags, 1.0, whole, ALU.mult, ALU.not_equal, accum_out=count).then_inc(compared, 1)

            nc.vector.memset(biggest[:, :, :], 0.0).then_inc(biggest_done, 1)
            nc.vector.memset(smallest[:, :, :], 0.0).then_inc(biggest_done, 1)

            def low_x(t, u):
                for c in range(EC):
                    dve.wait_ge(xt_high, EC * t + c + 1)
                    nc.vector.tensor_tensor(xt[u][1][:, c, :], x_ps[c][:, :], xt[u][0][:, c, :].bitcast(F32), ALU.subtract).then_inc(xt_low, 1)

            def tile(t, u, r, more):
                for m in range(M_TILES):
                    n = M_TILES * t + m
                    which = m // EC // 2
                    p = parts[m % 4]
                    dve.wait_ge(high_ready, n + 1)
                    dve.wait_ge(parts_ready, n + 1)
                    nc.vector.tensor_tensor(resid[m % 2][:, :], qk_ps[m % 4][:, :], p[:, 0, :], ALU.subtract).then_inc(qk_bank_free, 1)
                    dve.wait_ge(biggest_done, 2 * n + 2)
                    nc.vector.tensor_tensor(biggest[:, which, :], biggest[:, which, :], p[:, 0, :], ALU.max).then_inc(biggest_done, 1)
                    nc.vector.tensor_tensor(smallest[:, which, :], smallest[:, which, :], p[:, 0, :], ALU.min).then_inc(biggest_done, 1)
                    if m in UNIT_AT:
                        k = UNIT_AT[m]
                        compare(UNITS * t + k, (UNITS * u + k) % 2, w_rows[u][:, k * UNIT:(k + 1) * UNIT], tile_counts[:, k, bass.ts(t, 1)])
                    if more and m == X_AT:
                        low_x(t + 1, 1 - u)

            for n in range(len(KINDS)):
                dve.wait_ge(wqk_high_done, n + 1)
                nc.vector.tensor_tensor(wqk[1][:, n, :, :], wqk_whole[:, n, :, :], wqk[0][:, n, :, :].bitcast(F32), ALU.subtract).then_inc(wqk_ready, 1)
                if n == 0:
                    low_x(0, 0)
            dve.wait_ge(wv_loaded, 16)
            nc.vector.tensor_reduce(wv_mean[:, :], wv_whole[:, :, :], AXIS.X, ALU.add).then_inc(wv_centred, 1)
            dve.wait_ge(wv_centred, 1)
            nc.vector.scalar_tensor_tensor(wv_whole[:, :, :], wv_mean[:, :].unsqueeze(2).to_broadcast([PARTS, EC * HEADS, VALUE_DIM]),
                                           -1.0 / VALUE_DIM, wv_whole[:, :, :], ALU.mult, ALU.add).then_inc(wv_centred, 1)
            dve.wait_ge(wv_high_done, 1)
            nc.vector.tensor_tensor(wv_p[1][:, :, :], wv_whole[:, :, :], wv_p[0][:, :, :].bitcast(F32), ALU.subtract).then_inc(wv_ready, 1)
            all_tiles(dve, tile)
            dve.wait_ge(lam_loaded, 16 * 4)
            for n in range(2):
                nc.vector.tensor_tensor(lam_sb[:, 2 * n, :], lam_sb[:, 2 * n, :], lam_sb[:, 2 * n + 1, :], ALU.mult).then_inc(lam_ready, 1)
            dve.wait_ge(lam_ready, 2)
            for n in range(2):
                nc.vector.tensor_reduce(lam_sum[:, n, :], lam_sb[:, 2 * n, :].rearrange("p (h d) -> p h d", h=HEADS), AXIS.X, ALU.add).then_inc(lam_ready, 1)
            dve.wait_ge(biggest_done, 2 + 2 * TILES * M_TILES)
            nc.vector.tensor_reduce(big_col[:, 0:2], biggest[:, :, :], AXIS.X, ALU.max).then_inc(flag_steps, 1)
            nc.vector.tensor_reduce(small_col[:, :], smallest[:, :, :], AXIS.X, ALU.min).then_inc(flag_steps, 1)
            dve.wait_ge(flag_steps, 2)
            nc.vector.scalar_tensor_tensor(big_col[:, 0:2], small_col[:, :], -1.0, big_col[:, 0:2], ALU.mult, ALU.max).then_inc(big_ready, 1)
            for n in range(W3_UNITS):
                compare(UNITS * TILES + n, n % 2, w_rows[0][:, n * UNIT:(n + 1) * UNIT], counts[:, UNITS * TILES + n:UNITS * TILES + n + 1])
            dve.wait_ge(compared, 2 + UNITS * TILES + W3_UNITS)
            nc.vector.tensor_reduce(big_col[:, 2:3], counts[:, :], AXIS.X, ALU.add).then_inc(big_ready, 1)
            dve.wait_ge(big_reduced, 1)
            bound = keep["bound"]
            nc.vector.tensor_tensor(bound[:, 0:1], big_all[:, 0:1], big_all[:, 1:2], ALU.mult).then_inc(flag_steps, 1)
            nc.vector.tensor_scalar(keep["wide"][:, :], big_all[:, 2:3], 0.0, None, ALU.is_gt).then_inc(flag_steps, 1)
            dve.wait_ge(flag_steps, 4)
            nc.vector.tensor_scalar(bound[:, 1:2], bound[:, 0:1], HEAD_DIM * BOUND_MARGIN, None, ALU.mult).then_inc(flag_steps, 1)
            dve.wait_ge(flag_steps, 5)
            nc.vector.tensor_scalar(keep["exact"][:, :], bound[:, 1:2], SAFE_BOUND / SCALE, None, ALU.is_gt).then_inc(flag_steps, 1)
            dve.wait_ge(flag_steps, 6)
            dve.wait_ge(exp_done, 1)
            nc.vector.scalar_tensor_tensor(keep["neg_lam"][:, :], lam_exp[:, 1, :], -LAM_INIT, lam_exp[:, 0, :], ALU.add, ALU.subtract)

        @block.tensor
        def _(pe):

            def turn_x(t, u, r):
                pe.wait_ge(x_loaded[u], 16 * r + 16)
                for c in range(EC):
                    for s in range(SUBS):
                        last = nc.tensor.transpose(x_ps[c][:, s * PARTS:(s + 1) * PARTS], x_sb[u][:, s, c * PARTS:(c + 1) * PARTS], ident[:, :])
                    last.then_inc(x_turned, 1)

            def tile(t, u, r, more):
                pe.wait_ge(xt_low, EC * t + EC)
                for m in range(M_TILES):
                    kind, o = divmod(m, EC)
                    if o == 0:
                        pe.wait_ge(wqk_ready, kind + 1)
                    pe.wait_ge(qk_bank_free, M_TILES * t + m + 1)
                    for c in range(EC):
                        for n, (a, b) in enumerate(PASSES):
                            last = nc.tensor.matmul(qk_ps[m % 4][:, :], wqk[a][:, kind, c, o * PARTS:(o + 1) * PARTS], xt[u][b][:, c, :],
                                                    start=(c == 0 and n == 0), stop=(c == EC - 1 and n == len(PASSES) - 1))
                    last.then_inc(qk_projected, 1)
                    if m in V_AT:
                        s = V_AT[m]
                        pe.wait_ge(wv_ready, 1)
                        pe.wait_ge(v_bank_free, SUBS * t + s + 1)
                        for c in range(EC):
                            for n, (a, b) in enumerate(PASSES):
                                last = nc.tensor.matmul(v_ps[:, :, :], xt[u][b][:, c, s * PARTS:(s + 1) * PARTS], wv_p[a][:, c * HEADS:(c + 1) * HEADS, :],
                                                        start=(c == 0 and n == 0), stop=(c == EC - 1 and n == len(PASSES) - 1))
                        last.then_inc(v_projected, 1)
                    if m in GROUP_AT:
                        g = GROUP_AT[m]
                        col, _, _, k = TURN_GROUPS[g]
                        pe.wait_ge(w_loaded[u], 64 * r + 64)
                        pe.wait_ge(w_bank_free, WG * t + g + 1)
                        for j in range(k):
                            last = nc.tensor.transpose(w_ps[:, j, :], w_rows[u][:, col + j * PARTS:col + (j + 1) * PARTS], ident[:, :])
                        last.then_inc(w_turned, 1)
                    if more and m == X_AT:
                        turn_x(t + 1, 1 - u, r + u)

            pe.wait_ge(ident_done, 2)
            turn_x(0, 0, 0)
            all_tiles(pe, tile)
            pe.wait_ge(w3_loaded, 16)
            for n, (o, c) in enumerate(W3_GROUPS):
                pe.wait_ge(w_bank_free, WG * TILES + n + 1)
                for k in range(4):
                    col = o * HIDDEN + (c + k) * PARTS
                    last = nc.tensor.transpose(w_ps[:, k, :], w_rows[0][:, col:col + PARTS], ident[:, :])
                last.then_inc(w_turned, 1)


STACK_RUNS = [(0, 3), (3, 2), (5, 1)]
STACK_DMAS = 2 * len(STACK_RUNS)
HEAD_LOADS = STACK_DMAS + 2


def load_stacks(dma, q, k, qk_parts, sem, head):
    for which, stack in enumerate((q, k)):
        for n, (place, places) in enumerate(STACK_RUNS):
            parts = slice(0, places) if which == 0 else slice(n, n + 1)
            for_both = qk_parts[which, parts, bass.ts(head, HEAD_DIM), :, :].rearrange("a r s n -> a r (s n)")
            if which == 1:
                for_both = for_both.to_broadcast([places, HEAD_DIM, 2 * TOKENS])
            dma(stack[place * HEAD_DIM:(place + places) * HEAD_DIM, :, :].rearrange("r s n -> r (s n)"), for_both).then_inc(sem, 16)


def head_buffers(room):
    return dict(
        q=[room.sb(f"q{u}", [STACK_ROWS, 2, TOKENS], BF16) for u in range(2)],
        k=[room.sb(f"k{u}", [STACK_ROWS, 2, TOKENS], BF16) for u in range(2)],
        v=[room.sb(f"v{u}", [PARTS, BLOCKS, VALUE_DIM]) for u in range(2)],
        loaded=[room.sem(f"loaded{u}") for u in range(2)],
    )


def load_head(dma, heads, qk_parts, values, h, u):
    load_stacks(dma, heads["q"][u][0:SCORE_ROWS, :, :], heads["k"][u][0:SCORE_ROWS, :, :], qk_parts, heads["loaded"][u], h)
    dma(heads["v"][u][:, :, :], values[h]).then_inc(heads["loaded"][u], 16)


def load_shift(dma, heads, shift, h, u):
    dma(heads["q"][u][SCORE_ROWS:STACK_ROWS, :, :], shift[:, h, :, :]).then_inc(heads["loaded"][u], 16)


def maximum_phase(nc, keep, heads, qk_parts, shift, values):
    CHUNKS = [(qb, s, c) for qb in range(KEY_BLOCKS) for s in range(2) for c in range(qb // SUBS + 1)]
    NCH = len(CHUNKS)
    BANKS = 4
    with Room(nc, "max") as room:
        q_sb = room.sb("q", [SCORE_ROWS, 2, TOKENS], BF16)
        k_sb = room.sb("k", [SCORE_ROWS, 2, TOKENS], BF16)
        future = room.sb("future", [PARTS, PARTS], BF16)
        ident_b = room.sb("ident_b", [PARTS, PARTS], BF16)
        chunk_max = room.sb("chunk_max", [PARTS, 2, KEY_BLOCKS, QUERY_TILES])
        row_max = room.sb("row_max", [PARTS, 2 * KEY_BLOCKS])
        neg = room.sb("neg", [2 * KEY_BLOCKS, PARTS])
        rest = room.sb("rest", [2 * KEY_BLOCKS, PARTS])
        neg_parts = room.sb("neg_parts", [2 * KEY_BLOCKS, 3, PARTS], BF16)
        fill = room.sb("fill", [PARTS, 2, HEADS * BATCH * 2 * SEQ // PARTS], BF16)
        s_ps = [room.ps(f"s_ps{n}", [PARTS, TILE]) for n in range(BANKS)]
        t_ps = room.ps("t_ps", [2 * KEY_BLOCKS, PARTS])

        const_done = room.sem("const_done")
        loaded = room.sem("loaded")
        scored = room.sem("scored")
        bank_free = room.sem("bank_free")
        reduced = room.sem("reduced")
        row_ready = room.sem("row_ready")
        transposed = room.sem("transposed")
        cut = room.sem("cut")
        stored = room.sem("stored")
        filled = room.sem("filled")
        fill_ready = room.sem("fill_ready")
        ones_done = room.sem("ones_done")
        ones_set = room.sem("ones_set")
        CUTS = 4
        STORES = 2 * 16

        give_credits(nc, [(bank_free, BANKS), (scored, 1), (cut, CUTS), (stored, STORES), (transposed, 1)])
        block = room.block()

        @block.scalar
        def _(act):
            load_head(act.dma_start, heads, qk_parts, values, 0, 0)

        @block.gpsimd
        def _(pool):
            pool.memset(heads["k"][1][SCORE_ROWS:STACK_ROWS, :, :], 1.0).then_inc(ones_done, 1)
            pool.wait_ge(ones_done, 1)
            exact = pool.value_load(keep["exact"][0:1, 0:1])
            with pool.If(exact != 0):
                pool.memset(future[:, :], 0.0).then_inc(const_done, 1)
                pool.memset(ident_b[:, :], 0.0).then_inc(const_done, 1)
                pool.wait_ge(const_done, 2)
                pool.affine_select(out=future[:, :], in_=future[:, :], compare_op=ALU.is_ge, fill=LOWEST, base=0,
                                   pattern=[[-1, PARTS]], channel_multiplier=1).then_inc(const_done, 1)
                pool.affine_select(out=ident_b[:, :], in_=ident_b[:, :], compare_op=ALU.not_equal, fill=1.0, base=0,
                                   pattern=[[-1, PARTS]], channel_multiplier=1).then_inc(const_done, 1)

        @block.sync
        def _(sp):
            exact = sp.value_load(keep["exact"][0:1, 0:1])
            with sp.If(exact != 0):
                with sp.Fori(0, HEADS) as h:
                    sp.wait_ge(scored, 1 + h * BATCH * NCH)
                    load_stacks(sp.dma_start, q_sb[:, :, :], k_sb[:, :, :], qk_parts, loaded, h)
                    for b in range(BATCH):
                        n = h * BATCH + b
                        sp.wait_ge(cut, CUTS * n + 2 * CUTS)
                        for s in range(2):
                            sp.dma_start(shift[:, h, s, b * SEQ:(b + 1) * SEQ].rearrange("a (r n) -> r a n", n=PARTS),
                                         neg_parts[s * KEY_BLOCKS:(s + 1) * KEY_BLOCKS, :, :]).then_inc(stored, 16)
                sp.wait_ge(stored, STORES + STORES * HEADS * BATCH)
            with sp.If(exact == 0):
                sp.wait_ge(fill_ready, 2)
                for a in range(SHIFT_ROWS):
                    sp.dma_start(shift[a].rearrange("h s n -> (h s n)").rearrange("(p n) -> p n", p=PARTS),
                                 fill[:, min(a, 1), :]).then_inc(filled, 16)
                sp.wait_ge(filled, 16 * SHIFT_ROWS)

        @block.tensor
        def _(pe):
            exact = pe.value_load(keep["exact"][0:1, 0:1])
            with pe.If(exact != 0):
                pe.wait_ge(const_done, 4)
                with pe.Fori(0, HEADS) as h:
                    pe.wait_ge(loaded, 16 * STACK_DMAS * h + 16 * STACK_DMAS)
                    for b in range(BATCH):
                        n = h * BATCH + b
                        for m, (qb, s, c) in enumerate(CHUNKS):
                            cols = min(TILE, (qb + 1) * PARTS - c * TILE)
                            bank = s_ps[m % BANKS]
                            on_diagonal = c == qb // SUBS
                            pe.wait_ge(bank_free, n * NCH + m + 1)
                            last = nc.tensor.matmul(bank[:, 0:cols], q_sb[:, s, b * SEQ + qb * PARTS:b * SEQ + (qb + 1) * PARTS],
                                                    k_sb[:, s, b * SEQ + c * TILE:b * SEQ + c * TILE + cols], start=True, stop=not on_diagonal)
                            if on_diagonal:
                                last = nc.tensor.matmul(bank[:, cols - PARTS:cols], ident_b[:, :], future[:, :], start=False, stop=True)
                            last.then_inc(scored, 1)
                        pe.wait_ge(row_ready, n + 1)
                        pe.wait_ge(cut, CUTS * n + CUTS)
                        nc.tensor.transpose(t_ps[:, :], row_max[:, :], keep["ident"][:, :]).then_inc(transposed, 1)

        @block.vector
        def _(dve):
            exact = dve.value_load(keep["exact"][0:1, 0:1])
            with dve.If(exact != 0):
                nc.vector.memset(chunk_max[:, :, :, :], LOWEST).then_inc(reduced, 1)
                dve.wait_ge(reduced, 1)
                with dve.Fori(0, HEADS) as h:
                    for b in range(BATCH):
                        n = h * BATCH + b
                        for m, (qb, s, c) in enumerate(CHUNKS):
                            cols = min(TILE, (qb + 1) * PARTS - c * TILE)
                            dve.wait_ge(scored, 1 + n * NCH + m + 1)
                            nc.vector.tensor_reduce(chunk_max[:, s, qb, c:c + 1], s_ps[m % BANKS][:, 0:cols], AXIS.X, ALU.max).then_inc(bank_free, 1)
                        dve.wait_ge(bank_free, BANKS + n * NCH + NCH)
                        dve.wait_ge(transposed, n + 1)
                        nc.vector.tensor_reduce(row_max[:, :].rearrange("p (s q) -> p s q", s=2), chunk_max[:, :, :, :], AXIS.X, ALU.max).then_inc(row_ready, 1)
                        dve.wait_ge(transposed, n + 2)
                        dve.wait_ge(stored, STORES * n + STORES)
                        nc.vector.tensor_scalar(neg[:, :], t_ps[:, :], -1.0, None, ALU.mult).then_inc(cut, 1)
                        dve.wait_ge(cut, CUTS * n + CUTS + 1)
                        nc.vector.tensor_copy(neg_parts[:, 0, :], neg[:, :]).then_inc(cut, 1)
                        dve.wait_ge(cut, CUTS * n + CUTS + 2)
                        nc.vector.tensor_tensor(rest[:, :], neg[:, :], neg_parts[:, 0, :], ALU.subtract).then_inc(reduced, 1)
                        dve.wait_ge(reduced, 1 + n + 1)
                        nc.vector.tensor_copy(neg_parts[:, 1, :], rest[:, :]).then_inc(cut, 1)
                        dve.wait_ge(cut, CUTS * n + CUTS + 3)
                        nc.vector.tensor_tensor(neg_parts[:, 2, :], rest[:, :], neg_parts[:, 1, :], ALU.subtract).then_inc(cut, 1)
            with dve.If(exact == 0):
                nc.vector.memset(fill[:, :, :], 0.0).then_inc(fill_ready, 1)
                dve.wait_ge(fill_ready, 1)
                nc.vector.tensor_scalar(fill[:, 0, :], fill[:, 1, :], keep["bound"][:, 1:2], -1.0, ALU.add, ALU.mult).then_inc(fill_ready, 1)
            nc.vector.memset(heads["k"][0][SCORE_ROWS:STACK_ROWS, :, :], 1.0).then_inc(ones_set, 1)


def attention_phase(nc, keep, heads, qk_parts, shift, values, diffs):
    STEPS = [(0, j) for j in (0, 2, 3, 1)]
    for t in range(1, QUERY_TILES):
        third = SUBS * t // 3
        order = list(range(SUBS * t)) + [SUBS * t, SUBS * t + 3]
        order.insert(2 * third + SUBS * t % 3 // 2, SUBS * t + 1)
        order.insert(third, SUBS * t + 2)
        STEPS += [(t, j) for j in order]
    END = [max(k for k, (t, _) in enumerate(STEPS) if t == tile) for tile in range(QUERY_TILES)]
    UNITS = []
    for k, (t, j) in enumerate(STEPS):
        UNITS += [(k, [0, 1])] if j - SUBS * t >= SUBS // 2 else [(k, [0]), (k, [1])]
    NU = len(UNITS)
    LAST_UNIT = [max(n for n, (step, _) in enumerate(UNITS) if step == k) for k in range(len(STEPS))]
    LAG = 3
    TURN_LAG = 2
    MASKS = [sum(j >= SUBS * t for t, j in STEPS[:k + 1]) for k in range(len(STEPS))]
    NS = len(STEPS)
    NT = QUERY_TILES
    SLOTS = 3
    PROBS = 4
    D = VALUE_DIM
    VEC = 6
    LAST = HEADS - 1

    def window(t, j):
        return max(0, j - SUBS * t) * PARTS

    with Room(nc, "attn") as room:
        q_sb, k_sb, v_sb, loaded = (heads[name] for name in ("q", "k", "v", "loaded"))
        probs = [room.sb(f"probs{n}", [PARTS, BATCH, 2, TILE]) for n in range(PROBS)]
        sums_sb = room.sb("sums_sb", [PARTS, TILE])
        raw = room.sb("raw", [PARTS, SUBS * BATCH, 2, D])
        recip = room.sb("recip", [PARTS, SUBS * BATCH, 2])
        first = room.sb("first", [PARTS, SUBS * BATCH, D - 1])
        second = room.sb("second", [PARTS, SUBS * BATCH, D - 1])
        total = room.sb("total", [PARTS, SUBS * BATCH])
        diff = room.sb("diff", [PARTS, KEY_BLOCKS * BATCH, D])
        s_ps = [room.ps(f"s_ps{n}", [PARTS, 2, TILE]) for n in range(SLOTS)]
        sums_ps = [room.ps(f"sums_ps{n}", [PARTS, TILE]) for n in range(2)]

        scored = room.sem("scored")
        exp_done = room.sem("exp_done")
        mask_begun = room.sem("mask_begun")
        masked = room.sem("masked")
        probs_free = room.sem("probs_free")
        sums_copied = room.sem("sums_copied")
        turned = room.sem("turned")
        sums_bank_free = room.sem("sums_bank_free")
        vec = room.sem("vec")
        diff_ready = room.sem("diff_ready")
        stored = room.sem("stored")
        STORES = 16 * BATCH

        give_credits(nc, [(probs_free, PROBS), (sums_bank_free, 2), (turned, 1), (stored, STORES)])
        block = room.block()

        def all_heads(eng, head):
            head(0, 0, 0, True, False)
            with eng.Fori(0, (HEADS - 2) // 2) as i:
                head(2 * i + 1, 1, i, False, False)
                head(2 * i + 2, 0, i + 1, False, False)
            head(LAST, LAST % 2, LAST // 2, False, True)

        @block.sync
        def _(sp):
            def head(h, u, r, first, last):
                if not last:
                    sp.wait_ge(probs_free, PROBS + NS * h)
                    load_head(sp.dma_start, heads, qk_parts, values, h + 1, 1 - u)
                    load_shift(sp.dma_start, heads, shift, h + 1, 1 - u)
                sp.wait_ge(diff_ready, NT * h + NT)
                for b in range(BATCH):
                    sp.dma_start(diffs[b * KEY_BLOCKS:(b + 1) * KEY_BLOCKS, :, h, :].rearrange("k p n -> p k n"),
                                 diff[:, :, :].rearrange("p (k b) n -> p k b n", b=BATCH)[:, :, b, :]).then_inc(stored, 16)

            load_shift(sp.dma_start, heads, shift, 0, 0)
            all_heads(sp, head)
            sp.wait_ge(stored, STORES + STORES * HEADS)

        @block.gpsimd
        def _(pool):
            with pool.Fori(0, HEADS) as h:
                for k, (t, j) in enumerate(STEPS):
                    if j < SUBS * t:
                        continue
                    off = window(t, j)
                    pool.wait_ge(exp_done, NU * h + LAST_UNIT[k] + 1)
                    pool.sem_inc(mask_begun, 1)
                    corner = probs[k % PROBS][:, :, :, off:off + PARTS].rearrange("p b s n -> p (b s) n")
                    pool.affine_select(out=corner, in_=corner, compare_op=ALU.is_ge, fill=0.0, base=0,
                                       pattern=[[0, 2 * BATCH], [1, PARTS]], channel_multiplier=-1).then_inc(masked, 1)

        @block.scalar
        def _(act):
            with act.Fori(0, HEADS) as h:
                for n, (k, batches) in enumerate(UNITS):
                    t, j = STEPS[k]
                    off = window(t, j)
                    width = TILE - off
                    if batches[0] == 0:
                        act.wait_ge(probs_free, NS * h + k + 1)
                    act.wait_ge(scored, NU * h + n + 1)
                    weights = probs[k % PROBS][:, batches[0]:batches[-1] + 1, :, off:TILE].rearrange("p b s n -> p s b n")
                    side_by_side = s_ps[n % SLOTS][:, :, 0:len(batches) * width].rearrange("p s (b n) -> p s b n", n=width)
                    nc.scalar.activation(weights, side_by_side, ACT.Exp, scale=SCALE).then_inc(exp_done, 1)

        @block.tensor
        def _(pe):
            def scores(h, u, r, first, n):
                k, batches = UNITS[n]
                t, j = STEPS[k]
                off = window(t, j)
                width = TILE - off
                if n == 0:
                    pe.wait_ge(loaded[u], 16 * HEAD_LOADS * r + 16 * HEAD_LOADS)
                if not first or n >= SLOTS:
                    pe.wait_ge(exp_done, NU * h + n - SLOTS + 1)
                for place, b in enumerate(batches):
                    for s in range(2):
                        last = nc.tensor.matmul(s_ps[n % SLOTS][:, s, place * width:(place + 1) * width],
                                                k_sb[u][:, s, b * SEQ + j * PARTS:b * SEQ + (j + 1) * PARTS],
                                                q_sb[u][:, s, b * SEQ + t * TILE + off:b * SEQ + (t + 1) * TILE], start=True, stop=True)
                last.then_inc(scored, 1)

            def weigh(h, u, k):
                t, j = STEPS[k]
                off = window(t, j)
                sums = sums_ps[t % 2]
                pe.wait_ge(exp_done, NU * h + LAST_UNIT[k] + 1)
                if j >= SUBS * t:
                    pe.wait_ge(masked, SUBS * NT * h + MASKS[k])
                if j == 0:
                    pe.wait_ge(sums_bank_free, NT * h + t + 1)
                for b in range(BATCH):
                    for s in range(2):
                        c = 2 * b + s
                        last = nc.tensor.matmul(sums[c * D:(c + 1) * D, off:TILE], v_sb[u][:, b * KEY_BLOCKS + j, :], probs[k % PROBS][:, b, s, off:TILE],
                                                start=(j == 0), stop=(k == END[t]))
                last.then_inc(probs_free, 1)

            def turn(h, t):
                pe.wait_ge(sums_copied, NT * h + t + 1)
                for i in range(SUBS):
                    last = nc.tensor.transpose(sums_ps[t % 2][:, i * PARTS:(i + 1) * PARTS], sums_sb[:, i * PARTS:(i + 1) * PARTS], keep["ident"][:, :])
                last.then_inc(turned, 1)

            def use(h, u, first, k):
                if k < 0:
                    if first:
                        return
                    h, u, k = h - 1, 1 - u, k + NS
                weigh(h, u, k)
                if k - TURN_LAG in END:
                    turn(h, END.index(k - TURN_LAG))
                elif k - TURN_LAG + NS in END and not first:
                    turn(h - 1, END.index(k - TURN_LAG + NS))

            def head(h, u, r, first, last):
                for k in range(NS):
                    for n, (step, _) in enumerate(UNITS):
                        if step == k:
                            scores(h, u, r, first, n)
                    use(h, u, first, k - LAG)
                if last:
                    for k in range(NS - LAG, NS):
                        use(h, u, first, k)
                    turn(h, QUERY_TILES - 1)

            all_heads(pe, head)

        @block.vector
        def _(dve):
            def tile(h, t):
                n = NT * h + t
                bank = sums_ps[t % 2]
                dve.wait_ge(probs_free, PROBS + NS * h + END[t] + 1)
                dve.wait_ge(turned, n + 1)
                nc.vector.tensor_copy(sums_sb[:, :], bank[:, :]).then_inc(sums_copied, 1)
                dve.wait_ge(turned, n + 2)
                nc.vector.tensor_copy(raw[:, :, :, :].rearrange("p k s d -> p (k s d)"), bank[:, :]).then_inc(sums_bank_free, 1)
                v0 = VEC * n
                rows = diff[:, SUBS * BATCH * t:SUBS * BATCH * (t + 1), :]
                wide = [PARTS, SUBS * BATCH, D - 1]
                dve.wait_ge(sums_bank_free, 2 + n + 1)
                nc.vector.reciprocal(recip[:, :, :], raw[:, :, :, D - 1]).then_inc(vec, 1)
                dve.wait_ge(vec, v0 + 1)
                nc.vector.tensor_tensor(first[:, :, :], raw[:, :, 0, 0:D - 1], recip[:, :, 0:1].to_broadcast(wide), ALU.mult).then_inc(vec, 1)
                nc.vector.tensor_tensor(second[:, :, :], raw[:, :, 1, 0:D - 1], recip[:, :, 1:2].to_broadcast(wide), ALU.mult).then_inc(vec, 1)
                dve.wait_ge(vec, v0 + 3)
                dve.wait_ge(stored, STORES * h + STORES)
                nc.vector.scalar_tensor_tensor(rows[:, :, 0:D - 1], second[:, :, :], keep["neg_lam"][:, bass.ts(h, 1)], first[:, :, :], ALU.mult, ALU.add).then_inc(vec, 1)
                dve.wait_ge(vec, v0 + 4)
                nc.vector.tensor_reduce(total[:, :], rows[:, :, 0:D - 1], AXIS.X, ALU.add).then_inc(vec, 1)
                dve.wait_ge(vec, v0 + 5)
                nc.vector.tensor_scalar(rows[:, :, D - 1], total[:, :], -1.0, None, ALU.mult).then_inc(vec, 1)
                dve.wait_ge(vec, v0 + 6)
                dve.sem_inc(diff_ready, 1)

            with dve.Fori(0, HEADS) as h:
                for t in range(QUERY_TILES):
                    tile(h, t)


def turn_weights_phase(nc, keep, ffn_w, whole_w):
    w1, w2, h1, h2, w3 = ffn_w
    G, W0 = len(TURN_GROUPS), len(W3_GROUPS)
    with Room(nc, "wide") as room:
        w_rows = [room.sb(f"w_rows{u}", [PARTS, ROW_COLS]) for u in range(2)]
        w3_rows = room.sb("w3_rows", [PARTS, EC * HIDDEN])
        turn_ps = [room.ps(f"turn_ps{n}", [PARTS, 4, PARTS]) for n in range(2)]
        w3_loaded = room.sem("w3_loaded")
        w_loaded = [room.sem(f"w_loaded{u}") for u in range(2)]
        turned = room.sem("turned")
        turn_bank_free = room.sem("turn_bank_free")
        give_credits(nc, [(turn_bank_free, 2)])
        block = room.block()

        @block.sync
        def _(sp):
            def load(t, u):
                col = 0
                for w in (w1, w2, h1, h2):
                    n = w.shape[1]
                    sp.dma_start(w_rows[u][:, col:col + n], w[bass.ts(t, PARTS), :]).then_inc(w_loaded[u], 16)
                    col += n

            wide = sp.value_load(keep["wide"][0:1, 0:1])
            with sp.If(wide != 0):
                sp.dma_start(w3_rows[:, :].rearrange("p (o i) -> p o i", o=EC), w3.rearrange("(o p) i -> p o i", p=PARTS)).then_inc(w3_loaded, 16)
                for u in range(2):
                    load(u, u)
                with sp.Fori(0, HC // 2 - 1) as i:
                    for u in range(2):
                        sp.wait_ge(turned, W0 + G * (2 * i + u) + G)
                        load(2 * i + u + 2, u)

        @block.tensor
        def _(pe):
            wide = pe.value_load(keep["wide"][0:1, 0:1])
            with pe.If(wide != 0):
                pe.wait_ge(w3_loaded, 16)
                for n, (o, c) in enumerate(W3_GROUPS):
                    pe.wait_ge(turn_bank_free, n + 1)
                    for k in range(4):
                        col = o * HIDDEN + (c + k) * PARTS
                        last = nc.tensor.transpose(turn_ps[n % 2][:, k, :], w3_rows[:, col:col + PARTS], keep["ident"][:, :])
                    last.then_inc(turned, 1)
                with pe.Fori(0, HC // 2) as i:
                    for u in range(2):
                        pe.wait_ge(w_loaded[u], 64 * i + 64)
                        for g, (col, _, _, n) in enumerate(TURN_GROUPS):
                            pe.wait_ge(turn_bank_free, W0 + G * (2 * i + u) + g + 1)
                            for k in range(n):
                                last = nc.tensor.transpose(turn_ps[g % 2][:, k, :], w_rows[u][:, col + k * PARTS:col + (k + 1) * PARTS], keep["ident"][:, :])
                            last.then_inc(turned, 1)

        @block.scalar
        def _(act):
            wide = act.value_load(keep["wide"][0:1, 0:1])
            with act.If(wide != 0):
                for n, (o, c) in enumerate(W3_GROUPS):
                    act.wait_ge(turned, n + 1)
                    nc.scalar.copy(whole_w["w3t"][:, c:c + 4, o * PARTS:(o + 1) * PARTS], turn_ps[n % 2][:, :, :]).then_inc(turn_bank_free, 1)
                with act.Fori(0, HC) as t:
                    for g, (_, name, c, n) in enumerate(TURN_GROUPS):
                        act.wait_ge(turned, W0 + G * t + g + 1)
                        nc.scalar.copy(whole_w[name][:, c:c + n, bass.ts(t, PARTS)], turn_ps[g % 2][:, 0:n, :]).then_inc(turn_bank_free, 1)


def finish_sems(nc, room):
    wo_loaded = room.sem("wo_loaded")
    heads_loaded = room.sem("heads_loaded")
    x_loaded = [room.sem(f"x_loaded{u}") for u in range(2)]
    squared = room.sem("squared")
    summed = room.sem("summed")
    head_vec = room.sem("head_vec")
    head_var_ready = room.sem("head_var_ready")
    head_root_ready = room.sem("head_root_ready")
    normed_ready = room.sem("normed_ready")
    normed_turned = room.sem("normed_turned")
    normed_copied = room.sem("normed_copied")
    normed_low = room.sem("normed_low")
    wo_high = room.sem("wo_high")
    wo_low = room.sem("wo_low")
    projected = room.sem("projected")
    mid_added = room.sem("mid_added")
    y_added = room.sem("y_added")
    norm_sems = {which: dict(
        vec=room.sem(f"{which}_vec"), aggr_begun=room.sem(f"{which}_aggr_begun"), var_ready=room.sem(f"{which}_var_ready"),
        root_ready=room.sem(f"{which}_root_ready"), ready=room.sem(f"{which}_ready"),
    ) for which in ("mid", "y")}
    mid_turned = room.sem("mid_turned")
    xt_high = room.sem("xt_high")
    xt_ready = room.sem("xt_ready")
    up_projected = room.sem("up_projected")
    gate_ready = room.sem("gate_ready")
    gated = room.sem("gated")
    gated_high = room.sem("gated_high")
    gated_low = room.sem("gated_low")
    hid_projected = room.sem("hid_projected")
    gelu_done = room.sem("gelu_done")
    hid_high = room.sem("hid_high")
    hid_low = room.sem("hid_low")
    y_projected = room.sem("y_projected")
    y_free = room.sem("y_free")
    stored = room.sem("stored")
    give_credits(nc, [(summed, 2), (xt_ready, EC), (gelu_done, LAYERS), (hid_low, LAYERS), (y_free, 2 * SUBS), (stored, 16)])
    return (wo_loaded, heads_loaded, x_loaded, squared, summed, head_vec, head_var_ready, head_root_ready, normed_ready, normed_turned,
            normed_copied, normed_low, wo_high, wo_low, projected, mid_added, y_added, norm_sems, mid_turned, xt_high, xt_ready, up_projected, gate_ready, gated,
            gated_high, gated_low, hid_projected, gelu_done, hid_high, hid_low, y_projected, y_free, stored)


def finish_phase(nc, keep, sems, phase, split, weights, x, wo, diffs, out):
    x_v = x.rearrange("b (t s p) e -> (b t) p s e", s=SUBS, p=PARTS)
    out_v = out.rearrange("b (t s p) e -> (b t) p s e", s=SUBS, p=PARTS)
    d_v = diffs.rearrange("(t s) p h d -> t p s (h d)", s=SUBS)
    D = VALUE_DIM
    HALF = SUBS // 2
    CUTS = 2 if split else 1
    part_type = F32R if split else F32
    PASSES = [(0, 0), (1, 0), (0, 1)] if split else [(0, 0)]
    with Room(nc, phase) as room:
        wo_p = [room.sb(f"wo{k}", [PARTS, VC, EMBED], part_type) for k in range(CUTS)]
        heads_sb = room.sb("heads", [PARTS, SUBS, HEADS * D])
        square = [room.sb(f"square{n}", [PARTS, HEADS, D]) for n in range(2)]
        head_var = room.sb("head_var", [PARTS, SUBS * HEADS])
        head_root = room.sb("head_root", [PARTS, SUBS * HEADS])
        head_quotient = room.sb("head_quotient", [PARTS, SUBS * HEADS])
        head_rstd = room.sb("head_rstd", [PARTS, SUBS * HEADS])
        normed_t = [room.sb(f"normed_t{k}", [PARTS, VC * PARTS], part_type) for k in range(CUTS)]
        mid = [room.sb(f"mid{u}", [PARTS, SUBS, EMBED]) for u in range(2)]
        xt = [room.sb(f"xt{k}", [PARTS, EC, TILE], part_type) for k in range(CUTS)]
        gate = [room.sb(f"gate{n}", [PARTS, TILE]) for n in range(2)]
        whole = [room.sb(f"whole{n}", [PARTS, TILE]) for n in range(2 * CUTS - 2)]
        hid_a = [room.sb(f"hid_a{k}", [PARTS, HC, TILE], part_type) for k in range(CUTS)]
        hid_b = [room.sb(f"hid_b{k}", [PARTS, HC, TILE], part_type) for k in range(CUTS)]
        y = room.sb("y", [PARTS, SUBS, EMBED])
        norm_bufs = {which: dict(
            stats=room.sb(f"{which}_stats", [PARTS, SUBS, 6]), mean_var=room.sb(f"{which}_mean_var", [PARTS, SUBS, 2]),
            var=room.sb(f"{which}_var", [PARTS, SUBS]), root=room.sb(f"{which}_root", [PARTS, SUBS]),
            quotient=room.sb(f"{which}_quotient", [PARTS, SUBS]), rstd=room.sb(f"{which}_rstd", [PARTS, SUBS]),
        ) for which in ("mid", "y")}
        hid_ps = [room.ps(f"hid_ps{n}", [PARTS, TILE]) for n in range(4)]
        y_ps = [room.ps(f"y_ps{n}", [PARTS, HALF, EMBED]) for n in range(2)]
        turn_ps = [room.ps(f"turn_ps{n}", [PARTS, TILE]) for n in range(2)]

        (wo_loaded, heads_loaded, x_loaded, squared, summed, head_vec, head_var_ready, head_root_ready, normed_ready, normed_turned,
         normed_copied, normed_low, wo_high, wo_low, projected, mid_added, y_added, norm_sems, mid_turned, xt_high, xt_ready, up_projected, gate_ready, gated,
         gated_high, gated_low, hid_projected, gelu_done, hid_high, hid_low, y_projected, y_free, stored) = sems
        normed_cut = normed_low if split else normed_copied
        gated_ready = gated_low if split else gated
        hid_ready = hid_low if split else gelu_done
        block = room.block()
        LAST = TILES - 1

        def all_tiles(eng, begin, tile, end):
            wide = eng.value_load(keep["wide"][0:1, 0:1])
            with eng.If(wide == 0 if split else wide != 0):
                begin()
                tile(0, 0, 0, False, True)
                with eng.Fori(0, (TILES - 2) // 2) as i:
                    tile(2 * i + 1, 1, i, True, True)
                    tile(2 * i + 2, 0, i + 1, True, True)
                tile(LAST, LAST % 2, LAST // 2, True, False)
                end()

        @block.sync
        def _(sp):
            def load_heads(n):
                sp.dma_start(heads_sb[:, :, :], d_v[n]).then_inc(heads_loaded, 16)

            def load_x(n, u):
                sp.dma_start(mid[u][:, :, :], x_v[n]).then_inc(x_loaded[u], 16)

            def store(t):
                sp.wait_ge(norm_sems["y"]["ready"], SUBS * t + SUBS)
                sp.dma_start(out_v[t], y[:, :, :]).then_inc(stored, 16)

            def begin():
                load_heads(0)
                load_x(0, 0)
                sp.dma_start(y[:, :, :] if split else wo_p[0][:, :, :], wo.rearrange("(c p) n -> p c n", p=PARTS)).then_inc(wo_loaded, 16)
                load_x(1, 1)

            def tile(t, u, r, prior, more):
                if more:
                    sp.wait_ge(normed_turned, SUBS * t + SUBS)
                    load_heads(t + 1)
                if prior:
                    if more:
                        sp.wait_ge(y_added, SUBS * t)
                        load_x(t + 1, 1 - u)
                    store(t - 1)

            def end():
                store(LAST)
                sp.wait_ge(stored, 16 + 16 * TILES)

            all_tiles(sp, begin, tile, end)

        @block.gpsimd
        def _(pool):
            def squares(n):
                pool.wait_ge(heads_loaded, 16 * n + 16)
                for s in range(SUBS):
                    pool.wait_ge(summed, SUBS * n + s + 1)
                    heads = heads_sb[:, s, :].rearrange("p (h d) -> p h d", d=D)
                    pool.tensor_tensor(square[s % 2][:, :, :], heads, heads, ALU.mult).then_inc(squared, 1)

            def tile(t, u, r, prior, more):
                if more:
                    squares(t + 1)

            all_tiles(pool, lambda: None, tile, lambda: None)

        @block.tensor
        def _(pe):
            ident = keep["ident"]

            def turn_heads(n, s):
                pe.wait_ge(normed_ready, SUBS * n + s + 1)
                if s == 0:
                    pe.wait_ge(xt_ready, EC * n + EC)
                if s >= 2:
                    pe.wait_ge(normed_cut, SUBS * n + s - 1)
                for c in range(VC):
                    last = nc.tensor.transpose(turn_ps[s % 2][:, c * PARTS:(c + 1) * PARTS], heads_sb[:, s, c * PARTS:(c + 1) * PARTS], ident[:, :])
                last.then_inc(normed_turned, 1)

            def project(n, s):
                pe.wait_ge(normed_cut, SUBS * n + s + 1)
                if s == 0:
                    pe.wait_ge(y_free, SUBS * n + SUBS)
                for c in range(VC):
                    for k, (a, b) in enumerate(PASSES):
                        last = nc.tensor.matmul(y_ps[s // HALF][:, s % HALF, :], normed_t[a][:, c * PARTS:(c + 1) * PARTS], wo_p[b][:, c, :],
                                                start=(c == 0 and k == 0), stop=(c == VC - 1 and k == len(PASSES) - 1))
                last.then_inc(projected, 1)

            def turn_mid(n, u):
                pe.wait_ge(norm_sems["mid"]["ready"], SUBS * n + SUBS)
                for c in range(EC):
                    for s in range(SUBS):
                        last = nc.tensor.transpose(turn_ps[c][:, s * PARTS:(s + 1) * PARTS], mid[u][:, s, c * PARTS:(c + 1) * PARTS], ident[:, :])
                    last.then_inc(mid_turned, 1)

            def begin():
                if split:
                    pe.wait_ge(wo_low, 1)
                else:
                    pe.wait_ge(wo_loaded, 16)
                for s in range(SUBS + 1):
                    if s < SUBS:
                        turn_heads(0, s)
                    if s > 0:
                        project(0, s - 1)
                turn_mid(0, 0)

            BETWEEN = {(0, 5): [(turn_heads, 0)], (0, 6): [(turn_heads, 1)], (0, 7): [(project, 0), (turn_heads, 2)],
                       (1, 0): [(project, 1), (turn_heads, 3)], (1, 1): [(project, 2)], (1, 2): [(project, 3)]}

            def tile(t, u, r, prior, more):
                pe.wait_ge(xt_ready, EC * t + 2 * EC)
                for m in range(HC):
                    pair = hid_ps[2 * (m % 2):2 * (m % 2) + 2]
                    if m < 2:
                        pe.wait_ge(gelu_done, LAYERS * t + LAYERS - 2 + 2 * m)
                    else:
                        pe.wait_ge(gated, HC * t + m - 1)
                    for w, bank in zip(("w1t", "w2t"), pair):
                        for c in range(EC):
                            for k in range(CUTS):
                                last = nc.tensor.matmul(bank[:, :], weights[w][:, c, m * PARTS:(m + 1) * PARTS], xt[k][:, c, :],
                                                        start=(c == 0 and k == 0), stop=(c == EC - 1 and k == CUTS - 1))
                    last.then_inc(up_projected, 1)
                for layer, (w, hid, ready, first) in enumerate([("h1t", hid_a, gated_ready, HC * t), ("h2t", hid_b, hid_ready, LAYERS * t + LAYERS)]):
                    for m in range(HC):
                        n = layer * HC + m
                        if n < 4:
                            pe.wait_ge(gated, HC * t + HC - 1 + n // 2)
                        else:
                            pe.wait_ge(gelu_done, LAYERS * t + LAYERS + n - 3)
                        for c in range(HC):
                            if m == 0:
                                pe.wait_ge(ready, first + c + 1)
                            for k in range(CUTS):
                                last = nc.tensor.matmul(hid_ps[m % 4][:, :], weights[w][:, c, m * PARTS:(m + 1) * PARTS], hid[k][:, c, :],
                                                        start=(c == 0 and k == 0), stop=(c == HC - 1 and k == CUTS - 1))
                        last.then_inc(hid_projected, 1)
                        if more:
                            for step, s in BETWEEN.get((layer, m), []):
                                step(t + 1, s)
                            if (layer, m) == (1, 6):
                                turn_mid(t + 1, 1 - u)
                for s, chunks in [(0, range(HC - 1)), (1, range(HC - 1)), (0, [HC - 1]), (1, [HC - 1]), (2, range(HC)), (3, range(HC))]:
                    if 0 in chunks:
                        pe.wait_ge(y_free, SUBS * t + 2 * SUBS + max(0, s - 1))
                    for c in chunks:
                        if s == 0:
                            pe.wait_ge(hid_ready, LAYERS * t + LAYERS + HC + c + 1)
                        for k in range(CUTS):
                            last = nc.tensor.matmul(y_ps[s % 2][:, s // 2, :], hid_a[k][:, c, s * PARTS:(s + 1) * PARTS], weights["w3t"][:, c, :],
                                                    start=(c == 0 and k == 0), stop=(c == HC - 1 and k == CUTS - 1))
                    if HC - 1 in chunks:
                        last.then_inc(y_projected, 1)

            all_tiles(pe, begin, tile, lambda: None)

        @block.scalar
        def _(act):
            def head_root_of(n):
                act.wait_ge(head_var_ready, n + 1)
                nc.scalar.activation(head_root[:, :], head_var[:, :], ACT.Sqrt).then_inc(head_root_ready, 1)

            def norm_root_of(which, n):
                act.wait_ge(norm_sems[which]["var_ready"], n + 1)
                nc.scalar.activation(norm_bufs[which]["root"][:, :], norm_bufs[which]["var"][:, :], ACT.Sqrt).then_inc(norm_sems[which]["root_ready"], 1)

            def copy_heads(n, s):
                act.wait_ge(normed_turned, SUBS * n + s + 1)
                if s > 0:
                    act.wait_ge(projected, SUBS * n + s)
                nc.scalar.copy(normed_t[0][:, :], turn_ps[s % 2][:, :]).then_inc(normed_copied, 1)

            def high_xt(n):
                for c in range(EC):
                    act.wait_ge(mid_turned, EC * n + c + 1)
                    nc.scalar.copy(xt[0][:, c, :], turn_ps[c][:, :]).then_inc(xt_high if split else xt_ready, 1)

            def begin():
                act.wait_ge(heads_loaded, 16)
                for s in range(SUBS):
                    act.wait_ge(summed, s + 1)
                    nc.scalar.activation(square[s % 2][:, :, :].rearrange("p h d -> p (h d)"), heads_sb[:, s, :], ACT.Square).then_inc(squared, 1)
                if split:
                    act.wait_ge(wo_loaded, 16)
                    nc.scalar.copy(wo_p[0][:, :, :], y[:, :, :]).then_inc(wo_high, 1)
                head_root_of(0)
                for s in range(SUBS):
                    copy_heads(0, s)
                norm_root_of("mid", 0)
                high_xt(0)

            BETWEEN = {(0, 6): 0, (0, 7): 1, (1, 0): 2, (1, 1): 3}

            def tile(t, u, r, prior, more):
                for m in range(HC + 1):
                    n = HC * t + m
                    if m < HC:
                        act.wait_ge(up_projected, n + 1)
                        if m >= 2:
                            act.wait_ge(gated, n - 1)
                        nc.scalar.activation(gate[m % 2][:, :], hid_ps[2 * (m % 2)][:, :], ACT.Silu, scale=keep["s1"][:, m:m + 1]).then_inc(gate_ready, 1)
                    if m > 0 and split:
                        act.wait_ge(gated, n)
                        nc.scalar.copy(hid_a[0][:, m - 1, :], whole[(m - 1) % 2][:, :]).then_inc(gated_high, 1)
                for layer, (hid, s) in enumerate([(hid_b, "hs1"), (hid_a, "hs2")]):
                    for m in range(HC):
                        n = layer * HC + m
                        act.wait_ge(hid_projected, LAYERS * t + n + 1)
                        if split:
                            if n < 2:
                                act.wait_ge(gated_low, HC * t + HC - 1 + n)
                            else:
                                act.wait_ge(hid_low, LAYERS * t + LAYERS + n - 1)
                        gelu = whole[m % 2][:, :] if split else hid[0][:, m, :]
                        nc.scalar.activation(gelu, hid_ps[m % 4][:, :], ACT.Gelu, scale=keep[s][:, m:m + 1]).then_inc(gelu_done, 1)
                        if split:
                            act.wait_ge(gelu_done, LAYERS * t + LAYERS + n + 1)
                            nc.scalar.copy(hid[0][:, m, :], whole[m % 2][:, :]).then_inc(hid_high, 1)
                        if (layer, m) == (0, 2):
                            if more:
                                head_root_of(t + 1)
                            if prior:
                                norm_root_of("y", t - 1)
                        if more:
                            if (layer, m) in BETWEEN:
                                copy_heads(t + 1, BETWEEN[layer, m])
                            if (layer, m) == (1, 4):
                                norm_root_of("mid", t + 1)
                if more:
                    high_xt(t + 1)

            all_tiles(act, begin, tile, lambda: norm_root_of("y", LAST))

        @block.vector
        def _(dve):
            LOW_AT = {(0, 6): 0, (0, 7): 1, (1, 0): 2, (1, 1): 3}

            def sum_squares(n):
                for s in range(SUBS):
                    dve.wait_ge(squared, SUBS * n + s + 1)
                    nc.vector.tensor_reduce(head_var[:, s * HEADS:(s + 1) * HEADS], square[s % 2][:, :, :], AXIS.X, ALU.add).then_inc(summed, 1)
                dve.wait_ge(summed, 2 + SUBS * n + SUBS)
                nc.vector.tensor_scalar(head_var[:, :], head_var[:, :], 1.0 / D, LN_EPS, ALU.mult, ALU.add).then_inc(head_var_ready, 1)

            def norm_heads(n):
                v0 = 4 * n
                dve.wait_ge(head_root_ready, n + 1)
                nc.vector.reciprocal(head_quotient[:, :], head_root[:, :]).then_inc(head_vec, 1)
                dve.wait_ge(head_vec, v0 + 1)
                nc.vector.tensor_tensor(head_quotient[:, :], head_quotient[:, :], head_var[:, :], ALU.mult).then_inc(head_vec, 1)
                dve.wait_ge(head_vec, v0 + 2)
                nc.vector.tensor_tensor(head_quotient[:, :], head_quotient[:, :], head_root[:, :], ALU.add).then_inc(head_vec, 1)
                dve.wait_ge(head_vec, v0 + 3)
                nc.vector.reciprocal(head_rstd[:, :], head_quotient[:, :]).then_inc(head_vec, 1)
                dve.wait_ge(head_vec, v0 + 4)
                for s in range(SUBS):
                    heads = heads_sb[:, s, :].rearrange("p (h d) -> p h d", d=D)
                    rstd = head_rstd[:, s * HEADS:(s + 1) * HEADS].unsqueeze(2).to_broadcast([PARTS, HEADS, D])
                    nc.vector.scalar_tensor_tensor(heads, heads, 2.0 * (1.0 - LAM_INIT), rstd, ALU.mult, ALU.mult).then_inc(normed_ready, 1)

            def low_heads(n, s):
                dve.wait_ge(normed_copied, SUBS * n + s + 1)
                nc.vector.tensor_tensor(normed_t[1][:, :], turn_ps[s % 2][:, :], normed_t[0][:, :].bitcast(F32), ALU.subtract).then_inc(normed_low, 1)

            def norm_stats(which, n, rows):
                bufs, sems = norm_bufs[which], norm_sems[which]
                v0 = (2 * SUBS + 5) * n
                for s in range(SUBS):
                    nc.vector.bn_stats(bufs["stats"][:, s, :], rows[:, s, :]).then_inc(sems["vec"], 1)
                dve.wait_ge(sems["vec"], v0 + SUBS)
                dve.sem_inc(sems["aggr_begun"], 1)
                for s in range(SUBS):
                    nc.vector.bn_aggr(bufs["mean_var"][:, s, :], bufs["stats"][:, s, :]).then_inc(sems["vec"], 1)
                dve.wait_ge(sems["vec"], v0 + 2 * SUBS)
                nc.vector.tensor_scalar(bufs["var"][:, :], bufs["mean_var"][:, :, 1], LN_EPS, None, ALU.add).then_inc(sems["var_ready"], 1)

            def norm_apply(which, n, rows):
                bufs, sems = norm_bufs[which], norm_sems[which]
                v0 = (2 * SUBS + 5) * n + 2 * SUBS
                quotient, root = bufs["quotient"], bufs["root"]
                dve.wait_ge(sems["root_ready"], n + 1)
                nc.vector.reciprocal(quotient[:, :], root[:, :]).then_inc(sems["vec"], 1)
                dve.wait_ge(sems["vec"], v0 + 1)
                nc.vector.tensor_tensor(quotient[:, :], quotient[:, :], bufs["var"][:, :], ALU.mult).then_inc(sems["vec"], 1)
                dve.wait_ge(sems["vec"], v0 + 2)
                nc.vector.tensor_tensor(quotient[:, :], quotient[:, :], root[:, :], ALU.add).then_inc(sems["vec"], 1)
                dve.wait_ge(sems["vec"], v0 + 3)
                nc.vector.tensor_scalar(quotient[:, :], quotient[:, :], 0.5, None, ALU.mult).then_inc(sems["vec"], 1)
                dve.wait_ge(sems["vec"], v0 + 4)
                nc.vector.reciprocal(bufs["rstd"][:, :], quotient[:, :]).then_inc(sems["vec"], 1)
                dve.wait_ge(sems["vec"], v0 + 5)
                for s in range(SUBS):
                    nc.vector.tensor_scalar(rows[:, s, :], rows[:, s, :], bufs["mean_var"][:, s, 0:1], bufs["rstd"][:, s:s + 1],
                                            ALU.subtract, ALU.mult).then_inc(sems["ready"], 1)

            def add_attention(n, u, r, half):
                if half == 0:
                    dve.wait_ge(x_loaded[u], 16 * r + 16)
                dve.wait_ge(projected, SUBS * n + HALF * (half + 1))
                rows = mid[u][:, HALF * half:HALF * (half + 1), :]
                nc.vector.tensor_tensor(rows, y_ps[half][:, :, :], rows, ALU.add).then_inc(mid_added, 1)

            def mid_stats(n, u):
                dve.wait_ge(mid_added, 2 * n + 2)
                norm_stats("mid", n, mid[u])

            def low_xt(n):
                for c in range(EC):
                    dve.wait_ge(xt_high, EC * n + c + 1)
                    nc.vector.tensor_tensor(xt[1][:, c, :], turn_ps[c][:, :], xt[0][:, c, :].bitcast(F32), ALU.subtract).then_inc(xt_ready, 1)

            def y_stats(t):
                dve.wait_ge(y_added, SUBS * t + SUBS)
                norm_stats("y", t, y)

            def begin():
                sum_squares(0)
                if split:
                    dve.wait_ge(wo_high, 1)
                    nc.vector.tensor_tensor(wo_p[1][:, :, :], y[:, :, :], wo_p[0][:, :, :].bitcast(F32), ALU.subtract).then_inc(wo_low, 1)
                norm_heads(0)
                if split:
                    for s in range(SUBS):
                        low_heads(0, s)
                for half in range(2):
                    add_attention(0, 0, 0, half)
                mid_stats(0, 0)
                norm_apply("mid", 0, mid[0])
                if split:
                    low_xt(0)

            def tile(t, u, r, prior, more):
                for m in range(HC + 1):
                    n = HC * t + m
                    if m < HC:
                        dve.wait_ge(gate_ready, n + 1)
                        if split:
                            if m < 2:
                                dve.wait_ge(hid_low, LAYERS * t + LAYERS)
                            else:
                                dve.wait_ge(gated_low, n - 1)
                        product = whole[m % 2][:, :] if split else hid_a[0][:, m, :]
                        nc.vector.scalar_tensor_tensor(product, hid_ps[2 * (m % 2) + 1][:, :], keep["s2"][:, m:m + 1], gate[m % 2][:, :],
                                                       ALU.mult, ALU.mult).then_inc(gated, 1)
                    if m > 0 and split:
                        dve.wait_ge(gated_high, n)
                        nc.vector.tensor_tensor(hid_a[1][:, m - 1, :], whole[(m - 1) % 2][:, :], hid_a[0][:, m - 1, :].bitcast(F32),
                                                ALU.subtract).then_inc(gated_low, 1)
                for layer, hid in enumerate((hid_b, hid_a)):
                    for m in range(HC):
                        if split:
                            dve.wait_ge(hid_high, LAYERS * t + HC * layer + m + 1)
                            nc.vector.tensor_tensor(hid[1][:, m, :], whole[m % 2][:, :], hid[0][:, m, :].bitcast(F32), ALU.subtract).then_inc(hid_low, 1)
                        if more and (layer, m) == (0, 0):
                            sum_squares(t + 1)
                        if prior and (layer, m) == (0, 1):
                            y_stats(t - 1)
                        if more and (layer, m) == (0, 2):
                            norm_heads(t + 1)
                        if prior and (layer, m) == (0, 3):
                            norm_apply("y", t - 1, y)
                        if more and split and (layer, m) in LOW_AT:
                            low_heads(t + 1, LOW_AT[layer, m])
                        if more and (layer, m) in ((1, 2), (1, 3)):
                            add_attention(t + 1, 1 - u, r + u, m - 2)
                        if more and (layer, m) == (1, 3):
                            mid_stats(t + 1, 1 - u)
                        if more and (layer, m) == (1, 4):
                            norm_apply("mid", t + 1, mid[1 - u])
                if more and split:
                    low_xt(t + 1)
                dve.wait_ge(stored, 16 * t + 16)
                for s in range(SUBS):
                    dve.wait_ge(y_projected, SUBS * t + s + 1)
                    nc.vector.tensor_tensor(y[:, s, :], y_ps[s % 2][:, s // 2, :], keep["s3"][:, :], ALU.mult).then_inc(y_free, 1)
                    dve.wait_ge(y_free, SUBS * t + 2 * SUBS + s + 1)
                    nc.vector.tensor_tensor(y[:, s, :], y[:, s, :], mid[u][:, s, :], ALU.add).then_inc(y_added, 1)

            def end():
                y_stats(LAST)
                norm_apply("y", LAST, y)

            all_tiles(dve, begin, tile, end)


INPUTS = ["L0_attn_x", "L0_attn_Wq1", "L0_attn_Wq2", "L0_attn_Wk1", "L0_attn_Wk2", "L0_attn_Wv", "L0_attn_Wo",
          "L0_attn_lq1", "L0_attn_lk1", "L0_attn_lq2", "L0_attn_lk2",
          "L0_ffn_w1_w", "L0_ffn_w1_s", "L0_ffn_w2_w", "L0_ffn_w2_s", "L0_ffn_h1_w", "L0_ffn_h1_s",
          "L0_ffn_h2_w", "L0_ffn_h2_s", "L0_ffn_w3_w", "L0_ffn_w3_s"]


def kernel(**inputs):
    import numpy as np
    import concourse.bacc as bacc
    from concourse.bass_utils import run_bass_kernel_spmd

    nc = bacc.Bacc("TRN2", target_bir_lowering=False, num_devices=1)
    arrays, args = {}, []
    for name in INPUTS:
        a = np.ascontiguousarray(inputs[name])
        arrays[f"in_{name}"] = a
        args.append(nc.dram_tensor(f"in_{name}", a.shape, mybir.dt.from_np(a.dtype), kind="ExternalInput").ap())
    out = nc.dram_tensor("out", (BATCH, SEQ, EMBED), F32, kind="ExternalOutput").ap()
    layer_kernel(nc, *args, out)
    result = run_bass_kernel_spmd(nc, [arrays], core_ids=[0])
    return result.results[0]["out"]
```
